# Optimizing a Trainium2 kernel written in Bass

```python
import numpy as np
import jax
import jax.numpy as jnp

def _softmax(x, axis=-1):
    return jax.nn.softmax(x, axis=axis)

def _gelu(x):
    return jax.nn.gelu(x, approximate=True)

def _silu(x):
    return jax.nn.silu(x)

def _sigmoid(x):
    return jax.nn.sigmoid(x)

def _layernorm(x, axis=-1, eps=1e-05):
    m = jnp.mean(x, axis=axis, keepdims=True)
    v = jnp.var(x, axis=axis, keepdims=True)
    return (x - m) / jnp.sqrt(v + eps)

def _scatter_add(tgt, idx, src, axis=0):
    return tgt.at[idx].add(src)

def _segment_sum(src, seg, n):
    return jax.ops.segment_sum(src, seg, n)
kernel_name = 'mk_lm_tower_d2_tok_ids1024_r4_66d633'

def setup_inputs(seed: int=0):
    np.random.seed(seed)
    _w = jnp.asarray

    def _rec_inputs():
        import jax
        import jax.numpy as jnp
        _rk = jax.random.key(seed)
        x = jax.random.randint(jax.random.fold_in(_rk, 1), (16, 512), 0, 64, jnp.int32)
        return x
    x = _rec_inputs()

    def _L0_tok_setup():
        import jax, jax.numpy as jnp
        import numpy as np
        N_FFT = 64
        HOP = 64
        NUM_FREQ = N_FFT // 2 + 1

        def _stft_mag(sig, window):
            L = sig.shape[1]
            pad = N_FFT // 2
            x = jnp.pad(sig, ((0, 0), (pad, pad)), mode='reflect')
            n_frames = 1 + L // HOP
            idx = jnp.arange(n_frames)[:, None] * HOP + jnp.arange(N_FFT)[None, :]
            frames = x[:, idx] * window
            spec = jnp.fft.rfft(frames, axis=-1)
            r, im = (spec.real, spec.imag)
            m2 = r * r + im * im
            mag = jnp.where(m2 == 0, 0.0, jnp.sqrt(jnp.where(m2 == 0, 1.0, m2)))
            return (mag, n_frames)

        def _linear_interp_last(feat, out_len):
            in_len = feat.shape[-1]
            coord = jnp.clip((jnp.arange(out_len) + 0.5) * (in_len / out_len) - 0.5, 0.0, in_len - 1.0)
            i0 = jnp.floor(coord).astype(jnp.int32)
            i1 = jnp.minimum(i0 + 1, in_len - 1)
            w = (coord - i0).astype(feat.dtype)
            return feat[..., i0] * (1.0 - w) + feat[..., i1] * w
        key = jax.random.key(seed)
        k0, k1, k2 = jax.random.split(key, 3)
        B, L, V, d_model = (2, 256, 64, 256)
        d_emb = int(d_model * 0.7)
        d_stft = d_model - d_emb
        input_ids = jax.random.randint(k0, (B, L), 0, V)
        emb_table = jax.random.normal(k1, (V, d_emb), jnp.float32) * 0.02
        proj_w = jax.random.normal(k2, (d_stft, V * NUM_FREQ), jnp.float32) * 0.02
        proj_b = jnp.zeros((d_stft,), jnp.float32)
        n = jnp.arange(N_FFT, dtype=jnp.float32)
        window = 0.5 * (1.0 - jnp.cos(2.0 * jnp.pi * n / N_FFT))
        return {'input_ids': input_ids, 'emb_table': emb_table, 'proj_w': proj_w, 'proj_b': proj_b, 'window': window}
    _L0_tok_all = _L0_tok_setup()
    _L0_tok_in = {k: v for k, v in _L0_tok_all.items() if k in ('emb_table', 'proj_w', 'proj_b', 'window')}
    del _L0_tok_all

    def _L0_attn_setup():
        import jax, jax.numpy as jnp
        import numpy as np
        N_HEAD = 16
        D_MODEL = 256
        HEAD_DIM = D_MODEL // N_HEAD
        LAMBDA_INIT = 0.8 - 0.6 * float(np.exp(-0.3 * 1))

        def _rms_norm(x):
            eps = jnp.finfo(x.dtype).eps
            return x * jax.lax.rsqrt(jnp.mean(jnp.square(x), axis=-1, keepdims=True) + eps)

        def _rotary_cos_sin(T, dim, base=10000.0):
            inv_freq = 1.0 / base ** (jnp.arange(0, dim, 2, dtype=jnp.float32) / dim)
            freqs = jnp.outer(jnp.arange(T, dtype=jnp.float32), inv_freq)
            return (jnp.cos(freqs), jnp.sin(freqs))

        def _apply_rotary(x, cos, sin):
            d = x.shape[-1] // 2
            c = cos[None, :, None, None, :]
            s = sin[None, :, None, None, :]
            x1, x2 = (x[..., :d], x[..., d:])
            return jnp.concatenate([x1 * c + x2 * s, -x1 * s + x2 * c], axis=-1)

        def _causal_attn(q, k, v, scale):
            T = q.shape[1]
            scores = jnp.einsum('bthd,bshd->bhts', q, k) * scale
            mask = jnp.tril(jnp.ones((T, T), dtype=bool))
            scores = jnp.where(mask, scores, -jnp.inf)
            w = jax.nn.softmax(scores, axis=-1)
            return jnp.einsum('bhts,bshd->bthd', w, v)
        key = jax.random.key(seed)
        ks = jax.random.split(key, 10)
        B, T, D = (1, 512, D_MODEL)
        std = 0.02
        return {'x': jax.random.normal(ks[0], (B, T, D), jnp.float32), 'Wq': jax.random.normal(ks[1], (D, D), jnp.float32) * std, 'Wk': jax.random.normal(ks[2], (D, D), jnp.float32) * std, 'Wv': jax.random.normal(ks[3], (D, D), jnp.float32) * std, 'Wproj': jax.random.normal(ks[4], (D, D), jnp.float32) * std, 'lambda_q1': jax.random.normal(ks[5], (HEAD_DIM // 2,), jnp.float32) * 0.1, 'lambda_k1': jax.random.normal(ks[6], (HEAD_DIM // 2,), jnp.float32) * 0.1, 'lambda_q2': jax.random.normal(ks[7], (HEAD_DIM // 2,), jnp.float32) * 0.1, 'lambda_k2': jax.random.normal(ks[8], (HEAD_DIM // 2,), jnp.float32) * 0.1}
    _L0_attn_all = _L0_attn_setup()
    _L0_attn_in = {k: v for k, v in _L0_attn_all.items() if k in ('Wq', 'Wk', 'Wv', 'Wproj', 'lambda_q1', 'lambda_k1', 'lambda_q2', 'lambda_k2')}
    del _L0_attn_all

    def _L0_ffn_setup():
        import jax, jax.numpy as jnp
        import numpy as np
        H = 256
        I = 512
        E = 32
        B, S = (4, 512)

        def _grouped_mm(a, w, group_sizes):
            return jax.lax.ragged_dot(a, w, group_sizes)

        def _swiglu(x, gw, uw, dw):
            return jax.nn.silu(x @ gw) * (x @ uw) @ dw
        key = jax.random.key(seed)
        ks = jax.random.split(key, 8)
        scale = 0.02
        inp = {'hidden_states': jax.random.normal(ks[0], (B, S, H), dtype=jnp.float32), 'gate_w': jax.random.normal(ks[1], (H, E), dtype=jnp.float32) * scale, 'shared_gate_w': jax.random.normal(ks[2], (H, I), dtype=jnp.float32) * scale, 'shared_up_w': jax.random.normal(ks[3], (H, I), dtype=jnp.float32) * scale, 'shared_down_w': jax.random.normal(ks[4], (I, H), dtype=jnp.float32) * scale, 'routed_gate_w': jax.random.normal(ks[5], (E, H, I), dtype=jnp.float32) * scale, 'routed_up_w': jax.random.normal(ks[6], (E, H, I), dtype=jnp.float32) * scale, 'routed_down_w': jax.random.normal(ks[7], (E, I, H), dtype=jnp.float32) * scale}
        return inp
    _L0_ffn_all = _L0_ffn_setup()
    _L0_ffn_in = {k: v for k, v in _L0_ffn_all.items() if k in ('gate_w', 'shared_gate_w', 'shared_up_w', 'shared_down_w', 'routed_gate_w', 'routed_up_w', 'routed_down_w')}
    del _L0_ffn_all

    def _L1_attn_setup():
        import jax, jax.numpy as jnp
        import numpy as np
        B, L, E, H = (4, 256, 256, 16)
        D = E // H
        SPARSITY = 0.4
        NEG_INF = jnp.float32(-1e+30)
        key = jax.random.key(seed)
        ks = jax.random.split(key, 8)
        s = 0.02
        return {'hidden_states': jax.random.normal(ks[0], (B, L, E), jnp.float32), 'qkv_w': jax.random.normal(ks[1], (3 * E, E), jnp.float32) * s, 'qkv_b': jax.random.normal(ks[2], (3 * E,), jnp.float32) * s, 'r_w1': jax.random.normal(ks[3], (E // 4, E), jnp.float32) * s, 'r_b1': jax.random.normal(ks[4], (E // 4,), jnp.float32) * s, 'r_w2': jax.random.normal(ks[5], (H, E // 4), jnp.float32) * s, 'r_b2': jax.random.normal(ks[6], (H,), jnp.float32) * s}
    _L1_attn_all = _L1_attn_setup()
    _L1_attn_in = {k: v for k, v in _L1_attn_all.items() if k in ('qkv_w', 'qkv_b', 'r_w1', 'r_b1', 'r_w2', 'r_b2')}
    del _L1_attn_all

    def _L1_ffn_setup():
        import jax, jax.numpy as jnp
        import numpy as np
        E = 16
        K = 2
        LOAD = 1.0

        def _dispatch(xb, pb, cap):
            T, C = xb.shape
            top_k_probs, ei = jax.lax.top_k(pb, K)
            flat = ei.swapaxes(0, 1).ravel()
            one_hot = jax.nn.one_hot(flat, E, dtype=jnp.int32)
            pos = jnp.cumsum(one_hot, axis=0) * one_hot
            pos = pos.reshape(K, T, E).swapaxes(0, 1)
            pos = jnp.max(pos, axis=-1) - 1
            ei2 = flat.reshape(K, T).swapaxes(0, 1)
            xr = jnp.repeat(xb, K, axis=0)
            buf = jnp.zeros((E, cap, C), xb.dtype)
            buf = buf.at[ei2.ravel(), pos.ravel()].set(xr, mode='drop')
            return (top_k_probs, pos, ei2, buf)

        def _collect(eo_b, ei_b, pos_b, tk_b):
            out = eo_b[ei_b, pos_b]
            return jnp.sum(tk_b[..., None] * out, axis=1)
        key = jax.random.key(seed)
        k1, k2, k3, k4, k5 = jax.random.split(key, 5)
        B, T, C, H = (8, 1024, 256, 128)
        n_layer = 12
        x = jax.random.normal(k1, (B, T, C), dtype=jnp.float32)
        w_router = jax.random.normal(k2, (C, E), dtype=jnp.float32) * 0.02
        w_fc = jax.random.normal(k3, (E, C, H), dtype=jnp.float32) * 0.02
        w_gate = jax.random.normal(k4, (E, C, H), dtype=jnp.float32) * 0.02
        w_proj = jax.random.normal(k5, (E, H, C), dtype=jnp.float32) * (0.02 * (2 * n_layer) ** (-0.5))
        return {'x': x, 'w_router': w_router, 'w_fc': w_fc, 'w_gate': w_gate, 'w_proj': w_proj}
    _L1_ffn_all = _L1_ffn_setup()
    _L1_ffn_in = {k: v for k, v in _L1_ffn_all.items() if k in ('w_router', 'w_fc', 'w_gate', 'w_proj')}
    del _L1_ffn_all
    return {'x': x, 'L0_tok_emb_table': _L0_tok_in['emb_table'], 'L0_tok_proj_w': _L0_tok_in['proj_w'], 'L0_tok_proj_b': _L0_tok_in['proj_b'], 'L0_tok_window': _L0_tok_in['window'], 'L0_attn_Wq': _L0_attn_in['Wq'], 'L0_attn_Wk': _L0_attn_in['Wk'], 'L0_attn_Wv': _L0_attn_in['Wv'], 'L0_attn_Wproj': _L0_attn_in['Wproj'], 'L0_attn_lambda_q1': _L0_attn_in['lambda_q1'], 'L0_attn_lambda_k1': _L0_attn_in['lambda_k1'], 'L0_attn_lambda_q2': _L0_attn_in['lambda_q2'], 'L0_attn_lambda_k2': _L0_attn_in['lambda_k2'], 'L0_ffn_gate_w': _L0_ffn_in['gate_w'], 'L0_ffn_shared_gate_w': _L0_ffn_in['shared_gate_w'], 'L0_ffn_shared_up_w': _L0_ffn_in['shared_up_w'], 'L0_ffn_shared_down_w': _L0_ffn_in['shared_down_w'], 'L0_ffn_routed_gate_w': _L0_ffn_in['routed_gate_w'], 'L0_ffn_routed_up_w': _L0_ffn_in['routed_up_w'], 'L0_ffn_routed_down_w': _L0_ffn_in['routed_down_w'], 'L1_attn_qkv_w': _L1_attn_in['qkv_w'], 'L1_attn_qkv_b': _L1_attn_in['qkv_b'], 'L1_attn_r_w1': _L1_attn_in['r_w1'], 'L1_attn_r_b1': _L1_attn_in['r_b1'], 'L1_attn_r_w2': _L1_attn_in['r_w2'], 'L1_attn_r_b2': _L1_attn_in['r_b2'], 'L1_ffn_w_router': _L1_ffn_in['w_router'], 'L1_ffn_w_fc': _L1_ffn_in['w_fc'], 'L1_ffn_w_gate': _L1_ffn_in['w_gate'], 'L1_ffn_w_proj': _L1_ffn_in['w_proj']}

def reference(x, L0_tok_emb_table, L0_tok_proj_w, L0_tok_proj_b, L0_tok_window, L0_attn_Wq, L0_attn_Wk, L0_attn_Wv, L0_attn_Wproj, L0_attn_lambda_q1, L0_attn_lambda_k1, L0_attn_lambda_q2, L0_attn_lambda_k2, L0_ffn_gate_w, L0_ffn_shared_gate_w, L0_ffn_shared_up_w, L0_ffn_shared_down_w, L0_ffn_routed_gate_w, L0_ffn_routed_up_w, L0_ffn_routed_down_w, L1_attn_qkv_w, L1_attn_qkv_b, L1_attn_r_w1, L1_attn_r_b1, L1_attn_r_w2, L1_attn_r_b2, L1_ffn_w_router, L1_ffn_w_fc, L1_ffn_w_gate, L1_ffn_w_proj):
    import jax
    import jax.numpy as jnp

    def _L0_tok_ref(input_ids, emb_table, proj_w, proj_b, window):
        import jax, jax.numpy as jnp
        import numpy as np
        N_FFT = 64
        HOP = 64
        NUM_FREQ = N_FFT // 2 + 1

        def _stft_mag(sig, window):
            L = sig.shape[1]
            pad = N_FFT // 2
            x = jnp.pad(sig, ((0, 0), (pad, pad)), mode='reflect')
            n_frames = 1 + L // HOP
            idx = jnp.arange(n_frames)[:, None] * HOP + jnp.arange(N_FFT)[None, :]
            frames = x[:, idx] * window
            spec = jnp.fft.rfft(frames, axis=-1)
            r, im = (spec.real, spec.imag)
            m2 = r * r + im * im
            mag = jnp.where(m2 == 0, 0.0, jnp.sqrt(jnp.where(m2 == 0, 1.0, m2)))
            return (mag, n_frames)

        def _linear_interp_last(feat, out_len):
            in_len = feat.shape[-1]
            coord = jnp.clip((jnp.arange(out_len) + 0.5) * (in_len / out_len) - 0.5, 0.0, in_len - 1.0)
            i0 = jnp.floor(coord).astype(jnp.int32)
            i1 = jnp.minimum(i0 + 1, in_len - 1)
            w = (coord - i0).astype(feat.dtype)
            return feat[..., i0] * (1.0 - w) + feat[..., i1] * w
        B, L = input_ids.shape
        V = emb_table.shape[0]
        word_embeds = emb_table[input_ids]
        sig = jax.nn.one_hot(input_ids, V, dtype=jnp.float32)
        sig = jnp.transpose(sig, (0, 2, 1)).reshape(B * V, L)
        mag, T = _stft_mag(sig, window)
        feat = mag.reshape(B, V, T, NUM_FREQ).transpose(0, 3, 1, 2)
        feat = feat.reshape(B, NUM_FREQ * V, T)
        up = _linear_interp_last(feat, L)
        stft_feat = jnp.transpose(up, (0, 2, 1))
        stft_enc = stft_feat @ proj_w.T + proj_b
        return jnp.concatenate([word_embeds, stft_enc], axis=-1)

    def _L0_attn_ref(x, Wq, Wk, Wv, Wproj, lambda_q1, lambda_k1, lambda_q2, lambda_k2):
        import jax, jax.numpy as jnp
        import numpy as np
        N_HEAD = 16
        D_MODEL = 256
        HEAD_DIM = D_MODEL // N_HEAD
        LAMBDA_INIT = 0.8 - 0.6 * float(np.exp(-0.3 * 1))

        def _rms_norm(x):
            eps = jnp.finfo(x.dtype).eps
            return x * jax.lax.rsqrt(jnp.mean(jnp.square(x), axis=-1, keepdims=True) + eps)

        def _rotary_cos_sin(T, dim, base=10000.0):
            inv_freq = 1.0 / base ** (jnp.arange(0, dim, 2, dtype=jnp.float32) / dim)
            freqs = jnp.outer(jnp.arange(T, dtype=jnp.float32), inv_freq)
            return (jnp.cos(freqs), jnp.sin(freqs))

        def _apply_rotary(x, cos, sin):
            d = x.shape[-1] // 2
            c = cos[None, :, None, None, :]
            s = sin[None, :, None, None, :]
            x1, x2 = (x[..., :d], x[..., d:])
            return jnp.concatenate([x1 * c + x2 * s, -x1 * s + x2 * c], axis=-1)

        def _causal_attn(q, k, v, scale):
            T = q.shape[1]
            scores = jnp.einsum('bthd,bshd->bhts', q, k) * scale
            mask = jnp.tril(jnp.ones((T, T), dtype=bool))
            scores = jnp.where(mask, scores, -jnp.inf)
            w = jax.nn.softmax(scores, axis=-1)
            return jnp.einsum('bhts,bshd->bthd', w, v)
        B, T, D = x.shape
        nh, hd = (N_HEAD, HEAD_DIM)
        q = (x @ Wq.T).reshape(B, T, 2, nh // 2, hd)
        k = (x @ Wk.T).reshape(B, T, 2, nh // 2, hd)
        v = (x @ Wv.T).reshape(B, T, nh // 2, 2 * hd)
        q, k = (_rms_norm(q), _rms_norm(k))
        cos, sin = _rotary_cos_sin(T, hd)
        q, k = (_apply_rotary(q, cos, sin), _apply_rotary(k, cos, sin))
        q1, q2 = (q[:, :, 0], q[:, :, 1])
        k1, k2 = (k[:, :, 0], k[:, :, 1])
        scale = 1.0 / jnp.sqrt(jnp.asarray(hd, x.dtype))
        y1 = _causal_attn(q1, k1, v, scale)
        y2 = _causal_attn(q2, k2, v, scale)
        lambda_1 = jnp.exp(jnp.sum(lambda_q1 * lambda_k1))
        lambda_2 = jnp.exp(jnp.sum(lambda_q2 * lambda_k2))
        lambda_full = lambda_1 - lambda_2 + LAMBDA_INIT
        y = (y1 - lambda_full * y2).reshape(B, T, D)
        return y @ Wproj.T

    def _L0_ffn_ref(hidden_states, gate_w, shared_gate_w, shared_up_w, shared_down_w, routed_gate_w, routed_up_w, routed_down_w):
        import jax, jax.numpy as jnp
        import numpy as np
        H = 256
        I = 512
        E = 32
        B, S = (4, 512)

        def _grouped_mm(a, w, group_sizes):
            return jax.lax.ragged_dot(a, w, group_sizes)

        def _swiglu(x, gw, uw, dw):
            return jax.nn.silu(x @ gw) * (x @ uw) @ dw
        b, s, h = hidden_states.shape
        x = hidden_states.reshape(-1, h)
        shared_out = _swiglu(x, shared_gate_w, shared_up_w, shared_down_w)
        logits = x @ gate_w
        topk_ids = jnp.argmax(logits, axis=-1)
        topk_val = jnp.max(logits, axis=-1)
        scores = jax.nn.sigmoid(topk_val)[:, None]
        xs = x * scores
        tokens_per_expert = jnp.zeros((E,), jnp.int32).at[topk_ids].add(1)
        order = jnp.argsort(topk_ids)
        sorted_x = xs[order]
        g = _grouped_mm(sorted_x, routed_gate_w, tokens_per_expert)
        u = _grouped_mm(sorted_x, routed_up_w, tokens_per_expert)
        d = _grouped_mm(jax.nn.silu(g) * u, routed_down_w, tokens_per_expert)
        inv = jnp.argsort(order)
        routed_out = d[inv]
        return (shared_out + routed_out).reshape(b, s, h)

    def _L1_attn_ref(hidden_states, qkv_w, qkv_b, r_w1, r_b1, r_w2, r_b2):
        import jax, jax.numpy as jnp
        import numpy as np
        B, L, E, H = (4, 256, 256, 16)
        D = E // H
        SPARSITY = 0.4
        NEG_INF = jnp.float32(-1e+30)
        bsz, tgt_len, embed_dim = hidden_states.shape
        qkv = (hidden_states @ qkv_w.T + qkv_b).reshape(bsz, tgt_len, 3, H, D)
        qkv = jnp.transpose(qkv, (2, 0, 3, 1, 4))
        q, k, v = (qkv[0], qkv[1], qkv[2])
        h1 = jax.nn.relu(hidden_states @ r_w1.T + r_b1)
        routing_logits = jax.nn.sigmoid(h1 @ r_w2.T + r_b2)
        routing_scores = jax.nn.sigmoid(routing_logits)
        attn = jnp.einsum('bhqd,bhkd->bhqk', q, k) / jnp.sqrt(jnp.float32(D))
        k_keep = max(1, int(tgt_len * SPARSITY))
        rs_t = jnp.transpose(routing_scores, (0, 2, 1))
        _, top_idx = jax.lax.top_k(rs_t, k_keep)
        keep = jnp.zeros((bsz, H, tgt_len), dtype=bool)
        keep = keep.at[jnp.arange(bsz)[:, None, None], jnp.arange(H)[None, :, None], top_idx].set(True)
        sparse = jnp.where(keep[:, :, None, :], attn, NEG_INF)
        w = jax.nn.softmax(sparse.astype(jnp.float32), axis=-1).astype(q.dtype)
        out = jnp.einsum('bhqk,bhkd->bhqd', w, v)
        out = jnp.transpose(out, (0, 2, 1, 3)).reshape(bsz, tgt_len, embed_dim)
        return out

    def _L1_ffn_ref(x, w_router, w_fc, w_gate, w_proj):
        import jax, jax.numpy as jnp
        import numpy as np
        E = 16
        K = 2
        LOAD = 1.0

        def _dispatch(xb, pb, cap):
            T, C = xb.shape
            top_k_probs, ei = jax.lax.top_k(pb, K)
            flat = ei.swapaxes(0, 1).ravel()
            one_hot = jax.nn.one_hot(flat, E, dtype=jnp.int32)
            pos = jnp.cumsum(one_hot, axis=0) * one_hot
            pos = pos.reshape(K, T, E).swapaxes(0, 1)
            pos = jnp.max(pos, axis=-1) - 1
            ei2 = flat.reshape(K, T).swapaxes(0, 1)
            xr = jnp.repeat(xb, K, axis=0)
            buf = jnp.zeros((E, cap, C), xb.dtype)
            buf = buf.at[ei2.ravel(), pos.ravel()].set(xr, mode='drop')
            return (top_k_probs, pos, ei2, buf)

        def _collect(eo_b, ei_b, pos_b, tk_b):
            out = eo_b[ei_b, pos_b]
            return jnp.sum(tk_b[..., None] * out, axis=1)
        B, T, C = x.shape
        cap = int(LOAD * K * max(1, T / E))
        g = jnp.einsum('btc,ce->bte', x, w_router)
        gate_probs = jax.nn.softmax(g, axis=-1)
        top_k_probs, positions, indices, expert_inputs = jax.vmap(lambda xb, pb: _dispatch(xb, pb, cap))(x, gate_probs)
        expert_inputs = jnp.swapaxes(expert_inputs, 0, 1).reshape(E, B * cap, C)
        gg = jnp.einsum('enc,ech->enh', expert_inputs, w_gate)
        h = jnp.einsum('enc,ech->enh', expert_inputs, w_fc)
        h = jax.nn.silu(gg) * h
        o = jnp.einsum('enh,ehc->enc', h, w_proj)
        expert_outputs = jnp.swapaxes(o.reshape(E, B, cap, C), 0, 1)
        y = jax.vmap(_collect)(expert_outputs, indices, positions, top_k_probs)
        return y
    h = _L0_tok_ref(x, L0_tok_emb_table, L0_tok_proj_w, L0_tok_proj_b, L0_tok_window)
    h = h + _L0_attn_ref(_layernorm(h, axis=-1), L0_attn_Wq, L0_attn_Wk, L0_attn_Wv, L0_attn_Wproj, L0_attn_lambda_q1, L0_attn_lambda_k1, L0_attn_lambda_q2, L0_attn_lambda_k2)
    h = h + _L0_ffn_ref(_layernorm(h, axis=-1), L0_ffn_gate_w, L0_ffn_shared_gate_w, L0_ffn_shared_up_w, L0_ffn_shared_down_w, L0_ffn_routed_gate_w, L0_ffn_routed_up_w, L0_ffn_routed_down_w)
    h = h + _L1_attn_ref(_layernorm(h, axis=-1), L1_attn_qkv_w, L1_attn_qkv_b, L1_attn_r_w1, L1_attn_r_b1, L1_attn_r_w2, L1_attn_r_b2)
    h = h + _L1_ffn_ref(_layernorm(h, axis=-1), L1_ffn_w_router, L1_ffn_w_fc, L1_ffn_w_gate, L1_ffn_w_proj)
    return h

_drawn_inputs = setup_inputs


def setup_inputs(seed=0):
    import zlib

    import numpy as np

    out = dict(_drawn_inputs(seed))
    spreads = {'L0_tok_proj_b': (0.0, 0.1)}
    factors = {'L0_attn_lambda_q1': 8.0,
     'L0_attn_lambda_k1': 5.582,
     'L0_attn_lambda_q2': 3.361,
     'L0_attn_lambda_k2': 3.059,
     'L1_attn_r_b1': 2.731,
     'L1_ffn_w_router': 8.0,
     'L1_ffn_w_fc': 8.0,
     'L1_ffn_w_gate': 8.0,
     'L1_ffn_w_proj': 8.0}
    for name, (base, spread) in spreads.items():
        noise = np.random.default_rng([zlib.crc32(name.encode()), seed]).standard_normal(out[name].shape)
        drawn = base * np.exp(spread * noise) if base else spread * noise
        out[name] = jnp.asarray(drawn.astype(out[name].dtype))
    for name, factor in factors.items():
        out[name] = (out[name] * factor).astype(out[name].dtype)
    return out
```

```python
from contextlib import ExitStack

import numpy as np

import concourse.bass as bass
from concourse import mybir

ALU = mybir.AluOpType
ACT = mybir.ActivationFunctionType
AX = mybir.AxisListType
F32 = mybir.dt.float32
BF16 = mybir.dt.bfloat16
I32 = mybir.dt.int32
U32 = mybir.dt.uint32

P = 128
B, T, D = 16, 512, 256
V, D_EMB = 64, 179
D_STFT = D - D_EMB
FRAMES, FREQS, NFFT = 9, 33, 64
TILES = B * T // P
TPB = T // P
LN_EPS = 1e-5
RMS_EPS = float(np.finfo(np.float32).eps)
LAMBDA_INIT = 0.8 - 0.6 * float(np.exp(-0.3 * 1))


class Bufs:

    def __init__(self, nc, ctx, stage):
        self.nc, self.ctx, self.stage, self.sems = nc, ctx, stage, []
        ctx.callback(self.clear)

    def clear(self):
        if self.sems:
            self.nc.clear_and_free_semaphores(self.sems)
            self.nc.all_engine_barrier()

    def sb(self, name, shape, dt=F32):
        return self.ctx.enter_context(self.nc.sbuf_tensor(f"{self.stage}_{name}", shape, dt))

    def ps(self, name, shape, dt=F32):
        return self.ctx.enter_context(self.nc.psum_tensor(f"{self.stage}_{name}", shape, dt))

    def sem(self, name):
        self.sems.append(self.nc.alloc_semaphore(f"{self.stage}_{name}"))
        return self.sems[-1]


def embed_tokens(nc, A, S, H):
    NBT = B * FRAMES
    HALF = NBT // 2
    PER = 7
    GROUPS = -(-NBT // PER)
    C2 = 2 * FREQS
    with ExitStack() as ctx:
        m = Bufs(nc, ctx, "tok")
        frame_ids = m.sb("frame_ids", [NFFT, NBT], I32)
        frame_idf = m.sb("frame_idf", [NFFT, NBT])
        iota_v = m.sb("iota_v", [NFFT, V])
        part_id = m.sb("part_id", [V, 1])
        window = m.sb("window", [NFFT, 1])
        dft = m.sb("dft", [NFFT, C2])
        wdft = m.sb("wdft", [NFFT, C2])
        frames = m.sb("frames", [NFFT, NBT, V])
        squares = m.sb("squares", [V, 2, PER, C2])
        mag = m.sb("mag", [V, FREQS, NBT])
        proj_w = m.sb("proj_w", [V, FREQS, D_STFT])
        emb = m.sb("emb", [V, D_EMB])
        pf = m.sb("pf", [HALF, 2, D_STFT])
        pfb = m.sb("pfb", [FRAMES + 1, B, D_STFT])
        interp = m.sb("interp", [FRAMES + 1, T])
        ids_row = m.sb("ids_row", [V, 2, T], I32)
        onehot = m.sb("onehot", [V, 2, T])
        spec = m.ps("spec", [V, 2, 512])
        pproj = m.ps("pproj", [HALF, 2, 512])
        tok = m.ps("tok", [P, 4, 512])
        consts_in, weights_in, bias_in, interp_in = m.sem("consts_in"), m.sem("weights_in"), m.sem("bias_in"), m.sem("interp_in")
        idf_ready, wdft_ready, frames_ready = m.sem("idf_ready"), m.sem("wdft_ready"), m.sem("frames_ready")
        spec_ready, squares_ready, power_ready, mag_ready = m.sem("spec_ready"), m.sem("squares_ready"), m.sem("power_ready"), m.sem("mag_ready")
        proj_ready, pf_ready, pf_out, pf_back = m.sem("proj_ready"), m.sem("pf_ready"), m.sem("pf_out"), m.sem("pf_back")
        ids_in = [m.sem(f"ids_in{k}") for k in range(2)]
        onehot_ready, tok_ready, tok_copied = m.sem("onehot_ready"), m.sem("tok_ready"), m.sem("tok_copied")
        block = ctx.enter_context(nc.Block())
        PAIRS = B // 2

        @block.sync
        def _(sp):
            sp.dma_start(frame_ids[:, :], A["frame_ids"][:, :]).then_inc(consts_in, 16)
            sp.dma_start(iota_v[:, :], A["iota_v"][0:NFFT, :]).then_inc(consts_in, 16)
            sp.dma_start(window[:, :], A["window"][:, :]).then_inc(consts_in, 16)
            sp.dma_start(dft[:, :], A["dft"][:, :]).then_inc(consts_in, 16)
            sp.dma_start(part_id[:, :], A["part_id"][0:V, :]).then_inc(consts_in, 16)
            sp.dma_start(proj_w[:, :, :], A["tok_proj_w"][:, :, :]).then_inc(weights_in, 16)
            sp.dma_start(emb[:, :], A["emb"][:, :]).then_inc(weights_in, 16)
            sp.dma_start(interp[:, :], A["interp"][:, :]).then_inc(interp_in, 16)
            for b in range(B):
                sp.dma_start(pfb[FRAMES:FRAMES + 1, b, :], A["proj_b"][:, :]).then_inc(bias_in, 16)
            sp.wait_ge(pf_ready, 2)
            sp.dma_start(S["frames"].rearrange("(g p) j -> p g j", g=2), pf[:, :, :]).then_inc(pf_out, 16)
            sp.wait_ge(pf_out, 16)
            sp.dma_start(pfb[0:FRAMES, :, :], S["frames"].rearrange("(b t) j -> t b j", t=FRAMES)).then_inc(pf_back, 16)
            with sp.Fori(0, PAIRS) as j:
                for k in range(2):
                    sp.wait_ge(onehot_ready, j * 2 + k + 1)
                    sp.dma_start(ids_row[:, k, :], A["ids"][bass.ds(j * 2 + k, 1), :].to_broadcast([V, T])
                                 ).then_inc(ids_in[k], 16)

        @block.vector
        def _(dve):
            dve.wait_ge(consts_in, 80)
            nc.vector.tensor_copy(frame_idf[:, :], frame_ids[:, :]).then_inc(idf_ready, 1)
            nc.vector.tensor_scalar(wdft[:, :], dft[:, :], window[:, 0:1], None, ALU.mult).then_inc(wdft_ready, 1)
            dve.wait_ge(idf_ready, 1)
            nc.vector.tensor_tensor(frames[:, :, :],
                                    frame_idf[:, :].unsqueeze(2).to_broadcast([NFFT, NBT, V]),
                                    iota_v[:, :].unsqueeze(1).to_broadcast([NFFT, NBT, V]),
                                    ALU.is_equal).then_inc(frames_ready, 1)
            for g in range(GROUPS):
                n = min(PER, NBT - g * PER)
                dve.wait_ge(squares_ready, g + 1)
                sq = squares[:, g % 2, 0:n, :]
                nc.vector.tensor_tensor(mag[:, :, g * PER:g * PER + n], sq[:, :, 0:FREQS].rearrange("v n f -> v f n"),
                                        sq[:, :, FREQS:C2].rearrange("v n f -> v f n"), ALU.add).then_inc(power_ready, 1)
            for h in range(2):
                dve.wait_ge(proj_ready, h + 1)
                nc.vector.tensor_copy(pf[:, h, :], pproj[:, h, 0:D_STFT]).then_inc(pf_ready, 1)
            nc.vector.sem_inc(onehot_ready, 2)
            with dve.Fori(0, PAIRS) as j:
                for k in range(2):
                    dve.wait_ge(ids_in[k], j * 16 + 16)
                    dve.wait_ge(tok_ready, j * 8 + k * 4 + 4)
                    nc.vector.tensor_scalar(onehot[:, k, :], ids_row[:, k, :], part_id[:, 0:1], None, ALU.is_equal
                                            ).then_inc(onehot_ready, 1)

        @block.scalar
        def _(act):
            for g in range(GROUPS):
                n = min(PER, NBT - g * PER)
                act.wait_ge(spec_ready, g + 1)
                if g >= 2:
                    act.wait_ge(power_ready, g - 1)
                nc.scalar.activation(squares[:, g % 2, 0:n, :],
                                     spec[:, g % 2, 0:n * C2].rearrange("v (n f) -> v n f", n=n), ACT.Square
                                     ).then_inc(squares_ready, 1)
            act.wait_ge(power_ready, GROUPS)
            nc.scalar.activation(mag[:, :, :], mag[:, :, :], ACT.Sqrt).then_inc(mag_ready, 1)
            with act.Fori(0, PAIRS) as j:
                for k in range(2):
                    for q in range(TPB):
                        act.wait_ge(tok_ready, j * 8 + k * 4 + q + 9)
                        nc.scalar.activation(H[:, bass.ds(j * 8 + k * 4 + q, 1), :], tok[:, q, 0:D].unsqueeze(1), ACT.Copy
                                             ).then_inc(tok_copied, 1)

        @block.tensor
        def _(pe):
            pe.sem_inc(tok_ready, 8)
            pe.wait_ge(frames_ready, 1)
            pe.wait_ge(wdft_ready, 1)
            for g in range(GROUPS):
                n = min(PER, NBT - g * PER)
                if g >= 2:
                    pe.wait_ge(squares_ready, g - 1)
                for i in range(n):
                    mm = nc.tensor.matmul(spec[:, g % 2, i * C2:(i + 1) * C2], frames[:, g * PER + i, :], wdft[:, :],
                                          start=True, stop=True)
                mm.then_inc(spec_ready, 1)
            pe.wait_ge(mag_ready, 1)
            pe.wait_ge(weights_in, 32)
            for h in range(2):
                for f in range(FREQS):
                    mm = nc.tensor.matmul(pproj[:, h, 0:D_STFT], mag[:, f, h * HALF:(h + 1) * HALF], proj_w[:, f, :],
                                          start=f == 0, stop=f == FREQS - 1)
                mm.then_inc(proj_ready, 1)
            pe.wait_ge(bias_in, 16 * B)
            pe.wait_ge(interp_in, 16)
            pe.wait_ge(pf_back, 16)
            pe.sem_inc(tok_copied, 4)
            with pe.Fori(0, PAIRS) as j:
                for k in range(2):
                    pe.wait_ge(onehot_ready, j * 2 + k + 3)
                    for q in range(TPB):
                        pe.wait_ge(tok_copied, j * 8 + k * 4 + q + 1)
                        nc.tensor.matmul(tok[:, q, 0:D_EMB], onehot[:, k, q * P:(q + 1) * P], emb[:, :],
                                         start=True, stop=True)
                        nc.tensor.matmul(tok[:, q, D_EMB:D], interp[:, q * P:(q + 1) * P],
                                         pfb[:, bass.ds(j * 2 + k, 1), :].squeeze(1),
                                         start=True, stop=True).then_inc(tok_ready, 1)


def pe_transpose(nc, out, in_, ident):
    return nc.tensor.transpose(out, in_, ident)


def diff_attention(nc, A, S, H):
    NPAIR, HD, VD = 8, 16, 32
    VO = VD + 1
    LAST = B - 1
    with ExitStack() as ctx:
        m = Bufs(nc, ctx, "dif")
        wqk, wv, wo = m.sb("wqk", [P, 2, 2 * D]), m.sb("wv", [P, 2, D]), m.sb("wo", [P, 2, D])
        ident, upper, rot = m.sb("ident", [P, P]), m.sb("upper", [P, P]), m.sb("rot", [P, 2, TPB, HD])
        lam_in, lam_prod, lam = m.sb("lam_in", [P, 2, 2, 8]), m.sb("lam_prod", [P, 2, 8]), m.sb("lam", [P, 4])
        pause = m.sb("pause", [P, 1])
        bn, mv, rstd = m.sb("bn", [P, TPB, 6]), m.sb("mv", [P, TPB, 2]), m.sb("rstd", [P, TPB])
        var, half_neg = m.sb("var", [P, TPB]), m.sb("half_neg", [P, TPB * 32])
        eps, rms_eps = m.sb("eps", [P, TPB]), m.sb("rms_eps", [P, TPB * 32])
        xn, xT = m.sb("xn", [P, TPB, D]), m.sb("xT", [P, 2, T])
        qk, sq = m.sb("qk", [P, TPB, 2 * D]), m.sb("sq", [P, TPB, 2 * D])
        ss, rr = m.sb("ss", [P, TPB * 32]), m.sb("rr", [P, TPB * 32])
        rc = m.sb("rc", [P, TPB, 2 * D])
        q, kp = m.sb("q", [P, TPB, D]), m.sb("kp", [P, TPB, 2, 8, 32])
        qT, kT = m.sb("qT", [P, 2, T]), m.sb("kT", [P, 4, T])
        v1 = m.sb("v1", [P, TPB, NPAIR, VO])
        prob = m.sb("prob", [P, 2, 2, 2560])
        rsum, parts = m.sb("rsum", [P, 2 * TPB]), m.sb("parts", [P, 2 * TPB, VD])
        y, yT = m.sb("y", [P, TPB, D]), m.sb("yT", [P, 2, T])
        score = [m.ps(f"score{i}", [P, 2, 512]) for i in range(2)]
        av = [m.ps(f"av{i}", [P, 512]) for i in range(2)]
        work = [m.ps(f"work{i}", [P, 512]) for i in range(2)]

        loaded, zeroed, lam_step = m.sem("loaded"), m.sem("zeroed"), m.sem("lam_step")
        bn_done, aggr_done, var_done, rstd_ready, xn_ready = (m.sem(s) for s in ("bn_done", "aggr_done", "var_done", "rstd_ready", "xn_ready"))
        work_full, work_copied = m.sem("work_full"), [m.sem(f"work_copied{i}") for i in range(2)]
        sq_ready, ss_ready, ms_ready, rms_ready = (m.sem(s) for s in ("sq_ready", "ss_ready", "ms_ready", "rms_ready"))
        rot_step, qk_ready = m.sem("rot_step"), m.sem("qk_ready")
        score_full, score_exped = m.sem("score_full"), m.sem("score_exped")
        masked, av_done, av_read, fin_step, y_ready = (m.sem(s) for s in ("masked", "av_done", "av_read", "fin_step", "y_ready"))
        h_done = m.sem("h_done")
        block = ctx.enter_context(nc.Block())

        def full_at(hb, e):
            return hb * 2 + (e + 1)

        def claim_at(hb, e):
            return hb + (e // 2 + 1)

        def copied_at(hb, e):
            return hb + (e // 2 + 2)

        @block.sync
        def _(sp):
            for dst, src in ((wqk[:, :, :], A["wqk"]), (wv[:, :, :], A["wv"]), (wo[:, :, :], A["wo"]), (ident[:, :], A["ident"]),
                             (upper[:, :], A["upper"]), (rot[:, :, :, :], A["rot"])):
                sp.dma_start(dst, src).then_inc(loaded, 16)
            sp.dma_start(lam_in[:, :, :, :], A["lambdas"].partition_broadcast(P)).then_inc(loaded, 16)
        LOADED = 16 * 7

        def norm_stats(dve, b):
            for t in range(TPB):
                nc.vector.bn_stats(bn[:, t, :], H[:, bass.ds(b * TPB + t, 1), :].squeeze(1)).then_inc(bn_done, 1)
            dve.wait_ge(bn_done, b * TPB + TPB)
            nc.vector.memset(pause[:, :], 0.0)
            for t in range(TPB):
                nc.vector.bn_aggr(mv[:, t, :], bn[:, t, :]).then_inc(aggr_done, 1)

        def norm_apply(dve, b):
            dve.wait_ge(rstd_ready, b + 1)
            for t in range(TPB):
                nc.vector.tensor_scalar(xn[:, t, :], H[:, bass.ds(b * TPB + t, 1), :].squeeze(1), mv[:, t, 0:1],
                                        rstd[:, t:t + 1], ALU.subtract, ALU.mult).then_inc(xn_ready, 1)

        def head_sums(dve, b):
            for t in range(TPB):
                dve.wait_ge(sq_ready, b * TPB + t + 1)
                nc.vector.tensor_reduce(ss[:, t * 32:(t + 1) * 32], sq[:, t, :].rearrange("p (h d) -> p h d", d=HD),
                                        AX.X, ALU.add).then_inc(ss_ready, 1)

        def rotate(dve, b):
            dve.wait_ge(rms_ready, b + 1)
            every = lambda x: x[:, :, :].rearrange("p t (h d) -> p (t h) d", d=HD)
            nc.vector.tensor_tensor(every(rc), every(qk), rr[:, :].unsqueeze(2).to_broadcast([P, TPB * 32, HD]),
                                    ALU.mult).then_inc(rot_step, 1)
            dve.wait_ge(rot_step, b * 4 + 1)
            by = lambda x: x[:, :, :].rearrange("p t (h d) -> p t h d", d=HD)
            cs = lambda i, a, z: rot[:, i, :, a:z].unsqueeze(2).to_broadcast([P, TPB, 32, z - a])
            nc.vector.tensor_tensor(by(sq)[:, :, :, 0:8], by(rc)[:, :, :, 8:16], cs(1, 0, 8), ALU.mult).then_inc(rot_step, 1)
            nc.vector.tensor_tensor(by(sq)[:, :, :, 8:16], by(rc)[:, :, :, 0:8], cs(1, 8, 16), ALU.mult).then_inc(rot_step, 1)
            dve.wait_ge(rot_step, b * 4 + 3)
            nc.vector.tensor_tensor(by(rc), by(rc), cs(0, 0, 16), ALU.mult).then_inc(rot_step, 1)
            dve.wait_ge(rot_step, b * 4 + 4)
            nc.vector.tensor_tensor(q[:, :, :], rc[:, :, 0:D], sq[:, :, 0:D], ALU.add).then_inc(qk_ready, 1)
            for ver in range(2):
                pick = lambda x: x[:, :, D:2 * D].rearrange("p t (s v d) -> p t s v d", v=2, d=HD)[:, :, :, ver, :]
                nc.vector.tensor_tensor(kp[:, :, ver, :, ver * HD:(ver + 1) * HD], pick(rc), pick(sq), ALU.add
                                        ).then_inc(qk_ready, 1)

        def copy_v(dve, b, hb):
            for x in range(2):
                dve.wait_ge(work_full, full_at(hb, 6 + x))
                nc.vector.tensor_copy(v1[:, 2 * x:2 * x + 2, :, 0:VD].rearrange("p t j d -> p t j d"),
                                      work[x][:, :].rearrange("p (t j d) -> p t j d", t=2, d=VD)).then_inc(work_copied[x], 1)

        def copy_qT(dve, hb):
            for e in range(2):
                dve.wait_ge(work_full, full_at(hb, 8 + e))
                nc.vector.tensor_copy(qT[:, e, :], work[e][:, :]).then_inc(work_copied[e], 1)

        def finish_unit(dve, b, j):
            dve.wait_ge(av_done, b * NPAIR + j + 3)
            o = av[j % 2][:, 0:2 * TPB * VO].rearrange("p (g c) -> p g c", c=VO)
            nc.vector.reciprocal(rsum[:, :], o[:, :, VD:VO].squeeze(2)).then_inc(fin_step, 1)
            dve.wait_ge(fin_step, (b * NPAIR + j) * 2 + 1)
            nc.vector.tensor_scalar(rsum[:, TPB:2 * TPB], rsum[:, TPB:2 * TPB], lam[:, 2:3], None, ALU.mult).then_inc(fin_step, 1)
            dve.wait_ge(fin_step, (b * NPAIR + j) * 2 + 2)
            nc.vector.tensor_tensor(parts[:, :, :], o[:, :, 0:VD], rsum[:, :].unsqueeze(2).to_broadcast([P, 2 * TPB, VD]),
                                    ALU.mult).then_inc(av_read, 1)
            dve.wait_ge(av_read, b * NPAIR + j + 3)
            nc.vector.tensor_tensor(y[:, :, j * VD:(j + 1) * VD], parts[:, 0:TPB, :], parts[:, TPB:2 * TPB, :], ALU.subtract
                                    ).then_inc(y_ready, 1)

        def add_out(dve, b, hb, e0):
            for x in range(2):
                dve.wait_ge(work_full, full_at(hb, e0 + 2 + x))
                hh = H[:, bass.ds(b * TPB + 2 * x, 2), :]
                nc.vector.tensor_tensor(hh, work[x][:, :].rearrange("p (t d) -> p t d", t=2), hh, ALU.add
                                        ).then_inc(work_copied[x], 1)

        @block.vector
        def _(dve):
            nc.vector.memset(half_neg[:, :], -0.5).then_inc(zeroed, 1)
            nc.vector.memset(eps[:, :], LN_EPS).then_inc(zeroed, 1)
            nc.vector.memset(rms_eps[:, :], RMS_EPS * HD).then_inc(zeroed, 1)
            nc.vector.memset(kp[:, :, :, :, :], 0.0).then_inc(zeroed, 1)
            nc.vector.memset(v1[:, :, :, VD:VO], 1.0).then_inc(zeroed, 1)
            nc.vector.sem_inc(av_read, 2)
            dve.wait_ge(zeroed, 5)
            dve.wait_ge(loaded, LOADED)
            nc.vector.tensor_tensor(lam_prod[:, :, :], lam_in[:, :, 0, :], lam_in[:, :, 1, :], ALU.mult).then_inc(lam_step, 1)
            dve.wait_ge(lam_step, 1)
            nc.vector.tensor_reduce(lam[:, 0:2], lam_prod[:, :, :], AX.X, ALU.add).then_inc(lam_step, 1)
            dve.wait_ge(lam_step, 3)
            nc.vector.tensor_tensor(lam[:, 2:3], lam[:, 0:1], lam[:, 1:2], ALU.subtract).then_inc(lam_step, 1)
            dve.wait_ge(lam_step, 4)
            nc.vector.tensor_scalar(lam[:, 2:3], lam[:, 2:3], LAMBDA_INIT, None, ALU.add).then_inc(lam_step, 1)
            dve.wait_ge(lam_step, 5)
            norm_stats(dve, 0)
            norm_apply(dve, 0)
            head_sums(dve, 0)
            rotate(dve, 0)
            copy_v(dve, 0, 0)
            copy_qT(dve, 0)

            def batch(b, hb, more):
                if more:
                    norm_stats(dve, b + 1)
                    norm_apply(dve, b + 1)
                for j in range(NPAIR):
                    finish_unit(dve, b, j)
                    if more and j == 4:
                        head_sums(dve, b + 1)
                    if more and j == 5:
                        rotate(dve, b + 1)
                if more:
                    copy_v(dve, b + 1, hb)
                    copy_qT(dve, hb)
                add_out(dve, b, hb, 14 if more else 0)

            with dve.Fori(0, LAST) as i:
                batch(i, i * 9 + 7, True)
            batch(LAST, LAST * 9 + 7, False)

        @block.gpsimd
        def _(pool):
            def norm_pow(b):
                pool.wait_ge(aggr_done, b * TPB + TPB)
                nc.gpsimd.tensor_tensor(var[:, :], mv[:, :, 1:2].squeeze(2), eps[:, 0:TPB], ALU.add).then_inc(var_done, 1)
                pool.wait_ge(var_done, b + 1)
                nc.gpsimd.tensor_tensor(rstd[:, :], var[:, :], half_neg[:, 0:TPB], ALU.pow).then_inc(rstd_ready, 1)

            def squares(b, hb):
                for t in range(TPB):
                    pool.wait_ge(work_copied[t % 2], copied_at(hb, 2 + t))
                    nc.gpsimd.tensor_tensor(sq[:, t, :], qk[:, t, :], qk[:, t, :], ALU.mult).then_inc(sq_ready, 1)

            def rms_pow(b):
                pool.wait_ge(ss_ready, b * TPB + TPB)
                nc.gpsimd.tensor_tensor(ss[:, :], ss[:, :], rms_eps[:, :], ALU.add).then_inc(ms_ready, 1)
                pool.wait_ge(ms_ready, b + 1)
                nc.gpsimd.tensor_tensor(rr[:, :], ss[:, :], half_neg[:, :], ALU.pow).then_inc(rms_ready, 1)

            def mask_unit(b, j):
                pool.wait_ge(score_exped, (b * NPAIR + j) * 4 + 6)
                diag = prob[:, j % 2, :, :].rearrange("p h (k s) -> p h k s", s=640)[:, :, :, 0:P]
                nc.gpsimd.tensor_tensor(diag, diag, upper[:, :].unsqueeze(1).unsqueeze(1).to_broadcast([P, 2, TPB, P]),
                                        ALU.mult).then_inc(masked, 1)

            pool.wait_ge(zeroed, 5)
            pool.wait_ge(loaded, LOADED)
            norm_pow(0)
            squares(0, 0)
            rms_pow(0)

            def batch(b, hb, more):
                if more:
                    norm_pow(b + 1)
                for j in range(NPAIR):
                    mask_unit(b, j)
                    if more and j == 4:
                        squares(b + 1, hb)
                    if more and j == 5:
                        rms_pow(b + 1)

            with pool.Fori(0, LAST) as i:
                batch(i, i * 9 + 7, True)
            batch(LAST, LAST * 9 + 7, False)

        @block.scalar
        def _(act):
            def copy(hb, e, dst):
                act.wait_ge(work_full, full_at(hb, e))
                nc.scalar.activation(dst, work[e % 2][:, :], ACT.Copy).then_inc(work_copied[e % 2], 1)

            def copy_xT(hb):
                for c in range(2):
                    copy(hb, c, xT[:, c, :])

            def copy_qk(b, hb):
                for t in range(TPB):
                    copy(hb, 2 + t, qk[:, t, :])

            def copy_kT(hb):
                for e in range(4):
                    copy(hb, 10 + e, kT[:, e, :])

            for k in range(2):
                nc.scalar.sem_inc(work_copied[k], 1)
            nc.scalar.sem_inc(score_exped, 2)
            act.wait_ge(lam_step, 2)
            nc.scalar.activation(lam[:, 0:2], lam[:, 0:2], ACT.Exp).then_inc(lam_step, 1)
            copy_xT(0)
            copy_qk(0, 0)
            copy_kT(0)

            def batch(b, hb, more):
                for j in range(NPAIR):
                    act.wait_ge(av_done, b * NPAIR + j + 1)
                    for kc in range(TPB):
                        act.wait_ge(score_full, (b * NPAIR + j) * 4 + kc + 1)
                        n = T - kc * P
                        nc.scalar.activation(prob[:, j % 2, :, kc * (T + P):kc * T + T], score[kc % 2][:, :, 0:n], ACT.Exp,
                                             scale=HD ** 0.5).then_inc(score_exped, 1)
                    if more and j == 1:
                        copy_xT(hb)
                    if more and j == 4:
                        copy_qk(b + 1, hb)
                if more:
                    copy_kT(hb)
                for c in range(2):
                    copy(hb, (14 if more else 0) + c, yT[:, c, :])

            with act.Fori(0, LAST) as i:
                batch(i, i * 9 + 7, True)
            batch(LAST, LAST * 9 + 7, False)

        @block.tensor
        def _(pe):
            def flip(hb, e, src):
                pe.wait_ge(work_copied[e % 2], claim_at(hb, e))
                for t in range(TPB):
                    mm = nc.tensor.transpose(work[e % 2][:, t * P:(t + 1) * P], src(t), ident[:, :])
                mm.then_inc(work_full, 1)

            def turn_x(b, hb):
                pe.wait_ge(xn_ready, b * TPB + TPB)
                for c in range(2):
                    flip(hb, c, lambda t: xn[:, t, c * P:(c + 1) * P])

            def mul(hb, e, n, src, w, cols):
                pe.wait_ge(work_copied[e % 2], claim_at(hb, e))
                for i, t in enumerate(cols):
                    for c in range(2):
                        mm = nc.tensor.matmul(work[e % 2][:, i * n:(i + 1) * n], src[:, c, t * P:(t + 1) * P], w[:, c, :],
                                              start=c == 0, stop=c == 1)
                mm.then_inc(work_full, 1)

            def make_qk(hb):
                for k in range(2):
                    pe.wait_ge(work_copied[k], copied_at(hb, k))
                for t in range(TPB):
                    mul(hb, 2 + t, 2 * D, xT, wqk, [t])

            def make_v_turn_qk(b, hb):
                for x in range(2):
                    mul(hb, 6 + x, D, xT, wv, [2 * x, 2 * x + 1])
                pe.wait_ge(qk_ready, b * 3 + 3)
                for c in range(2):
                    flip(hb, 8 + c, lambda t: q[:, t, c * P:(c + 1) * P])
                for e in range(4):
                    ver, half = e % 2, e // 2
                    flip(hb, 10 + e, lambda t: kp[:, t, ver, half * 4:half * 4 + 4, :].rearrange("p s d -> p (s d)"))

            def scores(b, j):
                for kc in range(TPB):
                    pe.wait_ge(score_exped, (b * NPAIR + j) * 4 + kc + 1)
                    for half in range(2):
                        s = (j // 2 + 2 * half) % 4
                        r = slice(32 * s, 32 * s + 32)
                        mm = nc.tensor.matmul(score[kc % 2][:, half, 0:T - kc * P], kT[r, half * 2 + j % 2, kc * P:(kc + 1) * P],
                                              qT[r, half, kc * P:T], start=True, stop=True)
                    mm.then_inc(score_full, 1)

            def values(b, j):
                pe.wait_ge(masked, b * NPAIR + j + 1)
                pe.wait_ge(av_read, b * NPAIR + j + 1)
                for half in range(2):
                    for qc in range(TPB):
                        g = half * TPB + qc
                        for kc in range(qc + 1):
                            at = kc * T + qc * P
                            mm = nc.tensor.matmul(av[j % 2][:, g * VO:(g + 1) * VO], prob[:, j % 2, half, at:at + P],
                                                  v1[:, kc, j, :], start=kc == 0, stop=kc == qc)
                mm.then_inc(av_done, 1)

            def project(b, hb, e0):
                pe.wait_ge(y_ready, b * NPAIR + NPAIR)
                for c in range(2):
                    flip(hb, e0 + c, lambda t: y[:, t, c * P:(c + 1) * P])
                for k in range(2):
                    pe.wait_ge(work_copied[k], copied_at(hb, e0 + k))
                for x in range(2):
                    mul(hb, e0 + 2 + x, D, yT, wo, [2 * x, 2 * x + 1])

            nc.tensor.sem_inc(av_done, 2)
            pe.wait_ge(loaded, LOADED)
            turn_x(0, 0)
            make_qk(0)
            make_v_turn_qk(0, 0)

            def batch(b, hb, prev, more):
                for e in range(6, 14):
                    pe.wait_ge(work_copied[e % 2], copied_at(prev, e))
                scores(b, 0)
                for j in range(NPAIR):
                    if j + 1 < NPAIR:
                        scores(b, j + 1)
                    if more and j == 0:
                        turn_x(b + 1, hb)
                    if more and j == 3:
                        make_qk(hb)
                    values(b, j)
                if more:
                    make_v_turn_qk(b + 1, hb)
                project(b, hb, 14 if more else 0)

            with pe.Fori(0, LAST) as i:
                batch(i, i * 9 + 7, i * 9 + 0, True)
            batch(LAST, LAST * 9 + 7, LAST * 9 - 2, False)


def expert_stream(nc, m, N, I, STEP, *, turn_ready, x_of, down_of, mul_ready, mul_also, identT,
                  dve_more, act_first, act_more, pool_prog, sync_prog, finish, prologue_dve, dve_before):
    NI = I // P
    xT, gs, hs, hT = (m.sb(s, sh) for s, sh in (("xT", [P, 2, 2, P]), ("gs", [P, 2, I]), ("hs", [P, 2, I]), ("hT", [P, 2, NI, P])))
    pT, pG, pU, pD = ([m.ps(f"{s}{k}", [P, 512]) for k in range(2)] for s in ("pT", "pG", "pU", "pD"))
    names = ("x_turned", "xT_ready", "gu_full", "silu_ready", "hs_ready", "h_turned", "hT_ready", "down_full", "down_read")
    s = {x: m.sem(x) for x in names}
    block = m.ctx.enter_context(nc.Block())

    def steps(eng, step):
        with eng.Fori(0, N // STEP - 1) as i:
            for q in range(STEP):
                step(i * STEP + q, q % 2, q, i, STEP)
        for q in range(STEP):
            step(N - STEP + q, q % 2, q, N // STEP - 1, STEP - 1 - q)

    @block.tensor
    def _(pe):
        for x, n in (("x_turned", 4), ("gu_full", 1), ("h_turned", 2), ("down_full", 1)):
            pe.sem_inc(s[x], n)

        def turn(n, k, q, i):
            turn_ready(pe, n, q, i)
            pe.wait_ge(s["xT_ready"], n + 1)
            for c in range(2):
                mm = nc.tensor.transpose(pT[k][:, c * P:(c + 1) * P], x_of(n, q, c), identT[:, :])
            mm.then_inc(s["x_turned"], 1)

        def multiply(n, k, i):
            gate, up = mul_ready(pe, n, i)
            pe.wait_ge(s["xT_ready"], n + 3)
            pe.wait_ge(s["hs_ready"], n + 1)
            mul_also(pe, n, k, xT, pT)
            for w, bank in ((gate, pG), (up, pU)):
                for c in range(2):
                    mm = nc.tensor.matmul(bank[k][:, 0:I], xT[:, k, c, :], w(c), start=c == 0, stop=c == 1)
            mm.then_inc(s["gu_full"], 1)

        def turn_h(n, k):
            pe.wait_ge(s["hs_ready"], n + 3)
            pe.wait_ge(s["down_read"], n + 1)
            for c in range(NI):
                mm = nc.tensor.transpose(pD[k][:, c * P:(c + 1) * P], hs[:, k, c * P:(c + 1) * P], identT[:, :])
            mm.then_inc(s["h_turned"], 1)

        def down(n, k, i):
            w = down_of(pe, n, i)
            pe.wait_ge(s["hT_ready"], n + 1)
            for c in range(NI):
                mm = nc.tensor.matmul(pD[k][:, 0:D], hT[:, k, c, :], w(c), start=c == 0, stop=c == NI - 1)
            mm.then_inc(s["down_full"], 1)

        turn(0, 0, 0, 0)
        turn(1, 1, 1, 0)
        multiply(0, 0, 0)

        def step(n, k, q, i, left):
            if left >= 2:
                turn(n + 2, k, (q + 2) % STEP, i + (q + 2) // STEP)
            turn_h(n, k)
            if left >= 1:
                multiply(n + 1, 1 - k, i + (q + 1) // STEP)
            down(n, k, i)

        steps(pe, step)

    @block.scalar
    def _(act):
        act.sem_inc(s["xT_ready"], 2)

        def copy_x(n, k):
            act.wait_ge(s["x_turned"], n + 5)
            nc.scalar.activation(xT[:, k, :, :], pT[k][:, 0:D].rearrange("p (c t) -> p c t", c=2), ACT.Copy).then_inc(s["xT_ready"], 1)

        def silu(n, k):
            act.wait_ge(s["gu_full"], n + 2)
            act.wait_ge(s["hs_ready"], n + 1)
            nc.scalar.activation(gs[:, k, :], pG[k][:, 0:I], ACT.Silu).then_inc(s["silu_ready"], 1)

        def copy_h(n, k):
            act.wait_ge(s["h_turned"], n + 3)
            nc.scalar.activation(hT[:, k, :, :], pD[k][:, 0:NI * P].rearrange("p (c t) -> p c t", c=NI), ACT.Copy).then_inc(s["hT_ready"], 1)

        act_first(act, s)
        copy_x(0, 0)
        copy_x(1, 1)
        silu(0, 0)

        def step(n, k, q, i, left):
            if left >= 2:
                copy_x(n + 2, k)
            copy_h(n, k)
            if left >= 1:
                silu(n + 1, 1 - k)
            act_more(act, n, k, q, i, left, s)

        steps(act, step)

    @block.vector
    def _(dve):
        dve.sem_inc(s["hs_ready"], 2)
        dve.sem_inc(s["down_read"], 2)
        prologue_dve(dve)

        def gated(n, k):
            dve.wait_ge(s["silu_ready"], n + 1)
            dve.wait_ge(s["h_turned"], n + 1)
            nc.vector.tensor_tensor(hs[:, k, :], gs[:, k, :], pU[k][:, 0:I], ALU.mult).then_inc(s["hs_ready"], 1)

        dve_more(dve, 0, 0, pT)
        gated(0, 0)
        

        def step(n, k, q, i, left):
            dve_before(dve, n, q, i, left, s)
            if left >= 1:
                dve_more(dve, n + 1, 1 - k, pT)
                gated(n + 1, 1 - k)
            finish(dve, n, k, q, i, left, s, pD)

        steps(dve, step)

    if pool_prog:
        @block.gpsimd
        def _(pool):
            pool_prog(pool, s)

    if sync_prog:
        @block.sync
        def _(sp):
            sync_prog(sp, s, steps)


def zero_rows(sp, dram, rows, zeros, zeroed):
    v = dram.rearrange("(g p r) d -> g p (r d)", p=P, r=8)
    for g in range(rows // (8 * P)):
        sp.dma_start(v[g], zeros[:, :]).then_inc(zeroed, 16)
    sp.wait_ge(zeroed, 16 * (rows // (8 * P)))


class Norm:

    def __init__(self, m):
        self.pause = m.sb("pause", [P, 1])
        self.bn, self.mv = m.sb("bn", [P, TPB, 6]), m.sb("mv", [P, TPB, 2])
        self.var, self.rstd = m.sb("var", [P, TPB]), m.sb("rstd", [P, TPB])
        self.eps, self.half_neg = m.sb("eps", [P, TPB]), m.sb("half_neg", [P, TPB])
        self.bn_done, self.aggr_done = m.sem("bn_done"), m.sem("aggr_done")
        self.var_done, self.rstd_ready, self.set = m.sem("var_done"), m.sem("rstd_ready"), m.sem("norm_set")

    def constants(self, nc):
        nc.vector.memset(self.eps[:, :], LN_EPS).then_inc(self.set, 1)
        nc.vector.memset(self.half_neg[:, :], -0.5).then_inc(self.set, 1)

    def stats(self, nc, dve, H, g):
        for t in range(TPB):
            nc.vector.bn_stats(self.bn[:, t, :], H[:, bass.ds(g * TPB + t, 1), :].squeeze(1)).then_inc(self.bn_done, 1)
        dve.wait_ge(self.bn_done, g * TPB + TPB)
        nc.vector.memset(self.pause[:, :], 0.0)
        for t in range(TPB):
            nc.vector.bn_aggr(self.mv[:, t, :], self.bn[:, t, :]).then_inc(self.aggr_done, 1)

    def power(self, nc, pool, g):
        pool.wait_ge(self.aggr_done, g * TPB + TPB)
        nc.gpsimd.tensor_tensor(self.var[:, :], self.mv[:, :, 1:2].squeeze(2), self.eps[:, :], ALU.add).then_inc(self.var_done, 1)
        pool.wait_ge(self.var_done, g + 1)
        nc.gpsimd.tensor_tensor(self.rstd[:, :], self.var[:, :], self.half_neg[:, :], ALU.pow).then_inc(self.rstd_ready, 1)

    def apply(self, nc, dve, H, g, dst, ready):
        dve.wait_ge(self.rstd_ready, g + 1)
        for t in range(TPB):
            nc.vector.tensor_scalar(dst(t), H[:, bass.ds(g * TPB + t, 1), :].squeeze(1), self.mv[:, t, 0:1],
                                    self.rstd[:, t:t + 1], ALU.subtract, ALU.mult).then_inc(ready, 1)


E1, I1 = 32, 512
SORT_TILES = 96
RING = 4


def top1_experts(nc, A, S, H):
    with ExitStack() as outer:
        m = Bufs(nc, outer, "t1")
        slot = m.sb("slot", [P, TILES], I32)
        tile_tab = m.sb("tile_tab", [P, 2, SORT_TILES], I32)
        end_tab = m.sb("end_tab", [P, RING + E1], I32)
        with ExitStack() as both:
            m = Bufs(nc, both, "t1n")
            xs = m.sb("xs", [P, TILES, D])
            top, top_i = m.sb("top", [P, TILES]), m.sb("top_i", [P, TILES])
            shared_expert(nc, A, S, H, xs, top, top_i)
            sort_tokens(nc, A, S, xs, top, top_i, slot, tile_tab, end_tab)
        routed_experts(nc, A, S, tile_tab, end_tab)
        gather_add(nc, S, H, slot)


def shared_expert(nc, A, S, H, xs, top, top_i):
    with ExitStack() as ctx:
        m = Bufs(nc, ctx, "sh")
        wg, wu, wd = m.sb("wg", [P, 2, I1]), m.sb("wu", [P, 2, I1]), m.sb("wd", [P, I1 // P, D])
        wr, ident = m.sb("wr", [P, 2, E1]), m.sb("ident", [P, P])
        xn = m.sb("xn", [P, TPB, D])
        zeros = m.sb("zeros", [P, 2048])
        norm, xn_ready = Norm(m), m.sem("xn_ready")
        loaded, xs_ready, zero_set, zeroed = m.sem("loaded"), m.sem("xs_ready"), m.sem("zero_set"), m.sem("zeroed")
        max_ready, index_ready, routed, logits_full = (m.sem(s) for s in ("max_ready", "index_ready", "routed", "logits_full"))
        pause = norm.pause
        lg, mx, mi = m.sb("lg", [P, E1]), m.sb("mx", [P, 8]), m.sb("mi", [P, 8], U32)

        def turn_ready(pe, n, q, i):
            pe.wait_ge(loaded, 16 * 5)
            pe.wait_ge(routed, n + 1)
            pe.wait_ge(xn_ready, n + 1)

        def logits(pe, n, k, xT, pT):
            for c in range(2):
                mm = nc.tensor.matmul(pT[k][:, D:D + E1], xT[:, k, c, :], wr[:, c, :], start=c == 0, stop=c == 1)
            mm.then_inc(logits_full, 1)

        def prologue(dve):
            norm.constants(nc)
            dve.sem_inc(routed, 2)
            nc.vector.memset(zeros[:, :], 0.0).then_inc(zero_set, 1)
            norm.stats(nc, dve, H, 0)
            norm.apply(nc, dve, H, 0, lambda t: xn[:, t, :], xn_ready)

        def norm_ahead(dve, n, q, i, left, s):
            if q == 0 and left == 4:
                norm.stats(nc, dve, H, i + 1)
            if q == 1 and left == 4:
                dve.wait_ge(s["x_turned"], i * 4 + 8)
                dve.wait_ge(xs_ready, i * 4 + 4)
                norm.apply(nc, dve, H, i + 1, lambda t: xn[:, t, :], xn_ready)

        def largest(dve, n, k, pT):
            dve.wait_ge(logits_full, n + 1)
            nc.vector.tensor_copy(lg[:, :], pT[k][:, D:D + E1]).then_inc(routed, 1)
            dve.wait_ge(routed, n + 3)
            nc.vector.memset(pause[:, :], 0.0)
            nc.vector.max(mx[:, :], lg[:, :]).then_inc(max_ready, 1)
            dve.wait_ge(max_ready, n + 1)
            nc.vector.memset(pause[:, :], 0.0)
            nc.vector.max_index(mi[:, :], mx[:, :], lg[:, :]).then_inc(index_ready, 1)
            dve.wait_ge(index_ready, n + 1)
            nc.vector.tensor_copy(top[:, bass.ds(n, 1)], mx[:, 0:1])
            nc.vector.tensor_copy(top_i[:, bass.ds(n, 1)], mi[:, 0:1])

        def finish(dve, n, k, q, i, left, s, pD):
            dve.wait_ge(s["down_full"], n + 2)
            hh = H[:, bass.ds(n, 1), :].squeeze(1)
            nc.vector.tensor_tensor(hh, pD[k][:, 0:D], hh, ALU.add).then_inc(s["down_read"], 1)

        def pool_prog(pool, s):
            pool.wait_ge(norm.set, 2)


            def keep(g):
                for t in range(TPB):
                    pool.wait_ge(xn_ready, g * TPB + t + 1)
                    nc.gpsimd.tensor_copy(xs[:, bass.ds(g * TPB + t, 1), :].squeeze(1), xn[:, t, :]).then_inc(xs_ready, 1)

            norm.power(nc, pool, 0)
            keep(0)
            with pool.Fori(0, B - 1) as i:
                norm.power(nc, pool, i + 1)
                keep(i + 1)

        def sync_prog(sp, s, steps):
            for dst, name in ((wg, "sh_gate"), (wu, "sh_up"), (wd, "sh_down"), (wr, "gate_w")):
                sp.dma_start(dst[:, :, :], A[name]).then_inc(loaded, 16)
            sp.dma_start(ident[:, :], A["ident"]).then_inc(loaded, 16)
            sp.wait_ge(zero_set, 1)
            zero_rows(sp, S["sorted_x"], SORT_TILES * P, zeros, zeroed)

        expert_stream(nc, m, TILES, I1, 4, turn_ready=turn_ready, x_of=lambda n, q, c: xn[:, q, c * P:(c + 1) * P],
                      mul_ready=lambda pe, n, i: (lambda c: wg[:, c, :], lambda c: wu[:, c, :]),
                      down_of=lambda pe, n, i: (lambda c: wd[:, c, :]), mul_also=logits, identT=ident, dve_more=largest,
                      act_first=lambda *a: None, act_more=lambda *a: None, pool_prog=pool_prog, sync_prog=sync_prog, finish=finish, prologue_dve=prologue, dve_before=norm_ahead)


def sort_tokens(nc, A, S, xs, top, top_i, slot, tile_tab, end_tab):
    with ExitStack() as ctx:
        m = Bufs(nc, ctx, "st")
        iota, k128 = m.sb("iota", [P, P]), m.sb("k128", [P, P])
        strict_f, strict, ones = m.sb("strict_f", [P, P]), m.sb("strict", [P, P], BF16), m.sb("ones", [P, P], BF16)
        idx, score = m.sb("idx", [P, TILES]), m.sb("score", [P, TILES])
        hot = m.sb("hot", [P, TILES, E1], BF16)
        tot, run, flag = m.sb("tot", [P, E1, TILES]), m.sb("run", [P, E1, TILES]), m.sb("flag", [P, E1, TILES])
        ntile, end, base = m.sb("ntile", [P, E1]), m.sb("end", [P, E1]), m.sb("base", [P, E1])
        tile_e, tile_f = m.sb("tile_e", [P, SORT_TILES, E1]), m.sb("tile_f", [P, SORT_TILES])
        slot_f, score_in = m.sb("slot_f", [P, TILES]), m.sb("score_in", [P, TILES])
        pre = [m.ps(f"pre{g}", [P, 512]) for g in range(4)]
        sums = [m.ps(f"sums{g}", [P, 512]) for g in range(4)]
        loaded, step, counted, score_ready = m.sem("loaded"), m.sem("step"), m.sem("counted"), m.sem("score_ready")
        scaled, scattered = m.sem("scaled"), m.sem("scattered")
        block = ctx.enter_context(nc.Block())
        GT = TILES // 4
        HOT_READY = 4

        @block.sync
        def _(sp):
            for dst, name in ((iota, "iota128"), (k128, "k128"), (strict_f, "strict")):
                sp.dma_start(dst[:, :], A[name]).then_inc(loaded, 16)

        @block.scalar
        def _(act):
            act.wait_ge(step, 1)
            nc.scalar.activation(score[:, :], score_in[:, :], ACT.Sigmoid).then_inc(score_ready, 1)

        @block.tensor
        def _(pe):
            pe.wait_ge(step, 5)
            for g in range(4):
                r = hot[:, g * GT:(g + 1) * GT, :].rearrange("p t e -> p (t e)")
                nc.tensor.matmul(pre[g][:, :], strict[:, :], r, start=True, stop=True).then_inc(counted, 1)
                nc.tensor.matmul(sums[g][:, :], ones[:, :], r, start=True, stop=True).then_inc(counted, 1)

        @block.vector
        def _(dve):
            n = [0]

            def link(ins):
                n[0] += 1
                ins.then_inc(step, 1)
                dve.wait_ge(step, n[0])

            link(nc.vector.tensor_copy(score_in[:, :], top[:, :]))
            dve.wait_ge(loaded, 48)
            link(nc.vector.tensor_copy(idx[:, :], top_i[:, :]))
            link(nc.vector.tensor_copy(strict[:, :], strict_f[:, :]))
            link(nc.vector.memset(ones[:, :], 1.0))
            link(nc.vector.tensor_tensor(hot[:, :, :], iota[:, 0:E1].unsqueeze(1).to_broadcast([P, TILES, E1]),
                                         idx[:, :].unsqueeze(2).to_broadcast([P, TILES, E1]), ALU.is_equal))
            link(nc.vector.memset(flag[:, :, :], 1.0))
            link(nc.vector.memset(flag[:, :, 0:1], 0.0))
            dve.wait_ge(counted, 8)
            for g in range(4):
                link(nc.vector.tensor_copy(tot[:, :, g * GT:(g + 1) * GT], sums[g][:, :].rearrange("p (t e) -> p e t", e=E1)))
            flat = lambda x: x[:, :, :].rearrange("p e t -> p (e t)")
            link(nc.vector.tensor_tensor_scan(flat(run), flat(flag), flat(tot), 0.0, ALU.mult, ALU.add))
            link(nc.vector.tensor_tensor(flag[:, :, :], run[:, :, TILES - 1:TILES].to_broadcast([P, E1, TILES]),
                                         k128[:, 0:TILES].unsqueeze(1).to_broadcast([P, E1, TILES]), ALU.is_gt))
            link(nc.vector.tensor_reduce(ntile[:, :], flag[:, :, :], AX.X, ALU.add))
            link(nc.vector.memset(base[:, :], 1.0))
            link(nc.vector.tensor_tensor_scan(end[:, :], base[:, :], ntile[:, :], 0.0, ALU.mult, ALU.add))
            link(nc.vector.tensor_tensor(base[:, :], end[:, :], ntile[:, :], ALU.subtract))
            link(nc.vector.tensor_scalar(base[:, :], base[:, :], float(P), None, ALU.mult))
            link(nc.vector.tensor_tensor(run[:, :, :], run[:, :, :], tot[:, :, :], ALU.subtract))
            link(nc.vector.tensor_tensor(run[:, :, :], run[:, :, :], base[:, :].unsqueeze(2).to_broadcast([P, E1, TILES]), ALU.add))
            place = tot[:, :, :].rearrange("p e t -> p (e t)").rearrange("p (t e) -> p t e", e=E1)
            for g in range(4):
                link(nc.vector.tensor_tensor(place[:, g * GT:(g + 1) * GT, :], pre[g][:, :].rearrange("p (t e) -> p t e", e=E1),
                                             run[:, :, g * GT:(g + 1) * GT].rearrange("p e t -> p t e"), ALU.add))
            link(nc.vector.tensor_tensor(place, place, hot[:, :, :], ALU.mult))
            link(nc.vector.tensor_reduce(slot_f[:, :], place, AX.X, ALU.add))
            link(nc.vector.tensor_copy(slot[:, :], slot_f[:, :]))
            dve.wait_ge(score_ready, 1)
            for g in range(8):
                nc.vector.tensor_tensor(xs[:, 8 * g:8 * g + 8, :], xs[:, 8 * g:8 * g + 8, :],
                                        score[:, 8 * g:8 * g + 8].unsqueeze(2).to_broadcast([P, 8, D]), ALU.mult).then_inc(scaled, 1)
            link(nc.vector.tensor_tensor(tile_e[:, :, :], end[:, :].unsqueeze(1).to_broadcast([P, SORT_TILES, E1]),
                                         iota[:, 0:SORT_TILES].unsqueeze(2).to_broadcast([P, SORT_TILES, E1]), ALU.is_le))
            link(nc.vector.tensor_reduce(tile_f[:, :], tile_e[:, :, :], AX.X, ALU.add))
            link(nc.vector.tensor_scalar(tile_f[:, :], tile_f[:, :], float(E1 - 1), None, ALU.min))
            link(nc.vector.tensor_copy(tile_tab[:, 0, :], tile_f[:, :]))
            link(nc.vector.tensor_scalar(tile_tab[:, 1, :], tile_tab[:, 0, :], RING - 1, None, ALU.bitwise_and))
            link(nc.vector.memset(end_tab[:, :], 0))
            link(nc.vector.tensor_copy(end_tab[:, RING:RING + E1], end[:, :]))

        @block.gpsimd
        def _(pool):
            for t in range(TILES):
                pool.wait_ge(scaled, t // 8 + 1)
                nc.gpsimd.indirect_dma_start(S["sorted_x"], bass.IndirectOffsetOnAxis(ap=slot[:, t:t + 1], axis=0),
                                             xs[:, t, :], None).then_inc(scattered, 16)
            pool.wait_ge(scattered, 16 * TILES)


def routed_experts(nc, A, S, tile_tab, end_tab):
    with ExitStack() as ctx:
        m = Bufs(nc, ctx, "ro")
        wgu, wd = m.sb("wgu", [P, RING, 2, 2 * I1]), m.sb("wd", [P, RING, I1 // P, D])
        ident, xt, o = m.sb("ident", [P, P]), m.sb("xt", [P, 4, D]), m.sb("o", [P, 4, D])
        id_in, gu_in, wd_in, gu_go, wd_go = (m.sem(x) for x in ("id_in", "gu_in", "wd_in", "gu_go", "wd_go"))
        x_in = [m.sem(f"x_in{k}") for k in range(4)]
        o_ready, o_out = m.sem("o_ready"), [m.sem(f"o_out{k}") for k in range(4)]
        xv = S["sorted_x"].rearrange("(n p) d -> n p d", p=P)
        yv = S["sorted_y"].rearrange("(n p) d -> n p d", p=P)

        def turn_ready(pe, n, q, i):
            pe.wait_ge(id_in, 16)
            pe.wait_ge(x_in[q], i * 16 + 16)

        def place(pe, n):
            e = pe.value_load(tile_tab[0:1, 0, bass.ds(n, 1)], min_val=0, max_val=E1 - 1)
            r = pe.value_load(tile_tab[0:1, 1, bass.ds(n, 1)], min_val=0, max_val=RING - 1)
            return e, r

        def mul_ready(pe, n, i):
            e, r = place(pe, n)
            pe.wait_ge(gu_in, e * 16 + 16)
            w = lambda a: (lambda c: wgu[:, bass.ds(r, 1), c, a:a + I1].squeeze(1))
            return w(0), w(I1)

        def down_of(pe, n, i):
            e, r = place(pe, n)
            pe.wait_ge(wd_in, e * 16 + 16)
            return lambda c: wd[:, bass.ds(r, 1), c, :].squeeze(1)

        def finish(dve, n, k, q, i, left, s, pD):
            dve.wait_ge(s["down_full"], n + 2)
            dve.wait_ge(o_out[q], i * 16 + 16)
            nc.vector.tensor_copy(o[:, q, :], pD[k][:, 0:D]).then_inc(s["down_read"], 1)

        def act_first(act, s):
            for k in range(4):
                act.dma_start(xt[:, k, :], xv[k]).then_inc(x_in[k], 16)
                act.sem_inc(o_out[k], 16)

        def act_more(act, n, k, q, i, left, s):
            if left == 4:
                act.wait_ge(s["x_turned"], n + 5)
                act.dma_start(xt[:, q, :], xv[bass.ds(n + 4, 1)].squeeze(0)).then_inc(x_in[q], 16)
            act.wait_ge(s["down_read"], n + 3)
            act.dma_start(yv[bass.ds(n, 1)].squeeze(0), o[:, q, :]).then_inc(o_out[q], 16)
            if left == 0:
                for k in range(4):
                    act.wait_ge(o_out[k], 16 * (SORT_TILES // 4) + 16)

        def load_expert(eng, e, k, dst, src, arrived, used, go, first=False):
            gone = eng.value_load(end_tab[0:1, bass.ds(e, 1)], min_val=0, max_val=SORT_TILES)
            eng.wait_ge(used, gone + 1)
            eng.sem_inc(go, 1)
            if not first:
                eng.wait_ge(arrived, e * 16)
                if src is A["ro_down"]:
                    eng.sem_inc(go, 1)
            eng.dma_start(dst[:, k, :, :], src[bass.ds(e, 1)].squeeze(0)).then_inc(arrived, 16)

        def pool_prog(pool, s):
            for k in range(RING):
                load_expert(pool, k, k, wd, A["ro_down"], wd_in, s["down_full"], wd_go, k == 0)
            with pool.Fori(1, E1 // RING) as i:
                for k in range(RING):
                    load_expert(pool, i * RING + k, k, wd, A["ro_down"], wd_in, s["down_full"], wd_go)

        def sync_prog(sp, s, steps):
            sp.dma_start(ident[:, :], A["ident"]).then_inc(id_in, 16)
            for k in range(RING):
                load_expert(sp, k, k, wgu, A["ro_gu"], gu_in, s["gu_full"], gu_go, k == 0)
            with sp.Fori(1, E1 // RING) as i:
                for k in range(RING):
                    load_expert(sp, i * RING + k, k, wgu, A["ro_gu"], gu_in, s["gu_full"], gu_go)

        expert_stream(nc, m, SORT_TILES, I1, 4, turn_ready=turn_ready, x_of=lambda n, q, c: xt[:, q, c * P:(c + 1) * P],
                      mul_ready=mul_ready, down_of=down_of, mul_also=lambda *a: None, identT=ident,
                      dve_more=lambda *a: None, act_first=act_first, act_more=act_more, pool_prog=pool_prog,
                      sync_prog=sync_prog, finish=finish, prologue_dve=lambda dve: None, dve_before=lambda *a: None)


def gather_add(nc, S, H, slot):
    R = 8
    with ExitStack() as ctx:
        m = Bufs(nc, ctx, "ga")
        g = m.sb("g", [P, R, D])
        got, added = [m.sem(f"got{r}") for r in range(R)], m.sem("added")
        block = ctx.enter_context(nc.Block())

        @block.gpsimd
        def _(pool):
            for t in range(TILES):
                if t >= R:
                    pool.wait_ge(added, t - R + 1)
                nc.gpsimd.indirect_dma_start(g[:, t % R, :], None, S["sorted_y"],
                                             bass.IndirectOffsetOnAxis(ap=slot[:, t:t + 1], axis=0)).then_inc(got[t % R], 16)

        @block.vector
        def _(dve):
            for t in range(TILES):
                dve.wait_ge(got[t % R], 16 * (t // R + 1))
                nc.vector.tensor_tensor(H[:, t, :], H[:, t, :], g[:, t % R, :], ALU.add).then_inc(added, 1)


NH, KEEP = 16, 204
DROP = -1e30


def sparse_attention(nc, A, S, H):
    routing_scores(nc, A, S, H)
    keep_largest(nc, S)
    masked_attention(nc, A, S, H)


def routing_scores(nc, A, S, H):
    HID = 64
    with ExitStack() as ctx:
        m = Bufs(nc, ctx, "rs")
        w1, w2, b1, b2, ident = m.sb("w1", [P, 2, HID]), m.sb("w2", [HID, P]), m.sb("b1", [HID, 1]), m.sb("b2", [NH, 1]), m.sb("ident", [P, P])
        xn, xT = m.sb("xn", [P, TPB, D]), m.sb("xT", [P, 2, 2, T])
        h1, r1, r2 = m.sb("h1", [HID, 2, T]), m.sb("r1", [NH, 2, T]), m.sb("r2", [NH, 2, T])
        norm = Norm(m)
        turn = [m.ps(f"turn{c}", [P, T]) for c in range(2)]
        hid, lg = [m.ps(f"hid{k}", [P, T]) for k in range(2)], [m.ps(f"lg{k}", [P, T]) for k in range(2)]
        loaded, xn_ready, x_turned, xT_ready = (m.sem(x) for x in ("loaded", "xn_ready", "x_turned", "xT_ready"))
        hid_full, h1_ready, lg_full, r1_ready, r2_ready = (m.sem(x) for x in ("hid_full", "h1_ready", "lg_full", "r1_ready", "r2_ready"))
        r_out = [m.sem(f"r_out{k}") for k in range(2)]
        block = ctx.enter_context(nc.Block())
        LOADED = 16 * 5

        @block.sync
        def _(sp):
            for dst, name in ((w1[:, :, :], "r_w1"), (w2[:, :], "r_w2"), (b1[:, :], "r_b1"), (b2[:, :], "r_b2"), (ident[:, :], "ident")):
                sp.dma_start(dst, A[name]).then_inc(loaded, 16)
            for k in range(2):
                sp.sem_inc(r_out[k], 16)
            rv = S["route"].rearrange("(b h) t -> b h t", h=NH)
            with sp.Fori(0, B // 2) as j:
                for k in range(2):
                    sp.wait_ge(r2_ready, j * 2 + k + 1)
                    sp.dma_start(rv[bass.ds(j * 2 + k, 1)].squeeze(0), r2[:, k, :]).then_inc(r_out[k], 16)
            for k in range(2):
                sp.wait_ge(r_out[k], 16 * (B // 2 + 1))

        @block.gpsimd
        def _(pool):
            pool.wait_ge(norm.set, 2)
            with pool.Fori(0, B) as g:
                norm.power(nc, pool, g)

        @block.vector
        def _(dve):
            norm.constants(nc)
            dve.sem_inc(x_turned, 2)
            with dve.Fori(0, B) as g:
                norm.stats(nc, dve, H, g)
                dve.wait_ge(x_turned, g * 2 + 2)
                norm.apply(nc, dve, H, g, lambda t: xn[:, t, :], xn_ready)

        @block.scalar
        def _(act):
            for s, n in ((xT_ready, 2), (h1_ready, 2), (r1_ready, 2)):
                act.sem_inc(s, n)
            act.wait_ge(loaded, LOADED)
            with act.Fori(0, B // 2) as j:
                for k in range(2):
                    b = j * 2 + k
                    for c in range(2):
                        act.wait_ge(x_turned, b * 2 + c + 3)
                        nc.scalar.activation(xT[:, k, c, :], turn[c][:, :], ACT.Copy).then_inc(xT_ready, 1)
                    act.wait_ge(hid_full, b + 1)
                    nc.scalar.activation(h1[:, k, :], hid[k][0:HID, :], ACT.Relu, bias=b1[:, 0:1]).then_inc(h1_ready, 1)
                    act.wait_ge(lg_full, b + 1)
                    nc.scalar.activation(r1[:, k, :], lg[k][0:NH, :], ACT.Sigmoid, bias=b2[:, 0:1]).then_inc(r1_ready, 1)
                    act.wait_ge(r1_ready, b + 3)
                    act.wait_ge(r_out[k], j * 16 + 16)
                    nc.scalar.activation(r2[:, k, :], r1[:, k, :], ACT.Sigmoid).then_inc(r2_ready, 1)

        @block.tensor
        def _(pe):
            pe.wait_ge(loaded, LOADED)
            with pe.Fori(0, B // 2) as j:
                for k in range(2):
                    b = j * 2 + k
                    pe.wait_ge(xn_ready, b * TPB + TPB)
                    for c in range(2):
                        pe.wait_ge(xT_ready, b * 2 + c + 1)
                        for t in range(TPB):
                            mm = nc.tensor.transpose(turn[c][:, t * P:(t + 1) * P], xn[:, t, c * P:(c + 1) * P], ident[:, :])
                        mm.then_inc(x_turned, 1)
                    pe.wait_ge(xT_ready, b * 2 + 4)
                    pe.wait_ge(h1_ready, b + 1)
                    for c in range(2):
                        mm = nc.tensor.matmul(hid[k][0:HID, :], w1[:, c, :], xT[:, k, c, :], start=c == 0, stop=c == 1)
                    mm.then_inc(hid_full, 1)
                    pe.wait_ge(h1_ready, b + 3)
                    pe.wait_ge(r1_ready, b + 1)
                    nc.tensor.matmul(lg[k][:, :], w2[:, :], h1[:, k, :], start=True, stop=True).then_inc(lg_full, 1)


def keep_largest(nc, S):
    ROUNDS = -(-KEEP // 8)
    SPARE = ROUNDS * 8 - KEEP
    TAKEN = -1.0
    with ExitStack() as ctx:
        m = Bufs(nc, ctx, "kl")
        v, mx, out = m.sb("v", [P, 2, 2, T]), m.sb("mx", [P, 2, 8]), m.sb("out", [P, 2, T])
        loaded, stored, made = m.sem("loaded"), m.sem("stored"), m.sem("made")
        found, taken = m.sem("found"), m.sem("taken")
        block = ctx.enter_context(nc.Block())

        @block.sync
        def _(sp):
            for g in range(2):
                sp.dma_start(v[:, g, 0, :], S["route"][g * P:(g + 1) * P, :]).then_inc(loaded, 16)
            for g in range(2):
                sp.wait_ge(made, g + 3)
                sp.dma_start(S["mask"][g * P:(g + 1) * P, :], out[:, g, :]).then_inc(stored, 16)
            sp.wait_ge(stored, 32)

        @block.vector
        def _(dve):
            dve.wait_ge(loaded, 32)
            n = 0
            for r in range(ROUNDS):
                for g in range(2):
                    if r:
                        dve.wait_ge(taken, 2 * r + g - 1)
                    nc.vector.max(mx[:, g, :], v[:, g, r % 2, :]).then_inc(found, 1)
                    n += 1
                for g in range(2):
                    dve.wait_ge(found, 2 * r + g + 1)
                    if r == ROUNDS - 1:
                        nc.vector.memset(mx[:, g, 8 - SPARE:8], TAKEN).then_inc(made, 1)
                for g in range(2):
                    if r == ROUNDS - 1:
                        dve.wait_ge(made, g + 1)
                    nc.vector.match_replace(v[:, g, 1 - r % 2, :], mx[:, g, :], v[:, g, r % 2, :], TAKEN).then_inc(taken, 1)
            dve.wait_ge(taken, 2 * ROUNDS)
            for g in range(2):
                nc.vector.tensor_scalar(v[:, g, 1 - ROUNDS % 2, :], v[:, g, ROUNDS % 2, :], TAKEN, 1.0, ALU.is_equal, ALU.subtract
                                        ).then_inc(taken, 1)
            for g in range(2):
                dve.wait_ge(taken, 2 * ROUNDS + g + 1)
                nc.vector.tensor_scalar(out[:, g, :], v[:, g, 1 - ROUNDS % 2, :], -DROP, None, ALU.mult).then_inc(made, 1)


def masked_attention(nc, A, S, H):
    HD, UNITS, EVENTS = 16, 32, 12
    AT = {3 + 2 * e: e for e in range(EVENTS)}
    with ExitStack() as ctx:
        m = Bufs(nc, ctx, "ma")
        wq, wk, wv, ident = m.sb("wq", [P, 2, T]), m.sb("wk", [P, 2, T]), m.sb("wv", [P, 2, D]), m.sb("ident", [P, P])
        bq, bq4, bk, bv = m.sb("bq", [P, 4]), m.sb("bq4", [P, 4]), m.sb("bk", [P, 4]), m.sb("bv", [P, D])
        xn, xT = m.sb("xn", [P, TPB, D]), m.sb("xT", [P, 2, T])
        qT, kT, v = m.sb("qT", [P, 2, 4, T]), m.sb("kT", [P, 2, 4, T]), m.sb("v", [P, 2, TPB, D])
        nmax, prob, probT = m.sb("nmax", [P, 2, 2]), m.sb("prob", [P, 2, 2, T]), m.sb("probT", [P, 2, T])
        den, rden, part = m.sb("den", [P, 2, NH]), m.sb("rden", [P, NH]), m.sb("part", [P, D])
        norm = Norm(m)
        score = [m.ps(f"score{i}", [P, 2, T]) for i in range(2)]
        turned = [m.ps(f"turned{i}", [P, T]) for i in range(2)]
        att, work = m.ps("att", [P, T]), m.ps("work", [P, T])
        loaded, bias_ready, xn_ready = m.sem("loaded"), m.sem("bias_ready"), m.sem("xn_ready")
        work_full, work_copied = m.sem("work_full"), m.sem("work_copied")
        mask_in = [m.sem(f"mask_in{k}") for k in range(2)]
        score_full, max_ready, exp_done = m.sem("score_full"), m.sem("max_ready"), m.sem("exp_done")
        p_turned, pT_ready, av_done = m.sem("p_turned"), [m.sem(f"pT_ready{k}") for k in range(2)], m.sem("av_done")
        att_read, rden_ready, part_ready, h_done = m.sem("att_read"), m.sem("rden_ready"), m.sem("part_ready"), m.sem("h_done")
        block = ctx.enter_context(nc.Block())
        LOADED = 16 * 7

        def run(eng, start, first, unit, event, norm_at=lambda b, u: None, end=lambda b: None):
            start(eng)
            for e in range(EVENTS):
                event(0, 0, e)

            def pair(b0, more):
                first(b0, 0)
                for half in range(2):
                    b = b0 + half
                    for u in range(UNITS):
                        if half == 0 or more:
                            norm_at(b + 1, u)
                        unit(b, half, u, half == 1 and u == UNITS - 1)
                        if u in AT and (half == 0 or more):
                            event(b + 1, 1 - half, AT[u])
                end(b0 + 1)

            with eng.Fori(0, B // 2 - 1) as j:
                pair(j * 2, True)
            pair(B - 2, False)

        @block.sync
        def _(sp):
            for dst, name in ((wq, "l1_wq"), (wk, "l1_wk"), (wv, "l1_wv")):
                sp.dma_start(dst[:, :, :], A[name]).then_inc(loaded, 16)
            for dst, name in ((ident, "ident"), (bq, "l1_bq"), (bk, "l1_bk")):
                sp.dma_start(dst[:, :], A[name]).then_inc(loaded, 16)
            sp.dma_start(bv[:, :], A["l1_bv"].to_broadcast([P, D])).then_inc(loaded, 16)
            mv = S["mask"].rearrange("(b a s) t -> b s a t", b=B, s=4)
            with sp.Fori(0, B // 2) as j:
                for k in range(2):
                    sp.wait_ge(work_copied, (j * 2 + k) * EVENTS + 11)
                    for s in range(4):
                        r = 32 * s + HD
                        sp.dma_start(kT[r:r + 1, k, :, :], mv[bass.ds(j * 2 + k, 1), s:s + 1].squeeze(0)).then_inc(mask_in[k], 16)
            for k in range(2):
                sp.wait_ge(mask_in[k], 64 * (B // 2))

        @block.gpsimd
        def _(pool):
            pool.wait_ge(norm.set, 2)
            with pool.Fori(0, B) as g:
                norm.power(nc, pool, g)

        @block.tensor
        def _(pe):
            def scores(b, k, u):
                qc, p = u // 8, u % 8
                pe.wait_ge(exp_done, b * UNITS + u + 1)
                for i in range(2):
                    r = slice(32 * (2 * (p % 2) + i), 32 * (2 * (p % 2) + i) + 32)
                    mm = nc.tensor.matmul(score[u % 2][:, i, :], qT[r, k, p // 2, qc * P:(qc + 1) * P], kT[r, k, p // 2, :],
                                          start=True, stop=True)
                mm.then_inc(score_full, 1)

            def turn_probs(b, u):
                pe.wait_ge(exp_done, b * UNITS + u + 3)
                for i in range(2):
                    pe.wait_ge(pT_ready[i], b * UNITS + u + 1)
                    for kc in range(TPB):
                        mm = nc.tensor.transpose(turned[i][:, kc * P:(kc + 1) * P], prob[:, u % 2, i, kc * P:(kc + 1) * P], ident[:, :])
                    mm.then_inc(p_turned, 1)

            def values(b, k, u):
                qc, p = u // 8, u % 8
                if p == 0:
                    pe.wait_ge(att_read, b * TPB + qc + 1)
                for i in range(2):
                    pe.wait_ge(pT_ready[i], b * UNITS + u + 2)
                    h = 2 * p + i
                    for kc in range(TPB):
                        mm = nc.tensor.matmul(att[:, h * HD:(h + 1) * HD], probT[:, i, kc * P:(kc + 1) * P],
                                              v[:, k, kc, h * HD:(h + 1) * HD], start=kc == 0, stop=kc == TPB - 1)
                    mm.then_inc(av_done, 1)

            def event(b, k, e):
                if e == 0:
                    pe.wait_ge(xn_ready, b * TPB + TPB)
                pe.wait_ge(work_copied, b * EVENTS + e + 1)
                if e < 2:
                    for t in range(TPB):
                        mm = nc.tensor.transpose(work[:, t * P:(t + 1) * P], xn[:, t, e * P:(e + 1) * P], ident[:, :])
                elif e < 10:
                    w, a = (wq, e - 2) if e < 6 else (wk, e - 6)
                    for c in range(2):
                        mm = nc.tensor.matmul(work[:, :], w[:, c, a * P:(a + 1) * P], xT[:, c, :], start=c == 0, stop=c == 1)
                else:
                    for i in range(2):
                        t = 2 * (e - 10) + i
                        for c in range(2):
                            mm = nc.tensor.matmul(work[:, i * D:(i + 1) * D], xT[:, c, t * P:(t + 1) * P], wv[:, c, :],
                                                  start=c == 0, stop=c == 1)
                mm.then_inc(work_full, 1)

            def start(pe):
                pe.sem_inc(p_turned, 4)
                pe.sem_inc(av_done, 2)
                pe.wait_ge(loaded, LOADED)

            def ready(b, k):
                pe.wait_ge(work_copied, b * EVENTS + EVENTS + 1)
                pe.wait_ge(mask_in[k], (b - k) * 32 + 64)

            def first(b, k):
                ready(b, k)
                scores(b, k, 0)

            def unit(b, k, u, last):
                if not last:
                    if u + 1 < UNITS:
                        scores(b, k, u + 1)
                    else:
                        ready(b + 1, 1)
                        scores(b + 1, 1, 0)
                turn_probs(b, u)
                if u:
                    values(b, k, u - 1)
                elif k:
                    values(b - 1, 0, UNITS - 1)
                if last:
                    values(b, k, u)

            run(pe, start, first, unit, event)

        @block.vector
        def _(dve):
            def start(dve):
                norm.constants(nc)
                dve.sem_inc(pT_ready[0], 1)
                dve.sem_inc(att_read, 1)
                dve.wait_ge(loaded, LOADED)
                nc.vector.tensor_scalar(bq4[:, :], bq[:, :], HD ** -0.5, None, ALU.mult).then_inc(bias_ready, 1)
                norm.stats(nc, dve, H, 0)
                norm.apply(nc, dve, H, 0, lambda t: xn[:, t, :], xn_ready)

            def norm_at(b, u):
                if u == 0:
                    norm.stats(nc, dve, H, b)
                if u == 1:
                    norm.apply(nc, dve, H, b, lambda t: xn[:, t, :], xn_ready)

            def maxima(b, u):
                dve.wait_ge(score_full, b * UNITS + u + 1)
                dve.wait_ge(exp_done, b * UNITS + u + 1)
                nc.vector.tensor_reduce(nmax[:, u % 2, :], score[u % 2][:, :, :], AX.X, ALU.max, negate=True).then_inc(max_ready, 1)

            def finish(b, qc):
                dve.wait_ge(av_done, (b * TPB + qc) * NH + NH + 2)
                nc.vector.reciprocal(rden[:, :], den[:, qc % 2, :]).then_inc(rden_ready, 1)
                dve.wait_ge(rden_ready, b * TPB + qc + 1)
                nc.vector.tensor_tensor(part[:, :].rearrange("p (h d) -> p h d", d=HD), att[:, 0:D].rearrange("p (h d) -> p h d", d=HD),
                                        rden[:, :].unsqueeze(2).to_broadcast([P, NH, HD]), ALU.mult).then_inc(att_read, 1)
                dve.wait_ge(att_read, b * TPB + qc + 2)
                hh = H[:, bass.ds(b * TPB + qc, 1), :].squeeze(1)
                nc.vector.tensor_tensor(hh, hh, part[:, :], ALU.add)

            def unit(b, k, u, last):
                if not last:
                    if u + 1 < UNITS:
                        maxima(b, u + 1)
                    else:
                        maxima(b + 1, 0)
                dve.wait_ge(p_turned, (b * UNITS + u) * 2 + 5)
                dve.wait_ge(av_done, (b * UNITS + u) * 2 + 1)
                nc.vector.tensor_copy(probT[:, 0, :], turned[0][:, :]).then_inc(pT_ready[0], 1)
                if u and u % 8 == 0:
                    finish(b, u // 8 - 1)
                elif u == 0 and k:
                    finish(b - 1, TPB - 1)

            def event(b, k, e):
                if e >= 6:
                    dve.wait_ge(work_full, b * EVENTS + e + 1)
                if 6 <= e < 10:
                    nc.vector.tensor_scalar(kT[:, k, e - 6, :], work[:, :], bk[:, e - 6:e - 5], None, ALU.add).then_inc(work_copied, 1)
                if e >= 10:
                    t = 2 * (e - 10)
                    nc.vector.tensor_tensor(v[:, k, t:t + 2, :], work[:, :].rearrange("p (t d) -> p t d", t=2),
                                            bv[:, :].unsqueeze(1).to_broadcast([P, 2, D]), ALU.add).then_inc(work_copied, 1)

            run(dve, start, lambda b, k: maxima(b, 0), unit, event, norm_at, lambda b: finish(b, TPB - 1))

        @block.scalar
        def _(act):
            def start(act):
                act.sem_inc(work_copied, 1)
                act.sem_inc(exp_done, 2)
                act.sem_inc(pT_ready[1], 1)
                act.wait_ge(bias_ready, 1)

            def exps(b, u):
                qc, p = u // 8, u % 8
                act.wait_ge(max_ready, b * UNITS + u + 1)
                act.wait_ge(p_turned, (b * UNITS + u) * 2 + 1)
                for i in range(2):
                    h = 2 * p + i
                    last = nc.scalar.activation(prob[:, u % 2, i, :], score[u % 2][:, i, :], ACT.Exp, bias=nmax[:, u % 2, i:i + 1],
                                                accum_out=den[:, qc % 2, h:h + 1])
                last.then_inc(exp_done, 1)

            def unit(b, k, u, last):
                act.wait_ge(p_turned, (b * UNITS + u) * 2 + 6)
                act.wait_ge(av_done, (b * UNITS + u) * 2 + 2)
                nc.scalar.activation(probT[:, 1, :], turned[1][:, :], ACT.Copy).then_inc(pT_ready[1], 1)
                if not last:
                    if u + 1 < UNITS:
                        exps(b, u + 1)
                    else:
                        exps(b + 1, 0)

            def event(b, k, e):
                if e >= 6:
                    return
                act.wait_ge(work_full, b * EVENTS + e + 1)
                if e < 2:
                    nc.scalar.activation(xT[:, e, :], work[:, :], ACT.Copy).then_inc(work_copied, 1)
                else:
                    nc.scalar.activation(qT[:, k, e - 2, :], work[:, :], ACT.Identity, bias=bq4[:, e - 2:e - 1], scale=HD ** -0.5
                                         ).then_inc(work_copied, 1)

            run(act, start, lambda b, k: exps(b, 0), unit, event)


E2, I2, CAP = 16, 128, 64
SLOT_ROWS = E2 * B * CAP


def top2_experts(nc, A, S, H, out):
    with ExitStack() as outer:
        m = Bufs(nc, outer, "t2")
        read_slot = m.sb("read_slot", [P, 2, TILES], I32)
        weight = m.sb("weight", [P, 2, TILES])
        with ExitStack() as both:
            m = Bufs(nc, both, "t2n")
            xs, lgs = m.sb("xs", [P, TILES, D]), m.sb("lgs", [P, TILES, E2])
            router_logits(nc, A, S, H, xs, lgs)
            dispatch(nc, A, S, xs, lgs, read_slot, weight)
        slot_experts(nc, A, S)
        collect(nc, S, H, read_slot, weight, out)


def router_logits(nc, A, S, H, xs, lgs):
    with ExitStack() as ctx:
        m = Bufs(nc, ctx, "rl")
        wr, ident, zeros = m.sb("wr", [P, 2, E2]), m.sb("ident", [P, P]), m.sb("zeros", [P, 2048])
        xn, xT = m.sb("xn", [P, TPB, D]), m.sb("xT", [P, 2, 2, T])
        norm = Norm(m)
        turn, lg = [m.ps(f"turn{c}", [P, T]) for c in range(2)], [m.ps(f"lg{k}", [P, T]) for k in range(2)]
        loaded, zero_set, zeroed = m.sem("loaded"), m.sem("zero_set"), m.sem("zeroed")
        xn_ready, xs_ready, x_turned, xT_ready, lg_full, lg_read = (m.sem(x) for x in (
            "xn_ready", "xs_ready", "x_turned", "xT_ready", "lg_full", "lg_read"))
        block = ctx.enter_context(nc.Block())

        @block.sync
        def _(sp):
            sp.dma_start(wr[:, :, :], A["w_router"]).then_inc(loaded, 16)
            sp.dma_start(ident[:, :], A["ident"]).then_inc(loaded, 16)
            sp.wait_ge(zero_set, 1)
            zero_rows(sp, S["slots_x"], SLOT_ROWS, zeros, zeroed)

        @block.gpsimd
        def _(pool):
            pool.wait_ge(norm.set, 2)
            with pool.Fori(0, B) as g:
                norm.power(nc, pool, g)
                for t in range(TPB):
                    pool.wait_ge(xn_ready, g * TPB + t + 1)
                    nc.gpsimd.tensor_copy(xs[:, bass.ds(g * TPB + t, 1), :].squeeze(1), xn[:, t, :]).then_inc(xs_ready, 1)

        @block.vector
        def _(dve):
            norm.constants(nc)
            nc.vector.memset(zeros[:, :], 0.0).then_inc(zero_set, 1)
            dve.sem_inc(x_turned, 2)
            dve.sem_inc(xs_ready, 1)
            with dve.Fori(0, B) as g:
                norm.stats(nc, dve, H, g)
                dve.wait_ge(x_turned, g * 2 + 2)
                dve.wait_ge(xs_ready, g * TPB + 1)
                norm.apply(nc, dve, H, g, lambda t: xn[:, t, :], xn_ready)

        @block.scalar
        def _(act):
            act.sem_inc(xT_ready, 2)
            act.sem_inc(lg_read, 2)
            with act.Fori(0, B // 2) as j:
                for k in range(2):
                    b = j * 2 + k
                    for c in range(2):
                        act.wait_ge(x_turned, b * 2 + c + 3)
                        nc.scalar.activation(xT[:, k, c, :], turn[c][:, :], ACT.Copy).then_inc(xT_ready, 1)
                    act.wait_ge(lg_full, b + 1)
                    nc.scalar.activation(lgs[:, bass.ds(b * TPB, TPB), :], lg[k][:, 0:TPB * E2].rearrange("p (t e) -> p t e", e=E2),
                                         ACT.Copy).then_inc(lg_read, 1)

        @block.tensor
        def _(pe):
            pe.wait_ge(loaded, 32)
            with pe.Fori(0, B // 2) as j:
                for k in range(2):
                    b = j * 2 + k
                    pe.wait_ge(xn_ready, b * TPB + TPB)
                    for c in range(2):
                        pe.wait_ge(xT_ready, b * 2 + c + 1)
                        for t in range(TPB):
                            mm = nc.tensor.transpose(turn[c][:, t * P:(t + 1) * P], xn[:, t, c * P:(c + 1) * P], ident[:, :])
                        mm.then_inc(x_turned, 1)
                    pe.wait_ge(xT_ready, b * 2 + 4)
                    pe.wait_ge(lg_read, b + 1)
                    for t in range(TPB):
                        for c in range(2):
                            mm = nc.tensor.matmul(lg[k][:, t * E2:(t + 1) * E2], xT[:, k, c, t * P:(t + 1) * P], wr[:, c, :],
                                                  start=c == 0, stop=c == 1)
                    mm.then_inc(lg_full, 1)


def dispatch(nc, A, S, xs, lgs, read_slot, weight):
    FAR = float(2 * SLOT_ROWS)
    with ExitStack() as ctx:
        m = Bufs(nc, ctx, "dp")
        iota, base = m.sb("iota", [P, P]), m.sb("base", [P, TILES])
        strict_f, strict, ones = m.sb("strict_f", [P, P]), m.sb("strict", [P, P], BF16), m.sb("ones", [P, P], BF16)
        big, probs = m.sb("big", [P, TILES]), m.sb("probs", [P, TILES, E2])
        top, top_i = m.sb("top", [P, TILES, 8]), m.sb("top_i", [P, TILES, 8], U32)
        idx, hot = m.sb("idx", [P, 2, TILES]), m.sb("hot", [P, 2, TILES, E2], BF16)
        tot, run, flag = (m.sb(x, [P, B, E2, 2 * TPB]) for x in ("tot", "run", "flag"))
        place, pos, over = m.sb("place", [P, TILES, E2]), m.sb("pos", [P, 2, TILES]), m.sb("over", [P, 2, TILES])
        row, write_slot = m.sb("row", [P, 2, TILES]), m.sb("write_slot", [P, 2, TILES], I32)
        pre = [m.ps(f"pre{g}", [P, 512]) for g in range(4)]
        sums = [m.ps(f"sums{g}", [P, 512]) for g in range(4)]
        loaded, step, counted, exp_done, slots_ready, scattered = (m.sem(x) for x in (
            "loaded", "step", "counted", "exp_done", "slots_ready", "scattered"))
        block = ctx.enter_context(nc.Block())
        bc = lambda x: x.unsqueeze(2).to_broadcast([P, TILES, E2])
        HOT_STEP = 2 + 2 * TILES + 5 + 3

        @block.sync
        def _(sp):
            for dst, name in ((iota, "iota128"), (base, "batch_row"), (strict_f, "strict")):
                sp.dma_start(dst[:, :], A[name]).then_inc(loaded, 16)

        @block.scalar
        def _(act):
            act.wait_ge(step, 2)
            nc.scalar.activation(probs[:, :, :], probs[:, :, :], ACT.Exp).then_inc(exp_done, 1)

        @block.tensor
        def _(pe):
            pe.wait_ge(step, HOT_STEP)
            for c in range(2):
                for g in range(2):
                    r = hot[:, c, g * 32:(g + 1) * 32, :].rearrange("p t e -> p (t e)")
                    nc.tensor.matmul(pre[2 * c + g][:, :], strict[:, :], r, start=True, stop=True).then_inc(counted, 1)
                    nc.tensor.matmul(sums[2 * c + g][:, :], ones[:, :], r, start=True, stop=True).then_inc(counted, 1)

        @block.vector
        def _(dve):
            n = [0]

            def link(ins, wait=True):
                n[0] += 1
                ins.then_inc(step, 1)
                if wait:
                    dve.wait_ge(step, n[0])

            link(nc.vector.tensor_reduce(big[:, :], lgs[:, :, :], AX.X, ALU.max))
            link(nc.vector.tensor_tensor(probs[:, :, :], lgs[:, :, :], bc(big[:, :]), ALU.subtract))
            dve.wait_ge(exp_done, 1)
            link(nc.vector.tensor_reduce(big[:, :], probs[:, :, :], AX.X, ALU.add))
            link(nc.vector.reciprocal(big[:, :], big[:, :]))
            link(nc.vector.tensor_tensor(probs[:, :, :], probs[:, :, :], bc(big[:, :]), ALU.mult))
            for t in range(TILES):
                link(nc.vector.max(top[:, t, :], probs[:, t, :]), wait=t == TILES - 1)
            for t in range(TILES):
                link(nc.vector.max_index(top_i[:, t, :], top[:, t, :], probs[:, t, :]), wait=t == TILES - 1)
            dve.wait_ge(loaded, 48)
            link(nc.vector.tensor_copy(strict[:, :], strict_f[:, :]))
            link(nc.vector.memset(ones[:, :], 1.0))
            link(nc.vector.tensor_copy(idx[:, :, :], top_i[:, :, 0:2].rearrange("p t c -> p c t")))
            for c in range(2):
                link(nc.vector.tensor_tensor(hot[:, c, :, :], iota[:, 0:E2].unsqueeze(1).to_broadcast([P, TILES, E2]),
                                             bc(idx[:, c, :]), ALU.is_equal))
            assert n[0] == HOT_STEP
            link(nc.vector.tensor_copy(weight[:, :, :], top[:, :, 0:2].rearrange("p t c -> p c t")))
            link(nc.vector.memset(flag[:, :, :, :], 1.0))
            link(nc.vector.memset(flag[:, :, :, 0:1], 0.0))
            dve.wait_ge(counted, 8)
            for c in range(2):
                for g in range(2):
                    link(nc.vector.tensor_copy(tot[:, 8 * g:8 * g + 8, :, c * TPB:(c + 1) * TPB],
                                               sums[2 * c + g][:, :].rearrange("p (b q e) -> p b e q", q=TPB, e=E2)))
            flat = lambda x: x[:, :, :, :].rearrange("p b e q -> p (b e q)")
            link(nc.vector.tensor_tensor_scan(flat(run), flat(flag), flat(tot), 0.0, ALU.mult, ALU.add))
            link(nc.vector.tensor_tensor(flat(run), flat(run), flat(tot), ALU.subtract))
            for c in range(2):
                for g in range(2):
                    link(nc.vector.tensor_tensor(place[:, 32 * g:32 * g + 32, :].rearrange("p (b q) e -> p b q e", q=TPB),
                                                 pre[2 * c + g][:, :].rearrange("p (b q e) -> p b q e", q=TPB, e=E2),
                                                 run[:, 8 * g:8 * g + 8, :, c * TPB:(c + 1) * TPB].rearrange("p b e q -> p b q e"), ALU.add))
                link(nc.vector.tensor_tensor(place[:, :, :], place[:, :, :], hot[:, c, :, :], ALU.mult))
                link(nc.vector.tensor_reduce(pos[:, c, :], place[:, :, :], AX.X, ALU.add))
                link(nc.vector.tensor_scalar(row[:, c, :], idx[:, c, :], float(B * CAP), None, ALU.mult))
                link(nc.vector.tensor_tensor(row[:, c, :], row[:, c, :], base[:, :], ALU.add))
            link(nc.vector.tensor_scalar(over[:, :, :], pos[:, :, :], float(CAP), FAR, ALU.is_ge, ALU.mult))
            link(nc.vector.tensor_scalar(pos[:, :, :], pos[:, :, :], float(CAP - 1), None, ALU.min))
            link(nc.vector.tensor_tensor(row[:, :, :], row[:, :, :], pos[:, :, :], ALU.add))
            link(nc.vector.tensor_copy(read_slot[:, :, :], row[:, :, :]))
            link(nc.vector.tensor_tensor(row[:, :, :], row[:, :, :], over[:, :, :], ALU.add))
            nc.vector.tensor_copy(write_slot[:, :, :], row[:, :, :]).then_inc(slots_ready, 1)

        @block.gpsimd
        def _(pool):
            pool.wait_ge(slots_ready, 1)
            for t in range(TILES):
                for c in range(2):
                    nc.gpsimd.indirect_dma_start(S["slots_x"], bass.IndirectOffsetOnAxis(ap=write_slot[:, c, t:t + 1], axis=0),
                                                 xs[:, t, :], None, bounds_check=SLOT_ROWS - 1, oob_is_err=False).then_inc(scattered, 16)
            pool.wait_ge(scattered, 32 * TILES)


def slot_experts(nc, A, S):
    N = SLOT_ROWS // P
    with ExitStack() as ctx:
        m = Bufs(nc, ctx, "se")
        wgu, wd = m.sb("wgu", [P, E2, 2, 2 * I2]), m.sb("wd", [P, E2, D])
        ident, xt, o = m.sb("ident", [P, P]), m.sb("xt", [P, 4, D]), m.sb("o", [P, 4, D])
        loaded = m.sem("loaded")
        x_in, o_out = [m.sem(f"x_in{k}") for k in range(4)], [m.sem(f"o_out{k}") for k in range(4)]
        xv = S["slots_x"].rearrange("(n p) d -> n p d", p=P)
        yv = S["slots_y"].rearrange("(n p) d -> n p d", p=P)

        def turn_ready(pe, n, q, i):
            pe.wait_ge(loaded, 48)
            pe.wait_ge(x_in[q % 4], (i * 2 + q // 4) * 16 + 16)

        def finish(dve, n, k, q, i, left, s, pD):
            dve.wait_ge(s["down_full"], n + 2)
            dve.wait_ge(o_out[q % 4], (i * 2 + q // 4) * 16 + 16)
            nc.vector.tensor_copy(o[:, q % 4, :], pD[k][:, 0:D]).then_inc(s["down_read"], 1)

        def sync_prog(sp, s, steps):
            sp.dma_start(ident[:, :], A["ident"]).then_inc(loaded, 16)
            for k in range(4):
                sp.dma_start(xt[:, k, :], xv[k]).then_inc(x_in[k], 16)
                sp.sem_inc(o_out[k], 16)
            sp.dma_start(wgu[:, :, :, :], A["ex_gu"]).then_inc(loaded, 16)
            sp.dma_start(wd[:, :, :], A["ex_down"]).then_inc(loaded, 16)

            def step(n, k, q, i, left):
                if left >= 4:
                    sp.wait_ge(s["x_turned"], n + 5)
                    sp.dma_start(xt[:, q % 4, :], xv[bass.ds(n + 4, 1)].squeeze(0)).then_inc(x_in[q % 4], 16)
                sp.wait_ge(s["down_read"], n + 3)
                sp.dma_start(yv[bass.ds(n, 1)].squeeze(0), o[:, q % 4, :]).then_inc(o_out[q % 4], 16)

            steps(sp, step)
            for k in range(4):
                sp.wait_ge(o_out[k], 16 * (N // 4) + 16)

        def mul_ready(pe, n, i):
            w = lambda a: (lambda c: wgu[:, bass.ds(i, 1), c, a:a + I2].squeeze(1))
            return w(0), w(I2)

        none = lambda *a: None
        expert_stream(nc, m, N, I2, 8, turn_ready=turn_ready, x_of=lambda n, q, c: xt[:, q % 4, c * P:(c + 1) * P],
                      mul_ready=mul_ready, down_of=lambda pe, n, i: (lambda c: wd[:, bass.ds(i, 1), :].squeeze(1)),
                      mul_also=none, identT=ident, dve_more=none, act_first=none, act_more=none, pool_prog=None,
                      sync_prog=sync_prog, finish=finish, prologue_dve=none, dve_before=none)


def collect(nc, S, H, read_slot, weight, out):
    R = 4
    with ExitStack() as ctx:
        m = Bufs(nc, ctx, "co")
        g = m.sb("g", [P, R, 2, D])
        got, summed, stored = [m.sem(f"got{r}") for r in range(R)], m.sem("summed"), m.sem("stored")
        block = ctx.enter_context(nc.Block())
        ov = out.rearrange("b (q p) d -> (b q) p d", p=P)

        @block.gpsimd
        def _(pool):
            for t in range(TILES):
                if t >= R:
                    pool.wait_ge(summed, 2 * (t - R + 1))
                for c in range(2):
                    nc.gpsimd.indirect_dma_start(g[:, t % R, c, :], None, S["slots_y"],
                                                 bass.IndirectOffsetOnAxis(ap=read_slot[:, c, t:t + 1], axis=0)).then_inc(got[t % R], 16)

        @block.vector
        def _(dve):
            for t in range(TILES):
                dve.wait_ge(got[t % R], 32 * (t // R + 1))
                for c in range(2):
                    if c:
                        dve.wait_ge(summed, 2 * t + 1)
                    nc.vector.scalar_tensor_tensor(out=H[:, t, :], in0=g[:, t % R, c, :], scalar=weight[:, c, t:t + 1],
                                                   in1=H[:, t, :], op0=ALU.mult, op1=ALU.add).then_inc(summed, 1)

        @block.sync
        def _(sp):
            for t in range(TILES):
                sp.wait_ge(summed, 2 * t + 2)
                sp.dma_start(ov[t], H[:, t, :]).then_inc(stored, 16)
            sp.wait_ge(stored, 16 * TILES)


SCRATCH = [("frames", [B * FRAMES, D_STFT], F32), ("sorted_x", [SORT_TILES * P, D], F32), ("sorted_y", [SORT_TILES * P, D], F32),
           ("slots_x", [SLOT_ROWS, D], F32), ("slots_y", [SLOT_ROWS, D], F32),
           ("route", [B * NH, T], F32), ("mask", [B * NH, T], F32)]


def build(nc, A, out):
    S = {name: nc.dram_tensor(f"scratch_{name}", shape, dt).ap() for name, shape, dt in SCRATCH}
    with nc.sbuf_tensor("hidden", [P, TILES, D], F32) as H:
        embed_tokens(nc, A, S, H)
        diff_attention(nc, A, S, H)
        top1_experts(nc, A, S, H)
        sparse_attention(nc, A, S, H)
        top2_experts(nc, A, S, H, out)


def shape_constants():
    import numpy as np

    n = np.arange(NFFT)[:, None] * np.arange(FREQS)[None, :] * (2 * np.pi / NFFT)
    dft = np.concatenate([np.cos(n), -np.sin(n)], 1).astype(np.float32)
    coord = np.clip((np.arange(T) + np.float32(0.5)) * (FRAMES / T) - 0.5, 0, FRAMES - 1).astype(np.float32)
    i0 = np.floor(coord).astype(np.int32)
    i1 = np.minimum(i0 + 1, FRAMES - 1)
    w = coord - i0
    interp = np.zeros((FRAMES + 1, T), np.float32)
    interp[i0, np.arange(T)] += 1 - w
    interp[i1, np.arange(T)] += w
    interp[FRAMES] = 1
    hd = 16
    inv = 1.0 / 10000.0 ** (np.arange(0, hd, 2, dtype=np.float32) / np.float32(hd))
    fr = np.outer(np.arange(T, dtype=np.float32), inv.astype(np.float32)).astype(np.float32)
    c, s = np.cos(fr), np.sin(fr)
    rot = np.stack([np.concatenate([c, c], 1), np.concatenate([s, -s], 1)], 0).astype(np.float32)
    rot = rot.reshape(2, TPB, P, hd).transpose(2, 0, 1, 3)
    k = np.arange(P)
    return {
        "dft": dft, "interp": interp, "rot": rot,
        "iota_v": np.tile(np.arange(V, dtype=np.float32), (P, 1)),
        "iota128": np.tile(np.arange(P, dtype=np.float32), (P, 1)),
        "k128": np.tile(np.arange(P, dtype=np.float32) * P, (P, 1)),
        "batch_row": np.tile((np.arange(TILES) // TPB * CAP).astype(np.float32), (P, 1)),
        "part_id": k.astype(np.float32)[:, None],
        "ident": np.eye(P, dtype=np.float32),
        "upper": (k[:, None] <= k[None, :]).astype(np.float32),
        "strict": (k[:, None] < k[None, :]).astype(np.float32),
        "ones": np.ones((P, P), np.float32),
    }
def layout(inputs):
    import numpy as np

    x = {k: np.asarray(v) for k, v in inputs.items()}
    L = shape_constants()
    ids = x["x"].astype(np.int32, copy=False)
    half = NFFT // 2
    padded = np.pad(ids, ((0, 0), (half, half)), mode="reflect")
    L["ids"] = ids
    L["frame_ids"] = padded.reshape(B * FRAMES, NFFT).T
    L["window"] = x["L0_tok_window"][:, None]
    L["tok_proj_w"] = x["L0_tok_proj_w"].reshape(D_STFT, FREQS, V).transpose(2, 1, 0)
    L["proj_b"] = x["L0_tok_proj_b"][None, :]
    L["emb"] = x["L0_tok_emb_table"]
    order = np.concatenate([np.arange(8), 8 + (np.arange(8) + 4) % 8])
    heads = lambda w: w.reshape(16, 16, D)[order].reshape(D, D).T
    rows = lambda w: w.reshape(2, P, -1).transpose(1, 0, 2)
    L["wqk"] = rows(np.concatenate([heads(x["L0_attn_Wq"]), heads(x["L0_attn_Wk"])], 1))
    L["wv"], L["wo"] = rows(x["L0_attn_Wv"].T), rows(x["L0_attn_Wproj"].T)
    L["lambdas"] = np.stack([x["L0_attn_lambda_q1"], x["L0_attn_lambda_k1"], x["L0_attn_lambda_q2"],
                             x["L0_attn_lambda_k2"]]).reshape(2, 2, 8)
    L["gate_w"], L["sh_gate"] = rows(x["L0_ffn_gate_w"]), rows(x["L0_ffn_shared_gate_w"])
    L["sh_up"], L["sh_down"] = rows(x["L0_ffn_shared_up_w"]), x["L0_ffn_shared_down_w"].reshape(4, P, D).transpose(1, 0, 2)
    gu = np.concatenate([x["L0_ffn_routed_gate_w"], x["L0_ffn_routed_up_w"]], 2)
    L["ro_gu"] = gu.reshape(32, 2, P, 1024).transpose(0, 2, 1, 3)
    L["ro_down"] = x["L0_ffn_routed_down_w"].reshape(32, 4, P, D).transpose(0, 2, 1, 3)
    L["r_w1"], L["r_w2"] = rows(x["L1_attn_r_w1"].T), np.pad(x["L1_attn_r_w2"].T, ((0, 0), (0, P - 16)))
    L["r_b1"], L["r_b2"] = x["L1_attn_r_b1"][:, None], x["L1_attn_r_b2"][:, None]
    w, bias = x["L1_attn_qkv_w"], x["L1_attn_qkv_b"]

    def slots(w, extra):
        s = np.zeros((16, 32, w.shape[1]), w.dtype)
        s[:, :16] = w.reshape(16, 16, -1)
        s[:, 16] = extra
        return s.reshape(512, -1)

    L["l1_wq"], L["l1_wk"] = rows(slots(w[0:D], 0).T), rows(slots(w[D:2 * D], 0).T)
    L["l1_wv"], L["l1_bv"] = rows(w[2 * D:].T), bias[None, 2 * D:]
    L["l1_bq"] = slots(bias[0:D, None], 4).reshape(4, P).T
    L["l1_bk"] = slots(bias[D:2 * D, None], 0).reshape(4, P).T
    L["w_router"] = rows(x["L1_ffn_w_router"])
    gu = np.concatenate([x["L1_ffn_w_gate"], x["L1_ffn_w_fc"]], 2)
    L["ex_gu"] = gu.reshape(16, 2, P, 256).transpose(2, 0, 1, 3)
    L["ex_down"] = x["L1_ffn_w_proj"].transpose(1, 0, 2)
    return {k: np.ascontiguousarray(v) for k, v in L.items()}


def kernel(**inputs):
    import numpy as _np
    import concourse.bacc as _bacc
    from concourse import mybir as _mybir
    from concourse.bass_utils import run_bass_kernel_spmd as _run

    nc = _bacc.Bacc("TRN2", target_bir_lowering=False, num_devices=1)
    arrays, args = {}, {}
    for name, a in layout(inputs).items():
        arrays[f"in_{name}_dram"] = a
        args[name] = nc.dram_tensor(f"in_{name}_dram", a.shape, _mybir.dt.from_np(a.dtype), kind="ExternalInput").ap()
    out = nc.dram_tensor("out_0_dram", (B, T, D), _mybir.dt.float32, kind="ExternalOutput").ap()
    build(nc, args, out)
    r = _run(nc, [arrays], core_ids=[0])
    return r.results[0]["out_0_dram"]
```

```python
from contextlib import ExitStack

import numpy as np

import concourse.bass as bass
from concourse import mybir

ALU = mybir.AluOpType
ACT = mybir.ActivationFunctionType
AX = mybir.AxisListType
F32 = mybir.dt.float32
BF16 = mybir.dt.bfloat16
I32 = mybir.dt.int32
U32 = mybir.dt.uint32

P = 128
B, T, D = 16, 512, 256
V, D_EMB = 64, 179
D_STFT = D - D_EMB
FRAMES, FREQS, NFFT = 9, 33, 64
TILES = B * T // P
TPB = T // P
LN_EPS = 1e-5
RMS_EPS = float(np.finfo(np.float32).eps)
LAMBDA_INIT = 0.8 - 0.6 * float(np.exp(-0.3 * 1))


class Bufs:

    def __init__(self, nc, ctx, stage):
        self.nc, self.ctx, self.stage, self.sems = nc, ctx, stage, []
        ctx.callback(self.clear)

    def clear(self):
        if self.sems:
            self.nc.clear_and_free_semaphores(self.sems)
            self.nc.all_engine_barrier()

    def sb(self, name, shape, dt=F32):
        return self.ctx.enter_context(self.nc.sbuf_tensor(f"{self.stage}_{name}", shape, dt))

    def ps(self, name, shape, dt=F32):
        return self.ctx.enter_context(self.nc.psum_tensor(f"{self.stage}_{name}", shape, dt))

    def sem(self, name):
        self.sems.append(self.nc.alloc_semaphore(f"{self.stage}_{name}"))
        return self.sems[-1]


def embed_tokens(nc, A, S, H):
    NBT = B * FRAMES
    HALF = NBT // 2
    PER = 7
    GROUPS = -(-NBT // PER)
    C2 = 2 * FREQS
    with ExitStack() as ctx:
        m = Bufs(nc, ctx, "tok")
        frame_ids = m.sb("frame_ids", [NFFT, NBT], I32)
        frame_idf = m.sb("frame_idf", [NFFT, NBT])
        iota_v = m.sb("iota_v", [NFFT, V])
        part_id = m.sb("part_id", [V, 1])
        window = m.sb("window", [NFFT, 1])
        dft = m.sb("dft", [NFFT, C2])
        wdft = m.sb("wdft", [NFFT, C2])
        frames = m.sb("frames", [NFFT, NBT, V])
        squares = m.sb("squares", [V, 2, PER, C2])
        mag = m.sb("mag", [V, FREQS, NBT])
        proj_w = m.sb("proj_w", [V, FREQS, D_STFT])
        emb = m.sb("emb", [V, D_EMB])
        pf = m.sb("pf", [HALF, 2, D_STFT])
        pfb = m.sb("pfb", [FRAMES + 1, B, D_STFT])
        interp = m.sb("interp", [FRAMES + 1, T])
        ids_row = m.sb("ids_row", [V, 2, T], I32)
        onehot = m.sb("onehot", [V, 2, T])
        spec = m.ps("spec", [V, 2, 512])
        pproj = m.ps("pproj", [HALF, 2, 512])
        tok = m.ps("tok", [P, 4, 512])
        consts_in, weights_in, bias_in, interp_in = m.sem("consts_in"), m.sem("weights_in"), m.sem("bias_in"), m.sem("interp_in")
        idf_ready, wdft_ready, frames_ready = m.sem("idf_ready"), m.sem("wdft_ready"), m.sem("frames_ready")
        spec_ready, squares_ready, power_ready, mag_ready = m.sem("spec_ready"), m.sem("squares_ready"), m.sem("power_ready"), m.sem("mag_ready")
        proj_ready, pf_ready, pf_out, pf_back = m.sem("proj_ready"), m.sem("pf_ready"), m.sem("pf_out"), m.sem("pf_back")
        ids_in = [m.sem(f"ids_in{k}") for k in range(2)]
        onehot_ready, tok_ready, tok_copied = m.sem("onehot_ready"), m.sem("tok_ready"), m.sem("tok_copied")
        block = ctx.enter_context(nc.Block())
        PAIRS = B // 2

        @block.sync
        def _(sp):
            sp.dma_start(frame_ids[:, :], A["frame_ids"][:, :]).then_inc(consts_in, 16)
            sp.dma_start(iota_v[:, :], A["iota_v"][0:NFFT, :]).then_inc(consts_in, 16)
            sp.dma_start(window[:, :], A["window"][:, :]).then_inc(consts_in, 16)
            sp.dma_start(dft[:, :], A["dft"][:, :]).then_inc(consts_in, 16)
            sp.dma_start(part_id[:, :], A["part_id"][0:V, :]).then_inc(consts_in, 16)
            sp.dma_start(proj_w[:, :, :], A["tok_proj_w"][:, :, :]).then_inc(weights_in, 16)
            sp.dma_start(emb[:, :], A["emb"][:, :]).then_inc(weights_in, 16)
            sp.dma_start(interp[:, :], A["interp"][:, :]).then_inc(interp_in, 16)
            for b in range(B):
                sp.dma_start(pfb[FRAMES:FRAMES + 1, b, :], A["proj_b"][:, :]).then_inc(bias_in, 16)
            sp.wait_ge(pf_ready, 2)
            sp.dma_start(S["frames"].rearrange("(g p) j -> p g j", g=2), pf[:, :, :]).then_inc(pf_out, 16)
            sp.wait_ge(pf_out, 16)
            sp.dma_start(pfb[0:FRAMES, :, :], S["frames"].rearrange("(b t) j -> t b j", t=FRAMES)).then_inc(pf_back, 16)
            with sp.Fori(0, PAIRS) as j:
                for k in range(2):
                    sp.wait_ge(onehot_ready, j * 2 + k + 1)
                    sp.dma_start(ids_row[:, k, :], A["ids"][bass.ds(j * 2 + k, 1), :].to_broadcast([V, T])
                                 ).then_inc(ids_in[k], 16)

        @block.vector
        def _(dve):
            dve.wait_ge(consts_in, 80)
            nc.vector.tensor_copy(frame_idf[:, :], frame_ids[:, :]).then_inc(idf_ready, 1)
            nc.vector.tensor_scalar(wdft[:, :], dft[:, :], window[:, 0:1], None, ALU.mult).then_inc(wdft_ready, 1)
            dve.wait_ge(idf_ready, 1)
            nc.vector.tensor_tensor(frames[:, :, :],
                                    frame_idf[:, :].unsqueeze(2).to_broadcast([NFFT, NBT, V]),
                                    iota_v[:, :].unsqueeze(1).to_broadcast([NFFT, NBT, V]),
                                    ALU.is_equal).then_inc(frames_ready, 1)
            for g in range(GROUPS):
                n = min(PER, NBT - g * PER)
                dve.wait_ge(squares_ready, g + 1)
                sq = squares[:, g % 2, 0:n, :]
                nc.vector.tensor_tensor(mag[:, :, g * PER:g * PER + n], sq[:, :, 0:FREQS].rearrange("v n f -> v f n"),
                                        sq[:, :, FREQS:C2].rearrange("v n f -> v f n"), ALU.add).then_inc(power_ready, 1)
            for h in range(2):
                dve.wait_ge(proj_ready, h + 1)
                nc.vector.tensor_copy(pf[:, h, :], pproj[:, h, 0:D_STFT]).then_inc(pf_ready, 1)
            nc.vector.sem_inc(onehot_ready, 2)
            with dve.Fori(0, PAIRS) as j:
                for k in range(2):
                    dve.wait_ge(ids_in[k], j * 16 + 16)
                    dve.wait_ge(tok_ready, j * 8 + k * 4 + 4)
                    nc.vector.tensor_scalar(onehot[:, k, :], ids_row[:, k, :], part_id[:, 0:1], None, ALU.is_equal
                                            ).then_inc(onehot_ready, 1)

        @block.scalar
        def _(act):
            for g in range(GROUPS):
                n = min(PER, NBT - g * PER)
                act.wait_ge(spec_ready, g + 1)
                if g >= 2:
                    act.wait_ge(power_ready, g - 1)
                nc.scalar.activation(squares[:, g % 2, 0:n, :],
                                     spec[:, g % 2, 0:n * C2].rearrange("v (n f) -> v n f", n=n), ACT.Square
                                     ).then_inc(squares_ready, 1)
            act.wait_ge(power_ready, GROUPS)
            nc.scalar.activation(mag[:, :, :], mag[:, :, :], ACT.Sqrt).then_inc(mag_ready, 1)
            with act.Fori(0, PAIRS) as j:
                for k in range(2):
                    for q in range(TPB):
                        act.wait_ge(tok_ready, j * 8 + k * 4 + q + 9)
                        nc.scalar.activation(H[:, bass.ds(j * 8 + k * 4 + q, 1), :], tok[:, q, 0:D].unsqueeze(1), ACT.Copy
                                             ).then_inc(tok_copied, 1)

        @block.tensor
        def _(pe):
            pe.sem_inc(tok_ready, 8)
            pe.wait_ge(frames_ready, 1)
            pe.wait_ge(wdft_ready, 1)
            for g in range(GROUPS):
                n = min(PER, NBT - g * PER)
                if g >= 2:
                    pe.wait_ge(squares_ready, g - 1)
                for i in range(n):
                    mm = nc.tensor.matmul(spec[:, g % 2, i * C2:(i + 1) * C2], frames[:, g * PER + i, :], wdft[:, :],
                                          start=True, stop=True)
                mm.then_inc(spec_ready, 1)
            pe.wait_ge(mag_ready, 1)
            pe.wait_ge(weights_in, 32)
            for h in range(2):
                for f in range(FREQS):
                    mm = nc.tensor.matmul(pproj[:, h, 0:D_STFT], mag[:, f, h * HALF:(h + 1) * HALF], proj_w[:, f, :],
                                          start=f == 0, stop=f == FREQS - 1)
                mm.then_inc(proj_ready, 1)
            pe.wait_ge(bias_in, 16 * B)
            pe.wait_ge(interp_in, 16)
            pe.wait_ge(pf_back, 16)
            pe.sem_inc(tok_copied, 4)
            with pe.Fori(0, PAIRS) as j:
                for k in range(2):
                    pe.wait_ge(onehot_ready, j * 2 + k + 3)
                    for q in range(TPB):
                        pe.wait_ge(tok_copied, j * 8 + k * 4 + q + 1)
                        nc.tensor.matmul(tok[:, q, 0:D_EMB], onehot[:, k, q * P:(q + 1) * P], emb[:, :],
                                         start=True, stop=True)
                        nc.tensor.matmul(tok[:, q, D_EMB:D], interp[:, q * P:(q + 1) * P],
                                         pfb[:, bass.ds(j * 2 + k, 1), :].squeeze(1),
                                         start=True, stop=True).then_inc(tok_ready, 1)


def pe_transpose(nc, out, in_, ident):
    return nc.tensor.transpose(out, in_, ident)


def diff_attention(nc, A, S, H):
    NPAIR, HD, VD = 8, 16, 32
    VO = VD + 1
    LAST = B - 1
    with ExitStack() as ctx:
        m = Bufs(nc, ctx, "dif")
        wqk, wv, wo = m.sb("wqk", [P, 2, 2 * D]), m.sb("wv", [P, 2, D]), m.sb("wo", [P, 2, D])
        ident, upper, rot = m.sb("ident", [P, P]), m.sb("upper", [P, P]), m.sb("rot", [P, 2, TPB, HD])
        lam_in, lam_prod, lam = m.sb("lam_in", [P, 2, 2, 8]), m.sb("lam_prod", [P, 2, 8]), m.sb("lam", [P, 4])
        pause = m.sb("pause", [P, 1])
        bn, mv, rstd = m.sb("bn", [P, TPB, 6]), m.sb("mv", [P, TPB, 2]), m.sb("rstd", [P, TPB])
        var, half_neg = m.sb("var", [P, TPB]), m.sb("half_neg", [P, TPB * 32])
        eps, rms_eps = m.sb("eps", [P, TPB]), m.sb("rms_eps", [P, TPB * 32])
        xn, xT = m.sb("xn", [P, TPB, D]), m.sb("xT", [P, 2, T])
        qk, sq = m.sb("qk", [P, TPB, 2 * D]), m.sb("sq", [P, TPB, 2 * D])
        ss, rr = m.sb("ss", [P, TPB * 32]), m.sb("rr", [P, TPB * 32])
        rc = m.sb("rc", [P, TPB, 2 * D])
        q, kp = m.sb("q", [P, TPB, D]), m.sb("kp", [P, TPB, 2, 8, 32])
        qT, kT = m.sb("qT", [P, 2, T]), m.sb("kT", [P, 4, T])
        v1 = m.sb("v1", [P, TPB, NPAIR, VO])
        prob = m.sb("prob", [P, 2, 2, 2560])
        rsum, parts = m.sb("rsum", [P, 2 * TPB]), m.sb("parts", [P, 2 * TPB, VD])
        y, yT = m.sb("y", [P, TPB, D]), m.sb("yT", [P, 2, T])
        score = [m.ps(f"score{i}", [P, 2, 512]) for i in range(2)]
        av = [m.ps(f"av{i}", [P, 512]) for i in range(2)]
        work = [m.ps(f"work{i}", [P, 512]) for i in range(2)]

        loaded, zeroed, lam_step = m.sem("loaded"), m.sem("zeroed"), m.sem("lam_step")
        bn_done, aggr_done, var_done, rstd_ready, xn_ready = (m.sem(s) for s in ("bn_done", "aggr_done", "var_done", "rstd_ready", "xn_ready"))
        work_full, work_copied = m.sem("work_full"), [m.sem(f"work_copied{i}") for i in range(2)]
        sq_ready, ss_ready, ms_ready, rms_ready = (m.sem(s) for s in ("sq_ready", "ss_ready", "ms_ready", "rms_ready"))
        rot_step, qk_ready = m.sem("rot_step"), m.sem("qk_ready")
        score_full, score_exped = m.sem("score_full"), m.sem("score_exped")
        masked, av_done, av_read, fin_step, y_ready = (m.sem(s) for s in ("masked", "av_done", "av_read", "fin_step", "y_ready"))
        h_done = m.sem("h_done")
        block = ctx.enter_context(nc.Block())

        def full_at(hb, e):
            return hb * 2 + (e + 1)

        def claim_at(hb, e):
            return hb + (e // 2 + 1)

        def copied_at(hb, e):
            return hb + (e // 2 + 2)

        @block.sync
        def _(sp):
            for dst, src in ((wqk[:, :, :], A["wqk"]), (wv[:, :, :], A["wv"]), (wo[:, :, :], A["wo"]), (ident[:, :], A["ident"]),
                             (upper[:, :], A["upper"]), (rot[:, :, :, :], A["rot"])):
                sp.dma_start(dst, src).then_inc(loaded, 16)
            sp.dma_start(lam_in[:, :, :, :], A["lambdas"].partition_broadcast(P)).then_inc(loaded, 16)
        LOADED = 16 * 7

        def norm_stats(dve, b):
            for t in range(TPB):
                nc.vector.bn_stats(bn[:, t, :], H[:, bass.ds(b * TPB + t, 1), :].squeeze(1)).then_inc(bn_done, 1)
            dve.wait_ge(bn_done, b * TPB + TPB)
            nc.vector.memset(pause[:, :], 0.0)
            for t in range(TPB):
                nc.vector.bn_aggr(mv[:, t, :], bn[:, t, :]).then_inc(aggr_done, 1)

        def norm_apply(dve, b):
            dve.wait_ge(rstd_ready, b + 1)
            for t in range(TPB):
                nc.vector.tensor_scalar(xn[:, t, :], H[:, bass.ds(b * TPB + t, 1), :].squeeze(1), mv[:, t, 0:1],
                                        rstd[:, t:t + 1], ALU.subtract, ALU.mult).then_inc(xn_ready, 1)

        def head_sums(dve, b):
            for t in range(TPB):
                dve.wait_ge(sq_ready, b * TPB + t + 1)
                nc.vector.tensor_reduce(ss[:, t * 32:(t + 1) * 32], sq[:, t, :].rearrange("p (h d) -> p h d", d=HD),
                                        AX.X, ALU.add).then_inc(ss_ready, 1)

        def rotate(dve, b):
            dve.wait_ge(rms_ready, b + 1)
            every = lambda x: x[:, :, :].rearrange("p t (h d) -> p (t h) d", d=HD)
            nc.vector.tensor_tensor(every(rc), every(qk), rr[:, :].unsqueeze(2).to_broadcast([P, TPB * 32, HD]),
                                    ALU.mult).then_inc(rot_step, 1)
            dve.wait_ge(rot_step, b * 4 + 1)
            by = lambda x: x[:, :, :].rearrange("p t (h d) -> p t h d", d=HD)
            cs = lambda i, a, z: rot[:, i, :, a:z].unsqueeze(2).to_broadcast([P, TPB, 32, z - a])
            nc.vector.tensor_tensor(by(sq)[:, :, :, 0:8], by(rc)[:, :, :, 8:16], cs(1, 0, 8), ALU.mult).then_inc(rot_step, 1)
            nc.vector.tensor_tensor(by(sq)[:, :, :, 8:16], by(rc)[:, :, :, 0:8], cs(1, 8, 16), ALU.mult).then_inc(rot_step, 1)
            dve.wait_ge(rot_step, b * 4 + 3)
            nc.vector.tensor_tensor(by(rc), by(rc), cs(0, 0, 16), ALU.mult).then_inc(rot_step, 1)
            dve.wait_ge(rot_step, b * 4 + 4)
            nc.vector.tensor_tensor(q[:, :, :], rc[:, :, 0:D], sq[:, :, 0:D], ALU.add).then_inc(qk_ready, 1)
            for ver in range(2):
                pick = lambda x: x[:, :, D:2 * D].rearrange("p t (s v d) -> p t s v d", v=2, d=HD)[:, :, :, ver, :]
                nc.vector.tensor_tensor(kp[:, :, ver, :, ver * HD:(ver + 1) * HD], pick(rc), pick(sq), ALU.add
                                        ).then_inc(qk_ready, 1)

        def copy_v(dve, b, hb):
            for x in range(2):
                dve.wait_ge(work_full, full_at(hb, 6 + x))
                nc.vector.tensor_copy(v1[:, 2 * x:2 * x + 2, :, 0:VD].rearrange("p t j d -> p t j d"),
                                      work[x][:, :].rearrange("p (t j d) -> p t j d", t=2, d=VD)).then_inc(work_copied[x], 1)

        def copy_qT(dve, hb):
            for e in range(2):
                dve.wait_ge(work_full, full_at(hb, 8 + e))
                nc.vector.tensor_copy(qT[:, e, :], work[e][:, :]).then_inc(work_copied[e], 1)

        def finish_unit(dve, b, j):
            dve.wait_ge(av_done, b * NPAIR + j + 3)
            o = av[j % 2][:, 0:2 * TPB * VO].rearrange("p (g c) -> p g c", c=VO)
            nc.vector.reciprocal(rsum[:, :], o[:, :, VD:VO].squeeze(2)).then_inc(fin_step, 1)
            dve.wait_ge(fin_step, (b * NPAIR + j) * 2 + 1)
            nc.vector.tensor_scalar(rsum[:, TPB:2 * TPB], rsum[:, TPB:2 * TPB], lam[:, 2:3], None, ALU.mult).then_inc(fin_step, 1)
            dve.wait_ge(fin_step, (b * NPAIR + j) * 2 + 2)
            nc.vector.tensor_tensor(parts[:, :, :], o[:, :, 0:VD], rsum[:, :].unsqueeze(2).to_broadcast([P, 2 * TPB, VD]),
                                    ALU.mult).then_inc(av_read, 1)
            dve.wait_ge(av_read, b * NPAIR + j + 3)
            nc.vector.tensor_tensor(y[:, :, j * VD:(j + 1) * VD], parts[:, 0:TPB, :], parts[:, TPB:2 * TPB, :], ALU.subtract
                                    ).then_inc(y_ready, 1)

        def add_out(dve, b, hb, e0):
            for x in range(2):
                dve.wait_ge(work_full, full_at(hb, e0 + 2 + x))
                hh = H[:, bass.ds(b * TPB + 2 * x, 2), :]
                nc.vector.tensor_tensor(hh, work[x][:, :].rearrange("p (t d) -> p t d", t=2), hh, ALU.add
                                        ).then_inc(work_copied[x], 1)

        @block.vector
        def _(dve):
            nc.vector.memset(half_neg[:, :], -0.5).then_inc(zeroed, 1)
            nc.vector.memset(eps[:, :], LN_EPS).then_inc(zeroed, 1)
            nc.vector.memset(rms_eps[:, :], RMS_EPS * HD).then_inc(zeroed, 1)
            nc.vector.memset(kp[:, :, :, :, :], 0.0).then_inc(zeroed, 1)
            nc.vector.memset(v1[:, :, :, VD:VO], 1.0).then_inc(zeroed, 1)
            nc.vector.sem_inc(av_read, 2)
            dve.wait_ge(zeroed, 5)
            dve.wait_ge(loaded, LOADED)
            nc.vector.tensor_tensor(lam_prod[:, :, :], lam_in[:, :, 0, :], lam_in[:, :, 1, :], ALU.mult).then_inc(lam_step, 1)
            dve.wait_ge(lam_step, 1)
            nc.vector.tensor_reduce(lam[:, 0:2], lam_prod[:, :, :], AX.X, ALU.add).then_inc(lam_step, 1)
            dve.wait_ge(lam_step, 3)
            nc.vector.tensor_tensor(lam[:, 2:3], lam[:, 0:1], lam[:, 1:2], ALU.subtract).then_inc(lam_step, 1)
            dve.wait_ge(lam_step, 4)
            nc.vector.tensor_scalar(lam[:, 2:3], lam[:, 2:3], LAMBDA_INIT, None, ALU.add).then_inc(lam_step, 1)
            dve.wait_ge(lam_step, 5)
            norm_stats(dve, 0)
            norm_apply(dve, 0)
            head_sums(dve, 0)
            rotate(dve, 0)
            copy_v(dve, 0, 0)
            copy_qT(dve, 0)

            def batch(b, hb, more):
                if more:
                    norm_stats(dve, b + 1)
                    norm_apply(dve, b + 1)
                for j in range(NPAIR):
                    finish_unit(dve, b, j)
                    if more and j == 4:
                        head_sums(dve, b + 1)
                    if more and j == 5:
                        rotate(dve, b + 1)
                if more:
                    copy_v(dve, b + 1, hb)
                    copy_qT(dve, hb)
                add_out(dve, b, hb, 14 if more else 0)

            with dve.Fori(0, LAST) as i:
                batch(i, i * 9 + 7, True)
            batch(LAST, LAST * 9 + 7, False)

        @block.gpsimd
        def _(pool):
            def norm_pow(b):
                pool.wait_ge(aggr_done, b * TPB + TPB)
                nc.gpsimd.tensor_tensor(var[:, :], mv[:, :, 1:2].squeeze(2), eps[:, 0:TPB], ALU.add).then_inc(var_done, 1)
                pool.wait_ge(var_done, b + 1)
                nc.gpsimd.tensor_tensor(rstd[:, :], var[:, :], half_neg[:, 0:TPB], ALU.pow).then_inc(rstd_ready, 1)

            def squares(b, hb):
                for t in range(TPB):
                    pool.wait_ge(work_copied[t % 2], copied_at(hb, 2 + t))
                    nc.gpsimd.tensor_tensor(sq[:, t, :], qk[:, t, :], qk[:, t, :], ALU.mult).then_inc(sq_ready, 1)

            def rms_pow(b):
                pool.wait_ge(ss_ready, b * TPB + TPB)
                nc.gpsimd.tensor_tensor(ss[:, :], ss[:, :], rms_eps[:, :], ALU.add).then_inc(ms_ready, 1)
                pool.wait_ge(ms_ready, b + 1)
                nc.gpsimd.tensor_tensor(rr[:, :], ss[:, :], half_neg[:, :], ALU.pow).then_inc(rms_ready, 1)

            def mask_unit(b, j):
                pool.wait_ge(score_exped, (b * NPAIR + j) * 4 + 6)
                diag = prob[:, j % 2, :, :].rearrange("p h (k s) -> p h k s", s=640)[:, :, :, 0:P]
                nc.gpsimd.tensor_tensor(diag, diag, upper[:, :].unsqueeze(1).unsqueeze(1).to_broadcast([P, 2, TPB, P]),
                                        ALU.mult).then_inc(masked, 1)

            pool.wait_ge(zeroed, 5)
            pool.wait_ge(loaded, LOADED)
            norm_pow(0)
            squares(0, 0)
            rms_pow(0)

            def batch(b, hb, more):
                if more:
                    norm_pow(b + 1)
                for j in range(NPAIR):
                    mask_unit(b, j)
                    if more and j == 4:
                        squares(b + 1, hb)
                    if more and j == 5:
                        rms_pow(b + 1)

            with pool.Fori(0, LAST) as i:
                batch(i, i * 9 + 7, True)
            batch(LAST, LAST * 9 + 7, False)

        @block.scalar
        def _(act):
            def copy(hb, e, dst):
                act.wait_ge(work_full, full_at(hb, e))
                nc.scalar.activation(dst, work[e % 2][:, :], ACT.Copy).then_inc(work_copied[e % 2], 1)

            def copy_xT(hb):
                for c in range(2):
                    copy(hb, c, xT[:, c, :])

            def copy_qk(b, hb):
                for t in range(TPB):
                    copy(hb, 2 + t, qk[:, t, :])

            def copy_kT(hb):
                for e in range(4):
                    copy(hb, 10 + e, kT[:, e, :])

            for k in range(2):
                nc.scalar.sem_inc(work_copied[k], 1)
            nc.scalar.sem_inc(score_exped, 2)
            act.wait_ge(lam_step, 2)
            nc.scalar.activation(lam[:, 0:2], lam[:, 0:2], ACT.Exp).then_inc(lam_step, 1)
            copy_xT(0)
            copy_qk(0, 0)
            copy_kT(0)

            def batch(b, hb, more):
                for j in range(NPAIR):
                    act.wait_ge(av_done, b * NPAIR + j + 1)
                    for kc in range(TPB):
                        act.wait_ge(score_full, (b * NPAIR + j) * 4 + kc + 1)
                        n = T - kc * P
                        nc.scalar.activation(prob[:, j % 2, :, kc * (T + P):kc * T + T], score[kc % 2][:, :, 0:n], ACT.Exp,
                                             scale=HD ** 0.5).then_inc(score_exped, 1)
                    if more and j == 1:
                        copy_xT(hb)
                    if more and j == 4:
                        copy_qk(b + 1, hb)
                if more:
                    copy_kT(hb)
                for c in range(2):
                    copy(hb, (14 if more else 0) + c, yT[:, c, :])

            with act.Fori(0, LAST) as i:
                batch(i, i * 9 + 7, True)
            batch(LAST, LAST * 9 + 7, False)

        @block.tensor
        def _(pe):
            def flip(hb, e, src):
                pe.wait_ge(work_copied[e % 2], claim_at(hb, e))
                for t in range(TPB):
                    mm = nc.tensor.transpose(work[e % 2][:, t * P:(t + 1) * P], src(t), ident[:, :])
                mm.then_inc(work_full, 1)

            def turn_x(b, hb):
                pe.wait_ge(xn_ready, b * TPB + TPB)
                for c in range(2):
                    flip(hb, c, lambda t: xn[:, t, c * P:(c + 1) * P])

            def mul(hb, e, n, src, w, cols):
                pe.wait_ge(work_copied[e % 2], claim_at(hb, e))
                for i, t in enumerate(cols):
                    for c in range(2):
                        mm = nc.tensor.matmul(work[e % 2][:, i * n:(i + 1) * n], src[:, c, t * P:(t + 1) * P], w[:, c, :],
                                              start=c == 0, stop=c == 1)
                mm.then_inc(work_full, 1)

            def make_qk(hb):
                for k in range(2):
                    pe.wait_ge(work_copied[k], copied_at(hb, k))
                for t in range(TPB):
                    mul(hb, 2 + t, 2 * D, xT, wqk, [t])

            def make_v_turn_qk(b, hb):
                for x in range(2):
                    mul(hb, 6 + x, D, xT, wv, [2 * x, 2 * x + 1])
                pe.wait_ge(qk_ready, b * 3 + 3)
                for c in range(2):
                    flip(hb, 8 + c, lambda t: q[:, t, c * P:(c + 1) * P])
                for e in range(4):
                    ver, half = e % 2, e // 2
                    flip(hb, 10 + e, lambda t: kp[:, t, ver, half * 4:half * 4 + 4, :].rearrange("p s d -> p (s d)"))

            def scores(b, j):
                for kc in range(TPB):
                    pe.wait_ge(score_exped, (b * NPAIR + j) * 4 + kc + 1)
                    for half in range(2):
                        s = (j // 2 + 2 * half) % 4
                        r = slice(32 * s, 32 * s + 32)
                        mm = nc.tensor.matmul(score[kc % 2][:, half, 0:T - kc * P], kT[r, half * 2 + j % 2, kc * P:(kc + 1) * P],
                                              qT[r, half, kc * P:T], start=True, stop=True)
                    mm.then_inc(score_full, 1)

            def values(b, j):
                pe.wait_ge(masked, b * NPAIR + j + 1)
                pe.wait_ge(av_read, b * NPAIR + j + 1)
                for half in range(2):
                    for qc in range(TPB):
                        g = half * TPB + qc
                        for kc in range(qc + 1):
                            at = kc * T + qc * P
                            mm = nc.tensor.matmul(av[j % 2][:, g * VO:(g + 1) * VO], prob[:, j % 2, half, at:at + P],
                                                  v1[:, kc, j, :], start=kc == 0, stop=kc == qc)
                mm.then_inc(av_done, 1)

            def project(b, hb, e0):
                pe.wait_ge(y_ready, b * NPAIR + NPAIR)
                for c in range(2):
                    flip(hb, e0 + c, lambda t: y[:, t, c * P:(c + 1) * P])
                for k in range(2):
                    pe.wait_ge(work_copied[k], copied_at(hb, e0 + k))
                for x in range(2):
                    mul(hb, e0 + 2 + x, D, yT, wo, [2 * x, 2 * x + 1])

            nc.tensor.sem_inc(av_done, 2)
            pe.wait_ge(loaded, LOADED)
            turn_x(0, 0)
            make_qk(0)
            make_v_turn_qk(0, 0)

            def batch(b, hb, prev, more):
                for e in range(6, 14):
                    pe.wait_ge(work_copied[e % 2], copied_at(prev, e))
                scores(b, 0)
                for j in range(NPAIR):
                    if j + 1 < NPAIR:
                        scores(b, j + 1)
                    if more and j == 0:
                        turn_x(b + 1, hb)
                    if more and j == 3:
                        make_qk(hb)
                    values(b, j)
                if more:
                    make_v_turn_qk(b + 1, hb)
                project(b, hb, 14 if more else 0)

            with pe.Fori(0, LAST) as i:
                batch(i, i * 9 + 7, i * 9 + 0, True)
            batch(LAST, LAST * 9 + 7, LAST * 9 - 2, False)


def expert_stream(nc, m, N, I, STEP, *, turn_ready, x_of, down_of, mul_ready, mul_also, identT,
                  dve_more, act_first, act_more, pool_prog, sync_prog, finish, prologue_dve, dve_before):
    NI = I // P
    xT, gs, hs, hT = (m.sb(s, sh) for s, sh in (("xT", [P, 2, 2, P]), ("gs", [P, 2, I]), ("hs", [P, 2, I]), ("hT", [P, 2, NI, P])))
    pT, pG, pU, pD = ([m.ps(f"{s}{k}", [P, 512]) for k in range(2)] for s in ("pT", "pG", "pU", "pD"))
    names = ("x_turned", "xT_ready", "gu_full", "silu_ready", "hs_ready", "h_turned", "hT_ready", "down_full", "down_read")
    s = {x: m.sem(x) for x in names}
    block = m.ctx.enter_context(nc.Block())

    def steps(eng, step):
        with eng.Fori(0, N // STEP - 1) as i:
            for q in range(STEP):
                step(i * STEP + q, q % 2, q, i, STEP)
        for q in range(STEP):
            step(N - STEP + q, q % 2, q, N // STEP - 1, STEP - 1 - q)

    @block.tensor
    def _(pe):
        for x, n in (("x_turned", 4), ("gu_full", 1), ("h_turned", 2), ("down_full", 1)):
            pe.sem_inc(s[x], n)

        def turn(n, k, q, i):
            turn_ready(pe, n, q, i)
            pe.wait_ge(s["xT_ready"], n + 1)
            for c in range(2):
                mm = nc.tensor.transpose(pT[k][:, c * P:(c + 1) * P], x_of(n, q, c), identT[:, :])
            mm.then_inc(s["x_turned"], 1)

        def multiply(n, k, i):
            gate, up = mul_ready(pe, n, i)
            pe.wait_ge(s["xT_ready"], n + 3)
            pe.wait_ge(s["hs_ready"], n + 1)
            mul_also(pe, n, k, xT, pT)
            for w, bank in ((gate, pG), (up, pU)):
                for c in range(2):
                    mm = nc.tensor.matmul(bank[k][:, 0:I], xT[:, k, c, :], w(c), start=c == 0, stop=c == 1)
            mm.then_inc(s["gu_full"], 1)

        def turn_h(n, k):
            pe.wait_ge(s["hs_ready"], n + 3)
            pe.wait_ge(s["down_read"], n + 1)
            for c in range(NI):
                mm = nc.tensor.transpose(pD[k][:, c * P:(c + 1) * P], hs[:, k, c * P:(c + 1) * P], identT[:, :])
            mm.then_inc(s["h_turned"], 1)

        def down(n, k, i):
            w = down_of(pe, n, i)
            pe.wait_ge(s["hT_ready"], n + 1)
            for c in range(NI):
                mm = nc.tensor.matmul(pD[k][:, 0:D], hT[:, k, c, :], w(c), start=c == 0, stop=c == NI - 1)
            mm.then_inc(s["down_full"], 1)

        turn(0, 0, 0, 0)
        turn(1, 1, 1, 0)
        multiply(0, 0, 0)

        def step(n, k, q, i, left):
            if left >= 2:
                turn(n + 2, k, (q + 2) % STEP, i + (q + 2) // STEP)
            turn_h(n, k)
            if left >= 1:
                multiply(n + 1, 1 - k, i + (q + 1) // STEP)
            down(n, k, i)

        steps(pe, step)

    @block.scalar
    def _(act):
        act.sem_inc(s["xT_ready"], 2)

        def copy_x(n, k):
            act.wait_ge(s["x_turned"], n + 5)
            nc.scalar.activation(xT[:, k, :, :], pT[k][:, 0:D].rearrange("p (c t) -> p c t", c=2), ACT.Copy).then_inc(s["xT_ready"], 1)

        def silu(n, k):
            act.wait_ge(s["gu_full"], n + 2)
            act.wait_ge(s["hs_ready"], n + 1)
            nc.scalar.activation(gs[:, k, :], pG[k][:, 0:I], ACT.Silu).then_inc(s["silu_ready"], 1)

        def copy_h(n, k):
            act.wait_ge(s["h_turned"], n + 3)
            nc.scalar.activation(hT[:, k, :, :], pD[k][:, 0:NI * P].rearrange("p (c t) -> p c t", c=NI), ACT.Copy).then_inc(s["hT_ready"], 1)

        act_first(act, s)
        copy_x(0, 0)
        copy_x(1, 1)
        silu(0, 0)

        def step(n, k, q, i, left):
            if left >= 2:
                copy_x(n + 2, k)
            copy_h(n, k)
            if left >= 1:
                silu(n + 1, 1 - k)
            act_more(act, n, k, q, i, left, s)

        steps(act, step)

    @block.vector
    def _(dve):
        dve.sem_inc(s["hs_ready"], 2)
        dve.sem_inc(s["down_read"], 2)
        prologue_dve(dve)

        def gated(n, k):
            dve.wait_ge(s["silu_ready"], n + 1)
            dve.wait_ge(s["h_turned"], n + 1)
            nc.vector.tensor_tensor(hs[:, k, :], gs[:, k, :], pU[k][:, 0:I], ALU.mult).then_inc(s["hs_ready"], 1)

        dve_more(dve, 0, 0, pT)
        gated(0, 0)
        

        def step(n, k, q, i, left):
            dve_before(dve, n, q, i, left, s)
            if left >= 1:
                dve_more(dve, n + 1, 1 - k, pT)
                gated(n + 1, 1 - k)
            finish(dve, n, k, q, i, left, s, pD)

        steps(dve, step)

    if pool_prog:
        @block.gpsimd
        def _(pool):
            pool_prog(pool, s)

    if sync_prog:
        @block.sync
        def _(sp):
            sync_prog(sp, s, steps)


def zero_rows(sp, dram, rows, zeros, zeroed):
    v = dram.rearrange("(g p r) d -> g p (r d)", p=P, r=8)
    for g in range(rows // (8 * P)):
        sp.dma_start(v[g], zeros[:, :]).then_inc(zeroed, 16)
    sp.wait_ge(zeroed, 16 * (rows // (8 * P)))


class Norm:

    def __init__(self, m):
        self.pause = m.sb("pause", [P, 1])
        self.bn, self.mv = m.sb("bn", [P, TPB, 6]), m.sb("mv", [P, TPB, 2])
        self.var, self.rstd = m.sb("var", [P, TPB]), m.sb("rstd", [P, TPB])
        self.eps, self.half_neg = m.sb("eps", [P, TPB]), m.sb("half_neg", [P, TPB])
        self.bn_done, self.aggr_done = m.sem("bn_done"), m.sem("aggr_done")
        self.var_done, self.rstd_ready, self.set = m.sem("var_done"), m.sem("rstd_ready"), m.sem("norm_set")

    def constants(self, nc):
        nc.vector.memset(self.eps[:, :], LN_EPS).then_inc(self.set, 1)
        nc.vector.memset(self.half_neg[:, :], -0.5).then_inc(self.set, 1)

    def stats(self, nc, dve, H, g):
        for t in range(TPB):
            nc.vector.bn_stats(self.bn[:, t, :], H[:, bass.ds(g * TPB + t, 1), :].squeeze(1)).then_inc(self.bn_done, 1)
        dve.wait_ge(self.bn_done, g * TPB + TPB)
        nc.vector.memset(self.pause[:, :], 0.0)
        for t in range(TPB):
            nc.vector.bn_aggr(self.mv[:, t, :], self.bn[:, t, :]).then_inc(self.aggr_done, 1)

    def power(self, nc, pool, g):
        pool.wait_ge(self.aggr_done, g * TPB + TPB)
        nc.gpsimd.tensor_tensor(self.var[:, :], self.mv[:, :, 1:2].squeeze(2), self.eps[:, :], ALU.add).then_inc(self.var_done, 1)
        pool.wait_ge(self.var_done, g + 1)
        nc.gpsimd.tensor_tensor(self.rstd[:, :], self.var[:, :], self.half_neg[:, :], ALU.pow).then_inc(self.rstd_ready, 1)

    def apply(self, nc, dve, H, g, dst, ready):
        dve.wait_ge(self.rstd_ready, g + 1)
        for t in range(TPB):
            nc.vector.tensor_scalar(dst(t), H[:, bass.ds(g * TPB + t, 1), :].squeeze(1), self.mv[:, t, 0:1],
                                    self.rstd[:, t:t + 1], ALU.subtract, ALU.mult).then_inc(ready, 1)


E1, I1 = 32, 512
SORT_TILES = 96
RING = 4


def top1_experts(nc, A, S, H):
    with ExitStack() as outer:
        m = Bufs(nc, outer, "t1")
        slot = m.sb("slot", [P, TILES], I32)
        tile_tab = m.sb("tile_tab", [P, 2, SORT_TILES], I32)
        end_tab = m.sb("end_tab", [P, RING + E1], I32)
        with ExitStack() as both:
            m = Bufs(nc, both, "t1n")
            xs = m.sb("xs", [P, TILES, D])
            top, top_i = m.sb("top", [P, TILES]), m.sb("top_i", [P, TILES])
            shared_expert(nc, A, S, H, xs, top, top_i)
            sort_tokens(nc, A, S, xs, top, top_i, slot, tile_tab, end_tab)
        routed_experts(nc, A, S, tile_tab, end_tab)
        gather_add(nc, S, H, slot)


def shared_expert(nc, A, S, H, xs, top, top_i):
    with ExitStack() as ctx:
        m = Bufs(nc, ctx, "sh")
        wg, wu, wd = m.sb("wg", [P, 2, I1]), m.sb("wu", [P, 2, I1]), m.sb("wd", [P, I1 // P, D])
        wr, ident = m.sb("wr", [P, 2, E1]), m.sb("ident", [P, P])
        xn = m.sb("xn", [P, TPB, D])
        zeros = m.sb("zeros", [P, 2048])
        norm, xn_ready = Norm(m), m.sem("xn_ready")
        loaded, xs_ready, zero_set, zeroed = m.sem("loaded"), m.sem("xs_ready"), m.sem("zero_set"), m.sem("zeroed")
        max_ready, index_ready, routed, logits_full = (m.sem(s) for s in ("max_ready", "index_ready", "routed", "logits_full"))
        pause = norm.pause
        lg, mx, mi = m.sb("lg", [P, E1]), m.sb("mx", [P, 8]), m.sb("mi", [P, 8], U32)

        def turn_ready(pe, n, q, i):
            pe.wait_ge(loaded, 16 * 5)
            pe.wait_ge(routed, n + 1)
            pe.wait_ge(xn_ready, n + 1)

        def logits(pe, n, k, xT, pT):
            for c in range(2):
                mm = nc.tensor.matmul(pT[k][:, D:D + E1], xT[:, k, c, :], wr[:, c, :], start=c == 0, stop=c == 1)
            mm.then_inc(logits_full, 1)

        def prologue(dve):
            norm.constants(nc)
            dve.sem_inc(routed, 2)
            nc.vector.memset(zeros[:, :], 0.0).then_inc(zero_set, 1)
            norm.stats(nc, dve, H, 0)
            norm.apply(nc, dve, H, 0, lambda t: xn[:, t, :], xn_ready)

        def norm_ahead(dve, n, q, i, left, s):
            if q == 0 and left == 4:
                norm.stats(nc, dve, H, i + 1)
            if q == 1 and left == 4:
                dve.wait_ge(s["x_turned"], i * 4 + 8)
                dve.wait_ge(xs_ready, i * 4 + 4)
                norm.apply(nc, dve, H, i + 1, lambda t: xn[:, t, :], xn_ready)

        def largest(dve, n, k, pT):
            dve.wait_ge(logits_full, n + 1)
            nc.vector.tensor_copy(lg[:, :], pT[k][:, D:D + E1]).then_inc(routed, 1)
            dve.wait_ge(routed, n + 3)
            nc.vector.memset(pause[:, :], 0.0)
            nc.vector.max(mx[:, :], lg[:, :]).then_inc(max_ready, 1)
            dve.wait_ge(max_ready, n + 1)
            nc.vector.memset(pause[:, :], 0.0)
            nc.vector.max_index(mi[:, :], mx[:, :], lg[:, :]).then_inc(index_ready, 1)
            dve.wait_ge(index_ready, n + 1)
            nc.vector.tensor_copy(top[:, bass.ds(n, 1)], mx[:, 0:1])
            nc.vector.tensor_copy(top_i[:, bass.ds(n, 1)], mi[:, 0:1])

        def finish(dve, n, k, q, i, left, s, pD):
            dve.wait_ge(s["down_full"], n + 2)
            hh = H[:, bass.ds(n, 1), :].squeeze(1)
            nc.vector.tensor_tensor(hh, pD[k][:, 0:D], hh, ALU.add).then_inc(s["down_read"], 1)

        def pool_prog(pool, s):
            pool.wait_ge(norm.set, 2)


            def keep(g):
                for t in range(TPB):
                    pool.wait_ge(xn_ready, g * TPB + t + 1)
                    nc.gpsimd.tensor_copy(xs[:, bass.ds(g * TPB + t, 1), :].squeeze(1), xn[:, t, :]).then_inc(xs_ready, 1)

            norm.power(nc, pool, 0)
            keep(0)
            with pool.Fori(0, B - 1) as i:
                norm.power(nc, pool, i + 1)
                keep(i + 1)

        def sync_prog(sp, s, steps):
            for dst, name in ((wg, "sh_gate"), (wu, "sh_up"), (wd, "sh_down"), (wr, "gate_w")):
                sp.dma_start(dst[:, :, :], A[name]).then_inc(loaded, 16)
            sp.dma_start(ident[:, :], A["ident"]).then_inc(loaded, 16)
            sp.wait_ge(zero_set, 1)
            zero_rows(sp, S["sorted_x"], SORT_TILES * P, zeros, zeroed)

        expert_stream(nc, m, TILES, I1, 4, turn_ready=turn_ready, x_of=lambda n, q, c: xn[:, q, c * P:(c + 1) * P],
                      mul_ready=lambda pe, n, i: (lambda c: wg[:, c, :], lambda c: wu[:, c, :]),
                      down_of=lambda pe, n, i: (lambda c: wd[:, c, :]), mul_also=logits, identT=ident, dve_more=largest,
                      act_first=lambda *a: None, act_more=lambda *a: None, pool_prog=pool_prog, sync_prog=sync_prog, finish=finish, prologue_dve=prologue, dve_before=norm_ahead)


def sort_tokens(nc, A, S, xs, top, top_i, slot, tile_tab, end_tab):
    with ExitStack() as ctx:
        m = Bufs(nc, ctx, "st")
        iota, k128 = m.sb("iota", [P, P]), m.sb("k128", [P, P])
        strict_f, strict, ones = m.sb("strict_f", [P, P]), m.sb("strict", [P, P], BF16), m.sb("ones", [P, P], BF16)
        idx, score = m.sb("idx", [P, TILES]), m.sb("score", [P, TILES])
        hot = m.sb("hot", [P, TILES, E1], BF16)
        tot, run, flag = m.sb("tot", [P, E1, TILES]), m.sb("run", [P, E1, TILES]), m.sb("flag", [P, E1, TILES])
        ntile, end, base = m.sb("ntile", [P, E1]), m.sb("end", [P, E1]), m.sb("base", [P, E1])
        tile_e, tile_f = m.sb("tile_e", [P, SORT_TILES, E1]), m.sb("tile_f", [P, SORT_TILES])
        slot_f, score_in = m.sb("slot_f", [P, TILES]), m.sb("score_in", [P, TILES])
        pre = [m.ps(f"pre{g}", [P, 512]) for g in range(4)]
        sums = [m.ps(f"sums{g}", [P, 512]) for g in range(4)]
        loaded, step, counted, score_ready = m.sem("loaded"), m.sem("step"), m.sem("counted"), m.sem("score_ready")
        scaled, scattered = m.sem("scaled"), m.sem("scattered")
        block = ctx.enter_context(nc.Block())
        GT = TILES // 4
        HOT_READY = 4

        @block.sync
        def _(sp):
            for dst, name in ((iota, "iota128"), (k128, "k128"), (strict_f, "strict")):
                sp.dma_start(dst[:, :], A[name]).then_inc(loaded, 16)

        @block.scalar
        def _(act):
            act.wait_ge(step, 1)
            nc.scalar.activation(score[:, :], score_in[:, :], ACT.Sigmoid).then_inc(score_ready, 1)

        @block.tensor
        def _(pe):
            pe.wait_ge(step, 5)
            for g in range(4):
                r = hot[:, g * GT:(g + 1) * GT, :].rearrange("p t e -> p (t e)")
                nc.tensor.matmul(pre[g][:, :], strict[:, :], r, start=True, stop=True).then_inc(counted, 1)
                nc.tensor.matmul(sums[g][:, :], ones[:, :], r, start=True, stop=True).then_inc(counted, 1)

        @block.vector
        def _(dve):
            n = [0]

            def link(ins):
                n[0] += 1
                ins.then_inc(step, 1)
                dve.wait_ge(step, n[0])

            link(nc.vector.tensor_copy(score_in[:, :], top[:, :]))
            dve.wait_ge(loaded, 48)
            link(nc.vector.tensor_copy(idx[:, :], top_i[:, :]))
            link(nc.vector.tensor_copy(strict[:, :], strict_f[:, :]))
            link(nc.vector.memset(ones[:, :], 1.0))
            link(nc.vector.tensor_tensor(hot[:, :, :], iota[:, 0:E1].unsqueeze(1).to_broadcast([P, TILES, E1]),
                                         idx[:, :].unsqueeze(2).to_broadcast([P, TILES, E1]), ALU.is_equal))
            link(nc.vector.memset(flag[:, :, :], 1.0))
            link(nc.vector.memset(flag[:, :, 0:1], 0.0))
            dve.wait_ge(counted, 8)
            for g in range(4):
                link(nc.vector.tensor_copy(tot[:, :, g * GT:(g + 1) * GT], sums[g][:, :].rearrange("p (t e) -> p e t", e=E1)))
            flat = lambda x: x[:, :, :].rearrange("p e t -> p (e t)")
            link(nc.vector.tensor_tensor_scan(flat(run), flat(flag), flat(tot), 0.0, ALU.mult, ALU.add))
            link(nc.vector.tensor_tensor(flag[:, :, :], run[:, :, TILES - 1:TILES].to_broadcast([P, E1, TILES]),
                                         k128[:, 0:TILES].unsqueeze(1).to_broadcast([P, E1, TILES]), ALU.is_gt))
            link(nc.vector.tensor_reduce(ntile[:, :], flag[:, :, :], AX.X, ALU.add))
            link(nc.vector.memset(base[:, :], 1.0))
            link(nc.vector.tensor_tensor_scan(end[:, :], base[:, :], ntile[:, :], 0.0, ALU.mult, ALU.add))
            link(nc.vector.tensor_tensor(base[:, :], end[:, :], ntile[:, :], ALU.subtract))
            link(nc.vector.tensor_scalar(base[:, :], base[:, :], float(P), None, ALU.mult))
            link(nc.vector.tensor_tensor(run[:, :, :], run[:, :, :], tot[:, :, :], ALU.subtract))
            link(nc.vector.tensor_tensor(run[:, :, :], run[:, :, :], base[:, :].unsqueeze(2).to_broadcast([P, E1, TILES]), ALU.add))
            place = tot[:, :, :].rearrange("p e t -> p (e t)").rearrange("p (t e) -> p t e", e=E1)
            for g in range(4):
                link(nc.vector.tensor_tensor(place[:, g * GT:(g + 1) * GT, :], pre[g][:, :].rearrange("p (t e) -> p t e", e=E1),
                                             run[:, :, g * GT:(g + 1) * GT].rearrange("p e t -> p t e"), ALU.add))
            link(nc.vector.tensor_tensor(place, place, hot[:, :, :], ALU.mult))
            link(nc.vector.tensor_reduce(slot_f[:, :], place, AX.X, ALU.add))
            link(nc.vector.tensor_copy(slot[:, :], slot_f[:, :]))
            dve.wait_ge(score_ready, 1)
            for g in range(8):
                nc.vector.tensor_tensor(xs[:, 8 * g:8 * g + 8, :], xs[:, 8 * g:8 * g + 8, :],
                                        score[:, 8 * g:8 * g + 8].unsqueeze(2).to_broadcast([P, 8, D]), ALU.mult).then_inc(scaled, 1)
            link(nc.vector.tensor_tensor(tile_e[:, :, :], end[:, :].unsqueeze(1).to_broadcast([P, SORT_TILES, E1]),
                                         iota[:, 0:SORT_TILES].unsqueeze(2).to_broadcast([P, SORT_TILES, E1]), ALU.is_le))
            link(nc.vector.tensor_reduce(tile_f[:, :], tile_e[:, :, :], AX.X, ALU.add))
            link(nc.vector.tensor_scalar(tile_f[:, :], tile_f[:, :], float(E1 - 1), None, ALU.min))
            link(nc.vector.tensor_copy(tile_tab[:, 0, :], tile_f[:, :]))
            link(nc.vector.tensor_scalar(tile_tab[:, 1, :], tile_tab[:, 0, :], RING - 1, None, ALU.bitwise_and))
            link(nc.vector.memset(end_tab[:, :], 0))
            link(nc.vector.tensor_copy(end_tab[:, RING:RING + E1], end[:, :]))

        @block.gpsimd
        def _(pool):
            for t in range(TILES):
                pool.wait_ge(scaled, t // 8 + 1)
                nc.gpsimd.indirect_dma_start(S["sorted_x"], bass.IndirectOffsetOnAxis(ap=slot[:, t:t + 1], axis=0),
                                             xs[:, t, :], None).then_inc(scattered, 16)
            pool.wait_ge(scattered, 16 * TILES)


def routed_experts(nc, A, S, tile_tab, end_tab):
    with ExitStack() as ctx:
        m = Bufs(nc, ctx, "ro")
        wgu, wd = m.sb("wgu", [P, RING, 2, 2 * I1]), m.sb("wd", [P, RING, I1 // P, D])
        ident, xt, o = m.sb("ident", [P, P]), m.sb("xt", [P, 4, D]), m.sb("o", [P, 4, D])
        id_in, gu_in, wd_in, gu_go, wd_go = (m.sem(x) for x in ("id_in", "gu_in", "wd_in", "gu_go", "wd_go"))
        x_in = [m.sem(f"x_in{k}") for k in range(4)]
        o_ready, o_out = m.sem("o_ready"), [m.sem(f"o_out{k}") for k in range(4)]
        xv = S["sorted_x"].rearrange("(n p) d -> n p d", p=P)
        yv = S["sorted_y"].rearrange("(n p) d -> n p d", p=P)

        def turn_ready(pe, n, q, i):
            pe.wait_ge(id_in, 16)
            pe.wait_ge(x_in[q], i * 16 + 16)

        def place(pe, n):
            e = pe.value_load(tile_tab[0:1, 0, bass.ds(n, 1)], min_val=0, max_val=E1 - 1)
            r = pe.value_load(tile_tab[0:1, 1, bass.ds(n, 1)], min_val=0, max_val=RING - 1)
            return e, r

        def mul_ready(pe, n, i):
            e, r = place(pe, n)
            pe.wait_ge(gu_in, e * 16 + 16)
            w = lambda a: (lambda c: wgu[:, bass.ds(r, 1), c, a:a + I1].squeeze(1))
            return w(0), w(I1)

        def down_of(pe, n, i):
            e, r = place(pe, n)
            pe.wait_ge(wd_in, e * 16 + 16)
            return lambda c: wd[:, bass.ds(r, 1), c, :].squeeze(1)

        def finish(dve, n, k, q, i, left, s, pD):
            dve.wait_ge(s["down_full"], n + 2)
            dve.wait_ge(o_out[q], i * 16 + 16)
            nc.vector.tensor_copy(o[:, q, :], pD[k][:, 0:D]).then_inc(s["down_read"], 1)

        def act_first(act, s):
            for k in range(4):
                act.dma_start(xt[:, k, :], xv[k]).then_inc(x_in[k], 16)
                act.sem_inc(o_out[k], 16)

        def act_more(act, n, k, q, i, left, s):
            if left == 4:
                act.wait_ge(s["x_turned"], n + 5)
                act.dma_start(xt[:, q, :], xv[bass.ds(n + 4, 1)].squeeze(0)).then_inc(x_in[q], 16)
            act.wait_ge(s["down_read"], n + 3)
            act.dma_start(yv[bass.ds(n, 1)].squeeze(0), o[:, q, :]).then_inc(o_out[q], 16)
            if left == 0:
                for k in range(4):
                    act.wait_ge(o_out[k], 16 * (SORT_TILES // 4) + 16)

        def load_expert(eng, e, k, dst, src, arrived, used, go, first=False):
            gone = eng.value_load(end_tab[0:1, bass.ds(e, 1)], min_val=0, max_val=SORT_TILES)
            eng.wait_ge(used, gone + 1)
            eng.sem_inc(go, 1)
            if not first:
                eng.wait_ge(arrived, e * 16)
                if src is A["ro_down"]:
                    eng.sem_inc(go, 1)
            eng.dma_start(dst[:, k, :, :], src[bass.ds(e, 1)].squeeze(0)).then_inc(arrived, 16)

        def pool_prog(pool, s):
            for k in range(RING):
                load_expert(pool, k, k, wd, A["ro_down"], wd_in, s["down_full"], wd_go, k == 0)
            with pool.Fori(1, E1 // RING) as i:
                for k in range(RING):
                    load_expert(pool, i * RING + k, k, wd, A["ro_down"], wd_in, s["down_full"], wd_go)

        def sync_prog(sp, s, steps):
            sp.dma_start(ident[:, :], A["ident"]).then_inc(id_in, 16)
            for k in range(RING):
                load_expert(sp, k, k, wgu, A["ro_gu"], gu_in, s["gu_full"], gu_go, k == 0)
            with sp.Fori(1, E1 // RING) as i:
                for k in range(RING):
                    load_expert(sp, i * RING + k, k, wgu, A["ro_gu"], gu_in, s["gu_full"], gu_go)

        expert_stream(nc, m, SORT_TILES, I1, 4, turn_ready=turn_ready, x_of=lambda n, q, c: xt[:, q, c * P:(c + 1) * P],
                      mul_ready=mul_ready, down_of=down_of, mul_also=lambda *a: None, identT=ident,
                      dve_more=lambda *a: None, act_first=act_first, act_more=act_more, pool_prog=pool_prog,
                      sync_prog=sync_prog, finish=finish, prologue_dve=lambda dve: None, dve_before=lambda *a: None)


def gather_add(nc, S, H, slot):
    R = 8
    with ExitStack() as ctx:
        m = Bufs(nc, ctx, "ga")
        g = m.sb("g", [P, R, D])
        got, added = [m.sem(f"got{r}") for r in range(R)], m.sem("added")
        block = ctx.enter_context(nc.Block())

        @block.gpsimd
        def _(pool):
            for t in range(TILES):
                if t >= R:
                    pool.wait_ge(added, t - R + 1)
                nc.gpsimd.indirect_dma_start(g[:, t % R, :], None, S["sorted_y"],
                                             bass.IndirectOffsetOnAxis(ap=slot[:, t:t + 1], axis=0)).then_inc(got[t % R], 16)

        @block.vector
        def _(dve):
            for t in range(TILES):
                dve.wait_ge(got[t % R], 16 * (t // R + 1))
                nc.vector.tensor_tensor(H[:, t, :], H[:, t, :], g[:, t % R, :], ALU.add).then_inc(added, 1)


NH, KEEP = 16, 204
DROP = -1e30


def sparse_attention(nc, A, S, H):
    routing_scores(nc, A, S, H)
    keep_largest(nc, S)
    masked_attention(nc, A, S, H)


def routing_scores(nc, A, S, H):
    HID = 64
    with ExitStack() as ctx:
        m = Bufs(nc, ctx, "rs")
        w1, w2, b1, b2, ident = m.sb("w1", [P, 2, HID]), m.sb("w2", [HID, P]), m.sb("b1", [HID, 1]), m.sb("b2", [NH, 1]), m.sb("ident", [P, P])
        xn, xT = m.sb("xn", [P, TPB, D]), m.sb("xT", [P, 2, 2, T])
        h1, r1, r2 = m.sb("h1", [HID, 2, T]), m.sb("r1", [NH, 2, T]), m.sb("r2", [NH, 2, T])
        norm = Norm(m)
        turn = [m.ps(f"turn{c}", [P, T]) for c in range(2)]
        hid, lg = [m.ps(f"hid{k}", [P, T]) for k in range(2)], [m.ps(f"lg{k}", [P, T]) for k in range(2)]
        loaded, xn_ready, x_turned, xT_ready = (m.sem(x) for x in ("loaded", "xn_ready", "x_turned", "xT_ready"))
        hid_full, h1_ready, lg_full, r1_ready, r2_ready = (m.sem(x) for x in ("hid_full", "h1_ready", "lg_full", "r1_ready", "r2_ready"))
        r_out = [m.sem(f"r_out{k}") for k in range(2)]
        block = ctx.enter_context(nc.Block())
        LOADED = 16 * 5

        @block.sync
        def _(sp):
            for dst, name in ((w1[:, :, :], "r_w1"), (w2[:, :], "r_w2"), (b1[:, :], "r_b1"), (b2[:, :], "r_b2"), (ident[:, :], "ident")):
                sp.dma_start(dst, A[name]).then_inc(loaded, 16)
            for k in range(2):
                sp.sem_inc(r_out[k], 16)
            rv = S["route"].rearrange("(b h) t -> b h t", h=NH)
            with sp.Fori(0, B // 2) as j:
                for k in range(2):
                    sp.wait_ge(r2_ready, j * 2 + k + 1)
                    sp.dma_start(rv[bass.ds(j * 2 + k, 1)].squeeze(0), r2[:, k, :]).then_inc(r_out[k], 16)
            for k in range(2):
                sp.wait_ge(r_out[k], 16 * (B // 2 + 1))

        @block.gpsimd
        def _(pool):
            pool.wait_ge(norm.set, 2)
            with pool.Fori(0, B) as g:
                norm.power(nc, pool, g)

        @block.vector
        def _(dve):
            norm.constants(nc)
            dve.sem_inc(x_turned, 2)
            with dve.Fori(0, B) as g:
                norm.stats(nc, dve, H, g)
                dve.wait_ge(x_turned, g * 2 + 2)
                norm.apply(nc, dve, H, g, lambda t: xn[:, t, :], xn_ready)

        @block.scalar
        def _(act):
            for s, n in ((xT_ready, 2), (h1_ready, 2), (r1_ready, 2)):
                act.sem_inc(s, n)
            act.wait_ge(loaded, LOADED)
            with act.Fori(0, B // 2) as j:
                for k in range(2):
                    b = j * 2 + k
                    for c in range(2):
                        act.wait_ge(x_turned, b * 2 + c + 3)
                        nc.scalar.activation(xT[:, k, c, :], turn[c][:, :], ACT.Copy).then_inc(xT_ready, 1)
                    act.wait_ge(hid_full, b + 1)
                    nc.scalar.activation(h1[:, k, :], hid[k][0:HID, :], ACT.Relu, bias=b1[:, 0:1]).then_inc(h1_ready, 1)
                    act.wait_ge(lg_full, b + 1)
                    nc.scalar.activation(r1[:, k, :], lg[k][0:NH, :], ACT.Sigmoid, bias=b2[:, 0:1]).then_inc(r1_ready, 1)
                    act.wait_ge(r1_ready, b + 3)
                    act.wait_ge(r_out[k], j * 16 + 16)
                    nc.scalar.activation(r2[:, k, :], r1[:, k, :], ACT.Sigmoid).then_inc(r2_ready, 1)

        @block.tensor
        def _(pe):
            pe.wait_ge(loaded, LOADED)
            with pe.Fori(0, B // 2) as j:
                for k in range(2):
                    b = j * 2 + k
                    pe.wait_ge(xn_ready, b * TPB + TPB)
                    for c in range(2):
                        pe.wait_ge(xT_ready, b * 2 + c + 1)
                        for t in range(TPB):
                            mm = nc.tensor.transpose(turn[c][:, t * P:(t + 1) * P], xn[:, t, c * P:(c + 1) * P], ident[:, :])
                        mm.then_inc(x_turned, 1)
                    pe.wait_ge(xT_ready, b * 2 + 4)
                    pe.wait_ge(h1_ready, b + 1)
                    for c in range(2):
                        mm = nc.tensor.matmul(hid[k][0:HID, :], w1[:, c, :], xT[:, k, c, :], start=c == 0, stop=c == 1)
                    mm.then_inc(hid_full, 1)
                    pe.wait_ge(h1_ready, b + 3)
                    pe.wait_ge(r1_ready, b + 1)
                    nc.tensor.matmul(lg[k][:, :], w2[:, :], h1[:, k, :], start=True, stop=True).then_inc(lg_full, 1)


def keep_largest(nc, S):
    ROUNDS = -(-KEEP // 8)
    SPARE = ROUNDS * 8 - KEEP
    TAKEN = -1.0
    with ExitStack() as ctx:
        m = Bufs(nc, ctx, "kl")
        v, mx, out = m.sb("v", [P, 2, 2, T]), m.sb("mx", [P, 2, 8]), m.sb("out", [P, 2, T], BF16)
        loaded, stored, made = m.sem("loaded"), m.sem("stored"), m.sem("made")
        found, taken = m.sem("found"), m.sem("taken")
        block = ctx.enter_context(nc.Block())

        @block.sync
        def _(sp):
            for g in range(2):
                sp.dma_start(v[:, g, 0, :], S["route"][g * P:(g + 1) * P, :]).then_inc(loaded, 16)
            for g in range(2):
                sp.wait_ge(made, g + 3)
                sp.dma_start(S["mask"][g * P:(g + 1) * P, :], out[:, g, :]).then_inc(stored, 16)
            sp.wait_ge(stored, 32)

        @block.vector
        def _(dve):
            dve.wait_ge(loaded, 32)
            n = 0
            for r in range(ROUNDS):
                for g in range(2):
                    if r:
                        dve.wait_ge(taken, 2 * r + g - 1)
                    nc.vector.max(mx[:, g, :], v[:, g, r % 2, :]).then_inc(found, 1)
                    n += 1
                for g in range(2):
                    dve.wait_ge(found, 2 * r + g + 1)
                    if r == ROUNDS - 1:
                        nc.vector.memset(mx[:, g, 8 - SPARE:8], TAKEN).then_inc(made, 1)
                for g in range(2):
                    if r == ROUNDS - 1:
                        dve.wait_ge(made, g + 1)
                    nc.vector.match_replace(v[:, g, 1 - r % 2, :], mx[:, g, :], v[:, g, r % 2, :], TAKEN).then_inc(taken, 1)
            dve.wait_ge(taken, 2 * ROUNDS)
            for g in range(2):
                nc.vector.tensor_scalar(v[:, g, 1 - ROUNDS % 2, :], v[:, g, ROUNDS % 2, :], TAKEN, 1.0, ALU.is_equal, ALU.subtract
                                        ).then_inc(taken, 1)
            for g in range(2):
                dve.wait_ge(taken, 2 * ROUNDS + g + 1)
                nc.vector.tensor_scalar(out[:, g, :], v[:, g, 1 - ROUNDS % 2, :], -DROP, None, ALU.mult).then_inc(made, 1)


def masked_attention(nc, A, S, H):
    HD, NG, GH = 16, 4, 4
    ROWS = 6 * HD
    Q_PARTS, K_PARTS = (0, 0, 0, 1, 1, 2), (0, 1, 2, 0, 1, 0)
    STACK = 13 * 16
    ORD = {(0, "FIN"): 0, (0, "MAX"): 1, (0, "V0"): 2, (0, "V1"): 3, (1, "FIN"): 4, (1, "MAX"): 5,
           (2, "FIN"): 6, (2, "MAX"): 7, (2, "X0"): 8, (2, "X1"): 9, (2, "Q0"): 10,
           (3, "FIN"): 11, (3, "MAX"): 12, (3, "Q1"): 13, (3, "K0"): 14, (3, "K1"): 15}
    STEP = {(0, 3): "V0", (0, 5): "V1", (2, 3): "X0", (2, 4): "X1", (2, 6): "Q0",
            (3, 3): "Q1", (3, 5): "K0", (3, 7): "K1"}
    CHUNK = {"Q0": 0, "Q1": 1, "K0": 2, "K1": 3}
    MANY = 99
    PRO = ["X0", "X1", "Q0", "Q1", "K0", "K1", "V0", "V1"]
    with ExitStack() as ctx:
        m = Bufs(nc, ctx, "ma")
        w, wv, ident, bias = m.sb("w", [P, 2, 4, P]), m.sb("wv", [P, 2, D]), m.sb("ident", [P, P]), m.sb("bias", [P, 4])
        ident16, bv = m.sb("ident16", [P, P], BF16), m.sb("bv", [P, D])
        xn, xT = m.sb("xn", [P, TPB, D]), m.sb("xT", [P, 2, T])
        full, rest, parts = m.sb("full", [P, 2, T]), m.sb("rest", [P, 2, T]), m.sb("parts", [P, 2, 3, T], BF16)
        qs, ks = m.sb("qs", [P, 2, NH, T], BF16), m.sb("ks", [P, 2, NH, T], BF16)
        v1 = m.sb("v1", [P, 2, TPB, NH, 2 * HD])
        nmax, nrest, nparts = m.sb("nmax", [P, 2, GH, TPB]), m.sb("nrest", [P, GH, TPB]), m.sb("nparts", [P, 2, TPB, 3, GH], BF16)
        nturned = m.sb("nturned", [3 * GH, T], BF16)
        prob, sumT = m.sb("prob", [P, 8, T]), m.sb("sumT", [P, 2, T])
        rden, part = m.sb("rden", [P, TPB, GH]), m.sb("part", [P, TPB, GH, HD])
        norm = Norm(m)
        s1 = [m.ps(f"s1_{i}", [P, 2, T]) for i in range(2)]
        s2 = [m.ps(f"s2_{i}", [P, T]) for i in range(2)]
        sums, work = m.ps("sums", [P, T]), m.ps("work", [P, T])
        names = ("loaded", "ones_set", "id_ready", "xn_ready", "work_full", "work_copied", "rest_ready", "mid_ready", "low_ready", "full_ready",
                 "s1_full", "max_ready", "nsplit", "nparts_ready", "nturned_ready", "s2_full", "exp_done", "av_done",
                 "sum_copied", "rden_ready", "part_ready", "nmid_ready", "passed")
        (loaded, ones_set, id_ready, xn_ready, work_full, work_copied, rest_ready, mid_ready, low_ready, full_ready, s1_full, max_ready, nsplit,
         nparts_ready, nturned_ready, s2_full, exp_done, av_done, sum_copied, rden_ready, part_ready, nmid_ready, passed) = (m.sem(x) for x in names)
        parts_out = [m.sem(f"parts_out{k}") for k in range(2)]
        stack_in, nmax_out, nmax_in = ([m.sem(f"{x}{k}") for k in range(2)] for x in ("stack_in", "nmax_out", "nmax_in"))
        block = ctx.enter_context(nc.Block())
        LOADED = 16 * 5

        class At:

            def __init__(self, j, half):
                self.j, self.half, self.b = j, half, j * 2 + half

            def next(self, n):
                h = self.half + n
                return At(self.j + h // 2, h % 2) if h >= 2 else At(self.j, h)

        def later(at, g, n):
            return at.next((g + n) // NG) if g + n >= NG else at, (g + n) % NG

        def before(at, g):
            if g:
                return at, g - 1
            return (At(at.j, 0) if at.half else At(at.j - 1, 1)), NG - 1

        present = [(half, g, key) for half in range(2) for g, key in ORD
                   if key == "FIN" or (key == "MAX" and (half, g) != (1, NG - 1)) or (key[0] == "V" and half == 0)]
        LAST_ORD = {k: i for i, k in enumerate(present)}
        LAST_EVENT = (B - 2) * 16 + 16 + len(present)

        def ordinal(at, g, key, left):
            if left == MANY:
                return at.b * 16 + (16 + ORD[g, key])
            return (B - 2) * 16 + 16 + LAST_ORD[at.half, g, key]

        def run(eng, prologue, slot, end):
            prologue()

            def pair(j, first, last):
                for half in range(2):
                    for g in range(NG):
                        left = (1 - half) * NG + NG - 1 - g
                        slot(At(j, half), g, left if last else MANY, first and half == 0 and g == 0)

            pair(0, True, False)
            with eng.Fori(1, B // 2 - 1) as j:
                pair(j, False, False)
            pair(B // 2 - 1, False, True)
            end(At(B // 2 - 1, 1))

        def events(at, g, s, left):
            key = STEP.get((g, s))
            if key is None:
                return None
            ahead = 1 if g == 0 else 2
            if left < NG * ahead - g:
                return None
            return key, at.next(ahead), ordinal(at, g, key, left)

        @block.sync
        def _(sp):
            for dst, name in ((w[:, :, :, :], "l1_wqk"), (wv[:, :, :], "l1_wv"), (ident[:, :], "ident"), (bias[:, :], "l1_bias")):
                sp.dma_start(dst, A[name]).then_inc(loaded, 16)
            sp.dma_start(bv[:, :], A["l1_bv"].to_broadcast([P, D])).then_inc(loaded, 16)
            sp.wait_ge(ones_set, 3)
            for k in range(2):
                sp.sem_inc(parts_out[k], 16)
                sp.sem_inc(nmax_in[k], 16)

            def put_parts(at, x):
                sp.wait_ge(low_ready, at.b * 4 + x + 1)
                sp.dma_start(S["parts"][at.half, x // 2, :, (x % 2) * P:(x % 2) * P + P, :].rearrange("a p t -> p a t"),
                             parts[:, x % 2, :, :]).then_inc(parts_out[x % 2], 16)

            def get_stacks(at):
                for k in range(2):
                    sp.wait_ge(parts_out[k], at.b * 32 + 48)
                    sp.sem_inc(passed, 1)
                for i, (stack, order) in enumerate(((qs, Q_PARTS), (ks, K_PARTS))):
                    for r, a in enumerate(order):
                        sp.dma_start(stack[r * HD:(r + 1) * HD, at.half, :, :],
                                     S["parts"][at.half, i, a].rearrange("(h d) t -> d h t", d=HD)).then_inc(stack_in[at.half], 16)
                sp.dma_start(ks[ROWS:ROWS + 1, at.half, :, :],
                             S["mask"].rearrange("(b h) t -> b h t", h=NH)[bass.ds(at.b, 1)]).then_inc(stack_in[at.half], 16)

            def move_maxima(at, g):
                sp.wait_ge(nturned_ready, at.b * NG + g + 1)
                sp.sem_inc(passed, 1)
                sp.wait_ge(nmax_in[g % 2], at.b * 32 + (g // 2 * 16 + 16))
                sp.dma_start(S["maxima"][g % 2], nturned[:, :]).then_inc(nmax_out[g % 2], 16)
                sp.wait_ge(nmax_out[g % 2], at.b * 32 + (g // 2 * 16 + 16))
                sp.dma_start(qs[ROWS + 1:ROWS + 4, at.half, g * GH:(g + 1) * GH, :],
                             S["maxima"][g % 2].rearrange("(a h) t -> a h t", h=GH)).then_inc(nmax_in[g % 2], 16)

            def prologue():
                for half in range(2):
                    for x in range(4):
                        put_parts(At(0, half), x)
                    get_stacks(At(0, half))
                move_maxima(At(0, 0), 0)

            def slot(at, g, left, first):
                if left >= 1:
                    move_maxima(*later(at, g, 1))
                if g == 0 and not first and left >= NG:
                    sp.wait_ge(s2_full, at.b * 64)
                    sp.sem_inc(passed, 1)
                    get_stacks(at.next(1))
                if g == 2 and left >= 2 * NG - g:
                    sp.wait_ge(stack_in[at.half], at.j * STACK + STACK)
                    sp.sem_inc(passed, 1)
                for x in {2: (0,), 3: (1, 2, 3)}.get(g, ()):
                    if left >= 2 * NG - g:
                        put_parts(at.next(2), x)

            run(sp, prologue, slot, lambda at: [sp.wait_ge(nmax_in[k], 32 * B + 16) for k in range(2)])

        @block.gpsimd
        def _(pool):
            def power(b):
                norm.power(nc, pool, b)

            def low_part(b, x, n):
                pool.wait_ge(work_copied, n + 2)
                k = x % 2
                nc.gpsimd.tensor_tensor(rest[:, k, :], full[:, k, :], parts[:, k, 0, :], ALU.subtract).then_inc(rest_ready, 1)
                pool.wait_ge(rest_ready, b * 4 + x + 1)
                pool.wait_ge(mid_ready, b * 4 + x + 1)
                nc.gpsimd.tensor_tensor(parts[:, k, 2, :], rest[:, k, :], parts[:, k, 1, :], ALU.subtract).then_inc(low_ready, 1)

            def prologue():
                pool.wait_ge(norm.set, 2)
                for b in range(2):
                    power(b)
                    for x in range(4):
                        low_part(b, x, b * 8 + 2 + x)

            def slot(at, g, left, first):
                if g == 1 and left >= 2 * NG - g:
                    power(at.b + 2)
                for s in range(8):
                    e = events(at, g, s, left)
                    if e and e[0] in CHUNK:
                        low_part(e[1].b, CHUNK[e[0]], e[2])

            run(pool, prologue, slot, lambda at: None)

        @block.tensor
        def _(pe):
            work16 = work[:, :].bitcast(BF16)

            def claim(n):
                pe.wait_ge(work_copied, n + 1)

            def event(key, at, n):
                if key == "X0":
                    pe.wait_ge(xn_ready, at.b * TPB + TPB)
                claim(n)
                if key[0] == "X":
                    c = int(key[1])
                    for t in range(TPB):
                        mm = nc.tensor.transpose(work[:, t * P:(t + 1) * P], xn[:, t, c * P:(c + 1) * P], ident[:, :])
                elif key[0] == "V":
                    for i in range(2):
                        t = 2 * int(key[1]) + i
                        for c in range(2):
                            mm = nc.tensor.matmul(work[:, i * D:(i + 1) * D], xT[:, c, t * P:(t + 1) * P], wv[:, c, :],
                                                  start=c == 0, stop=c == 1)
                else:
                    for c in range(2):
                        mm = nc.tensor.matmul(work[:, :], w[:, c, CHUNK[key], :], xT[:, c, :], start=c == 0, stop=c == 1)
                mm.then_inc(work_full, 1)

            def turn_maxima(at, g, n):
                pe.wait_ge(nparts_ready, at.b * NG + g + 1)
                claim(n)
                for qc in range(TPB):
                    mm = nc.tensor.transpose(work16[0:3 * GH, qc * P:(qc + 1) * P], nparts[:, g % 2, qc, :, :].rearrange("p a h -> p (a h)"),
                                             ident16[:, :])
                mm.then_inc(work_full, 1)

            def turn_sums(at, g, n):
                pe.wait_ge(sum_copied, at.b * NG + g + 1)
                claim(n)
                for qc in range(TPB):
                    mm = nc.tensor.transpose(work[:, qc * P:(qc + 1) * P], sumT[:, (g + 1) % 2, qc * P:(qc + 1) * P], ident[:, :])
                mm.then_inc(work_full, 1)

            def pass1(at, g, u):
                if g == 0 and u == 0:
                    pe.wait_ge(stack_in[at.half], at.j * STACK + STACK)
                h = g * GH + u // 2
                pe.wait_ge(max_ready, at.b * 32 + (g * 8 + u + 1))
                for i in range(2):
                    qc = (u % 2) * 2 + i
                    mm = nc.tensor.matmul(s1[u % 2][:, i, :], qs[0:ROWS + 1, at.half, h, qc * P:(qc + 1) * P],
                                          ks[0:ROWS + 1, at.half, h, :], start=True, stop=True)
                mm.then_inc(s1_full, 1)

            def pass2(at, g, u):
                if u == 0:
                    pe.wait_ge(nmax_in[g % 2], at.b * 32 + (g // 2 * 16 + 32))
                kc, h = u // GH, g * GH + u % GH
                pe.wait_ge(exp_done, at.b * 64 + (g * 16 + u + 1))
                nc.tensor.matmul(s2[u % 2][:, :], ks[0:ROWS + 4, at.half, h, kc * P:(kc + 1) * P], qs[0:ROWS + 4, at.half, h, :],
                                 start=True, stop=True).then_inc(s2_full, 1)

            def values(at, g, kc):
                pe.wait_ge(exp_done, at.b * 64 + (g * 16 + kc * GH + GH + 2))
                if kc == 0:
                    pe.wait_ge(sum_copied, at.b * NG + g + 1)
                for i in range(GH):
                    mm = nc.tensor.matmul(sums[32 * i:32 * i + 32, :], v1[:, at.half, kc, g * GH + i, :], prob[:, (kc * GH + i) % 8, :],
                                          start=kc == 0, stop=kc == TPB - 1)
                mm.then_inc(av_done, 1)

            def prologue():
                pe.sem_inc(av_done, 2)
                pe.wait_ge(loaded, LOADED)
                pe.wait_ge(id_ready, 1)
                for n, key in enumerate(PRO + PRO[:6]):
                    event(key, At(0, n // 8), n)
                for u in range(8):
                    pass1(At(0, 0), 0, u)
                for u in range(8):
                    pass1(At(0, 0), 1, u)
                turn_maxima(At(0, 0), 0, 14)
                pe.wait_ge(work_copied, 16)
                pe.sem_inc(work_full, 2)

            def slot(at, g, left, first):
                for s in range(8):
                    if left >= 2:
                        a, h = later(at, g, 2)
                        pass1(a, h, s)
                    for u in (2 * s, 2 * s + 1):
                        pass2(at, g, u)
                    if s == 0 and not first:
                        values(*before(at, g), TPB - 1)
                    if s == 1 and not first:
                        turn_sums(at, g, ordinal(at, g, "FIN", left))
                    if s == 2 and left >= 1:
                        turn_maxima(*later(at, g, 1), ordinal(at, g, "MAX", left))
                    if s in (3, 5, 7):
                        values(at, g, (s - 3) // 2)
                    e = events(at, g, s, left)
                    if e:
                        event(*e)

            def end(at):
                values(at, NG - 1, TPB - 1)
                turn_sums(At(at.j + 1, 0), 0, LAST_EVENT)

            run(pe, prologue, slot, end)

        @block.vector
        def _(dve):
            def maximum(at, g, u):
                dve.wait_ge(s1_full, at.b * 32 + (g * 8 + u + 1))
                if u == 0:
                    dve.wait_ge(nsplit, at.b * 2 * NG + (g * 2 + 2))
                h, q = u // 2, (u % 2) * 2
                nc.vector.tensor_reduce(nmax[:, g % 2, h, q:q + 2], s1[u % 2][:, :, :], AX.X, ALU.max, negate=True).then_inc(max_ready, 1)

            def split_maxima(at, g):
                dve.wait_ge(max_ready, at.b * 32 + (g * 8 + 8 + 2))
                out = lambda a: nparts[:, g % 2, :, a, :].rearrange("p q h -> p h q")
                nc.vector.tensor_copy(out(0), nmax[:, g % 2, :, :]).then_inc(nsplit, 1)
                dve.wait_ge(nsplit, at.b * 2 * NG + (g * 2 + 5))
                nc.vector.tensor_tensor(nrest[:, :, :], nmax[:, g % 2, :, :], out(0), ALU.subtract).then_inc(nsplit, 1)
                dve.wait_ge(nsplit, at.b * 2 * NG + (g * 2 + 6))
                nc.vector.tensor_copy(out(1), nrest[:, :, :]).then_inc(nmid_ready, 1)
                dve.wait_ge(nmid_ready, at.b * NG + (g + 1))
                nc.vector.tensor_tensor(out(2), nrest[:, :, :], out(1), ALU.subtract).then_inc(nparts_ready, 1)

            def copy_maxima(at, g, n, first=False):
                if not first:
                    a, h = before(at, g)
                    dve.wait_ge(nmax_out[h % 2], a.b * 32 + (h // 2 * 16 + 16))
                dve.wait_ge(work_full, n + 1)
                nc.vector.tensor_copy(nturned[:, :], work[0:3 * GH, :].bitcast(BF16)[:, 0:T]).then_inc(work_copied, 1)

            def finish(at, g, n):
                G = at.b * NG + g
                a, h = before(at, g)
                dve.wait_ge(work_full, n + 1)
                o = work[:, :].rearrange("p (q h c) -> p q h c", q=TPB, h=GH)
                nc.vector.reciprocal(rden[:, :, :], o[:, :, :, HD:HD + 1].squeeze(3)).then_inc(rden_ready, 1)
                dve.wait_ge(rden_ready, G)
                nc.vector.tensor_tensor(part[:, :, :, :], o[:, :, :, 0:HD], rden[:, :, :].unsqueeze(3).to_broadcast([P, TPB, GH, HD]),
                                        ALU.mult).then_inc(work_copied, 1)
                dve.wait_ge(work_copied, n + 2)
                hh = H[:, bass.ds(a.b * TPB, TPB), h * GH * HD:(h + 1) * GH * HD]
                nc.vector.tensor_tensor(hh, hh, part[:, :, :, :].rearrange("p q h d -> p q (h d)"), ALU.add).then_inc(part_ready, 1)

            def event(key, at, n):
                if key[0] == "V":
                    t = 2 * int(key[1])
                    dve.wait_ge(work_full, n + 1)
                    nc.vector.tensor_tensor(v1[:, at.half, t:t + 2, :, 0:HD], work[:, :].rearrange("p (t h d) -> p t h d", t=2, d=HD),
                                            bv[:, :].rearrange("p (h d) -> p h d", d=HD).unsqueeze(1).to_broadcast([P, 2, NH, HD]),
                                            ALU.add).then_inc(work_copied, 1)
                if key in CHUNK:
                    x = CHUNK[key]
                    dve.wait_ge(work_copied, n + 2)
                    nc.vector.tensor_tensor(parts[:, x % 2, 1, :], full[:, x % 2, :], parts[:, x % 2, 0, :], ALU.subtract
                                            ).then_inc(mid_ready, 1)

            def prologue():
                norm.constants(nc)
                nc.vector.memset(v1[:, :, :, :, HD:2 * HD], 1.0).then_inc(ones_set, 1)
                nc.vector.memset(ks[ROWS:ROWS + 4, :, :, :], 1.0).then_inc(ones_set, 1)
                nc.vector.memset(qs[ROWS:ROWS + 1, :, :, :], 1.0).then_inc(ones_set, 1)
                dve.sem_inc(max_ready, 2)
                dve.sem_inc(nsplit, 4)
                dve.wait_ge(loaded, LOADED)
                nc.vector.tensor_copy(ident16[:, :], ident[:, :]).then_inc(id_ready, 1)
                dve.wait_ge(id_ready, 1)
                nc.vector.tensor_scalar(bias[:, 0:2], bias[:, 0:2], HD ** -0.5, None, ALU.mult).then_inc(id_ready, 1)
                for b in range(2):
                    norm.stats(nc, dve, H, b)
                    if b:
                        dve.wait_ge(work_full, 2)
                    norm.apply(nc, dve, H, b, lambda t: xn[:, t, :], xn_ready)
                    for n, key in enumerate(PRO if b == 0 else PRO[:6]):
                        event(key, At(0, b), b * 8 + n)
                for g in range(2):
                    for u in range(8):
                        maximum(At(0, 0), g, u)
                    split_maxima(At(0, 0), g)
                copy_maxima(At(0, 0), 0, 14, True)
                dve.wait_ge(work_copied, 16)
                dve.sem_inc(nturned_ready, 1)

            def slot(at, g, left, first):
                if g == 1 and left >= 2 * NG - g:
                    norm.stats(nc, dve, H, at.b + 2)
                for s in range(8):
                    if left >= 2:
                        a, h = later(at, g, 2)
                        maximum(a, h, s)
                    if g == 1 and s == 4 and left >= 2 * NG - g:
                        norm.apply(nc, dve, H, at.b + 2, lambda t: xn[:, t, :], xn_ready)
                    if s == 1 and not first:
                        finish(at, g, ordinal(at, g, "FIN", left))
                    if s == 2 and left >= 1:
                        a, h = later(at, g, 1)
                        copy_maxima(a, h, ordinal(at, g, "MAX", left))
                        dve.wait_ge(work_copied, ordinal(at, g, "MAX", left) + 2)
                        dve.sem_inc(nturned_ready, 1)
                    e = events(at, g, s, left)
                    if e:
                        event(*e)
                if left >= 2:
                    a, h = later(at, g, 2)
                    split_maxima(a, h)

            run(dve, prologue, slot, lambda at: finish(At(at.j + 1, 0), 0, LAST_EVENT))

        @block.scalar
        def _(act):
            def exps(at, g, u):
                act.wait_ge(s2_full, at.b * 64 + (g * 16 + u + 1))
                act.wait_ge(av_done, at.b * 16 + (g * 4 + u // GH + 1))
                nc.scalar.activation(prob[:, u % 8, :], s2[u % 2][:, :], ACT.Exp).then_inc(exp_done, 1)

            def copy_sums(at, g):
                act.wait_ge(av_done, at.b * 16 + (g * 4 + 6))
                nc.scalar.activation(sumT[:, g % 2, :], sums[:, :], ACT.Copy).then_inc(sum_copied, 1)

            def event(key, at, n):
                if key[0] == "V":
                    return
                act.wait_ge(work_full, n + 1)
                if key[0] == "X":
                    nc.scalar.activation(xT[:, int(key[1]), :], work[:, :], ACT.Copy).then_inc(work_copied, 1)
                    return
                x = CHUNK[key]
                kw = dict(bias=bias[:, x:x + 1], scale=HD ** -0.5 if x < 2 else 1.0)
                act.wait_ge(parts_out[x % 2], at.b * 32 + (x // 2 * 16 + 16))
                nc.scalar.activation(full[:, x % 2, :], work[:, :], ACT.Identity, **kw).then_inc(full_ready, 1)
                nc.scalar.activation(parts[:, x % 2, 0, :], work[:, :], ACT.Identity, **kw).then_inc(work_copied, 1)

            def prologue():
                act.sem_inc(work_copied, 1)
                act.sem_inc(exp_done, 2)
                act.sem_inc(sum_copied, 1)
                act.wait_ge(id_ready, 2)
                for n, key in enumerate(PRO + PRO[:6]):
                    event(key, At(0, n // 8), n)
                act.wait_ge(work_copied, 16)
                act.sem_inc(work_copied, 2)

            def slot(at, g, left, first):
                for s in range(8):
                    for u in (2 * s, 2 * s + 1):
                        exps(at, g, u)
                    if s == 0 and not first:
                        copy_sums(*before(at, g))
                    e = events(at, g, s, left)
                    if e:
                        event(*e)

            run(act, prologue, slot, lambda at: copy_sums(at, NG - 1))


E2, I2, CAP = 16, 128, 64
SLOT_ROWS = E2 * B * CAP


def top2_experts(nc, A, S, H, out):
    with ExitStack() as outer:
        m = Bufs(nc, outer, "t2")
        read_slot = m.sb("read_slot", [P, 2, TILES], I32)
        weight = m.sb("weight", [P, 2, TILES])
        with ExitStack() as both:
            m = Bufs(nc, both, "t2n")
            xs, lgs = m.sb("xs", [P, TILES, D]), m.sb("lgs", [P, TILES, E2])
            router_logits(nc, A, S, H, xs, lgs)
            dispatch(nc, A, S, xs, lgs, read_slot, weight)
        slot_experts(nc, A, S)
        collect(nc, S, H, read_slot, weight, out)


def router_logits(nc, A, S, H, xs, lgs):
    with ExitStack() as ctx:
        m = Bufs(nc, ctx, "rl")
        wr, ident, zeros = m.sb("wr", [P, 2, E2]), m.sb("ident", [P, P]), m.sb("zeros", [P, 2048])
        xn, xT = m.sb("xn", [P, TPB, D]), m.sb("xT", [P, 2, 2, T])
        norm = Norm(m)
        turn, lg = [m.ps(f"turn{c}", [P, T]) for c in range(2)], [m.ps(f"lg{k}", [P, T]) for k in range(2)]
        loaded, zero_set, zeroed = m.sem("loaded"), m.sem("zero_set"), m.sem("zeroed")
        xn_ready, xs_ready, x_turned, xT_ready, lg_full, lg_read = (m.sem(x) for x in (
            "xn_ready", "xs_ready", "x_turned", "xT_ready", "lg_full", "lg_read"))
        block = ctx.enter_context(nc.Block())

        @block.sync
        def _(sp):
            sp.dma_start(wr[:, :, :], A["w_router"]).then_inc(loaded, 16)
            sp.dma_start(ident[:, :], A["ident"]).then_inc(loaded, 16)
            sp.wait_ge(zero_set, 1)
            zero_rows(sp, S["slots_x"], SLOT_ROWS, zeros, zeroed)

        @block.gpsimd
        def _(pool):
            pool.wait_ge(norm.set, 2)
            with pool.Fori(0, B) as g:
                norm.power(nc, pool, g)
                for t in range(TPB):
                    pool.wait_ge(xn_ready, g * TPB + t + 1)
                    nc.gpsimd.tensor_copy(xs[:, bass.ds(g * TPB + t, 1), :].squeeze(1), xn[:, t, :]).then_inc(xs_ready, 1)

        @block.vector
        def _(dve):
            norm.constants(nc)
            nc.vector.memset(zeros[:, :], 0.0).then_inc(zero_set, 1)
            dve.sem_inc(x_turned, 2)
            dve.sem_inc(xs_ready, 1)
            with dve.Fori(0, B) as g:
                norm.stats(nc, dve, H, g)
                dve.wait_ge(x_turned, g * 2 + 2)
                dve.wait_ge(xs_ready, g * TPB + 1)
                norm.apply(nc, dve, H, g, lambda t: xn[:, t, :], xn_ready)

        @block.scalar
        def _(act):
            act.sem_inc(xT_ready, 2)
            act.sem_inc(lg_read, 2)
            with act.Fori(0, B // 2) as j:
                for k in range(2):
                    b = j * 2 + k
                    for c in range(2):
                        act.wait_ge(x_turned, b * 2 + c + 3)
                        nc.scalar.activation(xT[:, k, c, :], turn[c][:, :], ACT.Copy).then_inc(xT_ready, 1)
                    act.wait_ge(lg_full, b + 1)
                    nc.scalar.activation(lgs[:, bass.ds(b * TPB, TPB), :], lg[k][:, 0:TPB * E2].rearrange("p (t e) -> p t e", e=E2),
                                         ACT.Copy).then_inc(lg_read, 1)

        @block.tensor
        def _(pe):
            pe.wait_ge(loaded, 32)
            with pe.Fori(0, B // 2) as j:
                for k in range(2):
                    b = j * 2 + k
                    pe.wait_ge(xn_ready, b * TPB + TPB)
                    for c in range(2):
                        pe.wait_ge(xT_ready, b * 2 + c + 1)
                        for t in range(TPB):
                            mm = nc.tensor.transpose(turn[c][:, t * P:(t + 1) * P], xn[:, t, c * P:(c + 1) * P], ident[:, :])
                        mm.then_inc(x_turned, 1)
                    pe.wait_ge(xT_ready, b * 2 + 4)
                    pe.wait_ge(lg_read, b + 1)
                    for t in range(TPB):
                        for c in range(2):
                            mm = nc.tensor.matmul(lg[k][:, t * E2:(t + 1) * E2], xT[:, k, c, t * P:(t + 1) * P], wr[:, c, :],
                                                  start=c == 0, stop=c == 1)
                    mm.then_inc(lg_full, 1)


def dispatch(nc, A, S, xs, lgs, read_slot, weight):
    FAR = float(2 * SLOT_ROWS)
    with ExitStack() as ctx:
        m = Bufs(nc, ctx, "dp")
        iota, base = m.sb("iota", [P, P]), m.sb("base", [P, TILES])
        strict_f, strict, ones = m.sb("strict_f", [P, P]), m.sb("strict", [P, P], BF16), m.sb("ones", [P, P], BF16)
        big, probs = m.sb("big", [P, TILES]), m.sb("probs", [P, TILES, E2])
        top, top_i = m.sb("top", [P, TILES, 8]), m.sb("top_i", [P, TILES, 8], U32)
        idx, hot = m.sb("idx", [P, 2, TILES]), m.sb("hot", [P, 2, TILES, E2], BF16)
        tot, run, flag = (m.sb(x, [P, B, E2, 2 * TPB]) for x in ("tot", "run", "flag"))
        place, pos, over = m.sb("place", [P, TILES, E2]), m.sb("pos", [P, 2, TILES]), m.sb("over", [P, 2, TILES])
        row, write_slot = m.sb("row", [P, 2, TILES]), m.sb("write_slot", [P, 2, TILES], I32)
        pre = [m.ps(f"pre{g}", [P, 512]) for g in range(4)]
        sums = [m.ps(f"sums{g}", [P, 512]) for g in range(4)]
        loaded, step, counted, exp_done, slots_ready, scattered = (m.sem(x) for x in (
            "loaded", "step", "counted", "exp_done", "slots_ready", "scattered"))
        block = ctx.enter_context(nc.Block())
        bc = lambda x: x.unsqueeze(2).to_broadcast([P, TILES, E2])
        HOT_STEP = 2 + 2 * TILES + 5 + 3

        @block.sync
        def _(sp):
            for dst, name in ((iota, "iota128"), (base, "batch_row"), (strict_f, "strict")):
                sp.dma_start(dst[:, :], A[name]).then_inc(loaded, 16)

        @block.scalar
        def _(act):
            act.wait_ge(step, 2)
            nc.scalar.activation(probs[:, :, :], probs[:, :, :], ACT.Exp).then_inc(exp_done, 1)

        @block.tensor
        def _(pe):
            pe.wait_ge(step, HOT_STEP)
            for c in range(2):
                for g in range(2):
                    r = hot[:, c, g * 32:(g + 1) * 32, :].rearrange("p t e -> p (t e)")
                    nc.tensor.matmul(pre[2 * c + g][:, :], strict[:, :], r, start=True, stop=True).then_inc(counted, 1)
                    nc.tensor.matmul(sums[2 * c + g][:, :], ones[:, :], r, start=True, stop=True).then_inc(counted, 1)

        @block.vector
        def _(dve):
            n = [0]

            def link(ins, wait=True):
                n[0] += 1
                ins.then_inc(step, 1)
                if wait:
                    dve.wait_ge(step, n[0])

            link(nc.vector.tensor_reduce(big[:, :], lgs[:, :, :], AX.X, ALU.max))
            link(nc.vector.tensor_tensor(probs[:, :, :], lgs[:, :, :], bc(big[:, :]), ALU.subtract))
            dve.wait_ge(exp_done, 1)
            link(nc.vector.tensor_reduce(big[:, :], probs[:, :, :], AX.X, ALU.add))
            link(nc.vector.reciprocal(big[:, :], big[:, :]))
            link(nc.vector.tensor_tensor(probs[:, :, :], probs[:, :, :], bc(big[:, :]), ALU.mult))
            for t in range(TILES):
                link(nc.vector.max(top[:, t, :], probs[:, t, :]), wait=t == TILES - 1)
            for t in range(TILES):
                link(nc.vector.max_index(top_i[:, t, :], top[:, t, :], probs[:, t, :]), wait=t == TILES - 1)
            dve.wait_ge(loaded, 48)
            link(nc.vector.tensor_copy(strict[:, :], strict_f[:, :]))
            link(nc.vector.memset(ones[:, :], 1.0))
            link(nc.vector.tensor_copy(idx[:, :, :], top_i[:, :, 0:2].rearrange("p t c -> p c t")))
            for c in range(2):
                link(nc.vector.tensor_tensor(hot[:, c, :, :], iota[:, 0:E2].unsqueeze(1).to_broadcast([P, TILES, E2]),
                                             bc(idx[:, c, :]), ALU.is_equal))
            assert n[0] == HOT_STEP
            link(nc.vector.tensor_copy(weight[:, :, :], top[:, :, 0:2].rearrange("p t c -> p c t")))
            link(nc.vector.memset(flag[:, :, :, :], 1.0))
            link(nc.vector.memset(flag[:, :, :, 0:1], 0.0))
            dve.wait_ge(counted, 8)
            for c in range(2):
                for g in range(2):
                    link(nc.vector.tensor_copy(tot[:, 8 * g:8 * g + 8, :, c * TPB:(c + 1) * TPB],
                                               sums[2 * c + g][:, :].rearrange("p (b q e) -> p b e q", q=TPB, e=E2)))
            flat = lambda x: x[:, :, :, :].rearrange("p b e q -> p (b e q)")
            link(nc.vector.tensor_tensor_scan(flat(run), flat(flag), flat(tot), 0.0, ALU.mult, ALU.add))
            link(nc.vector.tensor_tensor(flat(run), flat(run), flat(tot), ALU.subtract))
            for c in range(2):
                for g in range(2):
                    link(nc.vector.tensor_tensor(place[:, 32 * g:32 * g + 32, :].rearrange("p (b q) e -> p b q e", q=TPB),
                                                 pre[2 * c + g][:, :].rearrange("p (b q e) -> p b q e", q=TPB, e=E2),
                                                 run[:, 8 * g:8 * g + 8, :, c * TPB:(c + 1) * TPB].rearrange("p b e q -> p b q e"), ALU.add))
                link(nc.vector.tensor_tensor(place[:, :, :], place[:, :, :], hot[:, c, :, :], ALU.mult))
                link(nc.vector.tensor_reduce(pos[:, c, :], place[:, :, :], AX.X, ALU.add))
                link(nc.vector.tensor_scalar(row[:, c, :], idx[:, c, :], float(B * CAP), None, ALU.mult))
                link(nc.vector.tensor_tensor(row[:, c, :], row[:, c, :], base[:, :], ALU.add))
            link(nc.vector.tensor_scalar(over[:, :, :], pos[:, :, :], float(CAP), FAR, ALU.is_ge, ALU.mult))
            link(nc.vector.tensor_scalar(pos[:, :, :], pos[:, :, :], float(CAP - 1), None, ALU.min))
            link(nc.vector.tensor_tensor(row[:, :, :], row[:, :, :], pos[:, :, :], ALU.add))
            link(nc.vector.tensor_copy(read_slot[:, :, :], row[:, :, :]))
            link(nc.vector.tensor_tensor(row[:, :, :], row[:, :, :], over[:, :, :], ALU.add))
            nc.vector.tensor_copy(write_slot[:, :, :], row[:, :, :]).then_inc(slots_ready, 1)

        @block.gpsimd
        def _(pool):
            pool.wait_ge(slots_ready, 1)
            for t in range(TILES):
                for c in range(2):
                    nc.gpsimd.indirect_dma_start(S["slots_x"], bass.IndirectOffsetOnAxis(ap=write_slot[:, c, t:t + 1], axis=0),
                                                 xs[:, t, :], None, bounds_check=SLOT_ROWS - 1, oob_is_err=False).then_inc(scattered, 16)
            pool.wait_ge(scattered, 32 * TILES)


def slot_experts(nc, A, S):
    N = SLOT_ROWS // P
    with ExitStack() as ctx:
        m = Bufs(nc, ctx, "se")
        wgu, wd = m.sb("wgu", [P, E2, 2, 2 * I2]), m.sb("wd", [P, E2, D])
        ident, xt, o = m.sb("ident", [P, P]), m.sb("xt", [P, 4, D]), m.sb("o", [P, 4, D])
        loaded = m.sem("loaded")
        x_in, o_out = [m.sem(f"x_in{k}") for k in range(4)], [m.sem(f"o_out{k}") for k in range(4)]
        xv = S["slots_x"].rearrange("(n p) d -> n p d", p=P)
        yv = S["slots_y"].rearrange("(n p) d -> n p d", p=P)

        def turn_ready(pe, n, q, i):
            pe.wait_ge(loaded, 48)
            pe.wait_ge(x_in[q % 4], (i * 2 + q // 4) * 16 + 16)

        def finish(dve, n, k, q, i, left, s, pD):
            dve.wait_ge(s["down_full"], n + 2)
            dve.wait_ge(o_out[q % 4], (i * 2 + q // 4) * 16 + 16)
            nc.vector.tensor_copy(o[:, q % 4, :], pD[k][:, 0:D]).then_inc(s["down_read"], 1)

        def sync_prog(sp, s, steps):
            sp.dma_start(ident[:, :], A["ident"]).then_inc(loaded, 16)
            for k in range(4):
                sp.dma_start(xt[:, k, :], xv[k]).then_inc(x_in[k], 16)
                sp.sem_inc(o_out[k], 16)
            sp.dma_start(wgu[:, :, :, :], A["ex_gu"]).then_inc(loaded, 16)
            sp.dma_start(wd[:, :, :], A["ex_down"]).then_inc(loaded, 16)

            def step(n, k, q, i, left):
                if left >= 4:
                    sp.wait_ge(s["x_turned"], n + 5)
                    sp.dma_start(xt[:, q % 4, :], xv[bass.ds(n + 4, 1)].squeeze(0)).then_inc(x_in[q % 4], 16)
                sp.wait_ge(s["down_read"], n + 3)
                sp.dma_start(yv[bass.ds(n, 1)].squeeze(0), o[:, q % 4, :]).then_inc(o_out[q % 4], 16)

            steps(sp, step)
            for k in range(4):
                sp.wait_ge(o_out[k], 16 * (N // 4) + 16)

        def mul_ready(pe, n, i):
            w = lambda a: (lambda c: wgu[:, bass.ds(i, 1), c, a:a + I2].squeeze(1))
            return w(0), w(I2)

        none = lambda *a: None
        expert_stream(nc, m, N, I2, 8, turn_ready=turn_ready, x_of=lambda n, q, c: xt[:, q % 4, c * P:(c + 1) * P],
                      mul_ready=mul_ready, down_of=lambda pe, n, i: (lambda c: wd[:, bass.ds(i, 1), :].squeeze(1)),
                      mul_also=none, identT=ident, dve_more=none, act_first=none, act_more=none, pool_prog=None,
                      sync_prog=sync_prog, finish=finish, prologue_dve=none, dve_before=none)


def collect(nc, S, H, read_slot, weight, out):
    R = 4
    with ExitStack() as ctx:
        m = Bufs(nc, ctx, "co")
        g = m.sb("g", [P, R, 2, D])
        got, summed, stored = [m.sem(f"got{r}") for r in range(R)], m.sem("summed"), m.sem("stored")
        block = ctx.enter_context(nc.Block())
        ov = out.rearrange("b (q p) d -> (b q) p d", p=P)

        @block.gpsimd
        def _(pool):
            for t in range(TILES):
                if t >= R:
                    pool.wait_ge(summed, 2 * (t - R + 1))
                for c in range(2):
                    nc.gpsimd.indirect_dma_start(g[:, t % R, c, :], None, S["slots_y"],
                                                 bass.IndirectOffsetOnAxis(ap=read_slot[:, c, t:t + 1], axis=0)).then_inc(got[t % R], 16)

        @block.vector
        def _(dve):
            for t in range(TILES):
                dve.wait_ge(got[t % R], 32 * (t // R + 1))
                for c in range(2):
                    if c:
                        dve.wait_ge(summed, 2 * t + 1)
                    nc.vector.scalar_tensor_tensor(out=H[:, t, :], in0=g[:, t % R, c, :], scalar=weight[:, c, t:t + 1],
                                                   in1=H[:, t, :], op0=ALU.mult, op1=ALU.add).then_inc(summed, 1)

        @block.sync
        def _(sp):
            for t in range(TILES):
                sp.wait_ge(summed, 2 * t + 2)
                sp.dma_start(ov[t], H[:, t, :]).then_inc(stored, 16)
            sp.wait_ge(stored, 16 * TILES)


SCRATCH = [("frames", [B * FRAMES, D_STFT], F32), ("sorted_x", [SORT_TILES * P, D], F32), ("sorted_y", [SORT_TILES * P, D], F32),
           ("slots_x", [SLOT_ROWS, D], F32), ("slots_y", [SLOT_ROWS, D], F32),
           ("route", [B * NH, T], F32), ("mask", [B * NH, T], BF16),
           ("parts", [2, 2, 3, D, T], BF16), ("maxima", [2, 12, T], BF16)]


def build(nc, A, out):
    S = {name: nc.dram_tensor(f"scratch_{name}", shape, dt).ap() for name, shape, dt in SCRATCH}
    with nc.sbuf_tensor("hidden", [P, TILES, D], F32) as H:
        embed_tokens(nc, A, S, H)
        diff_attention(nc, A, S, H)
        top1_experts(nc, A, S, H)
        sparse_attention(nc, A, S, H)
        top2_experts(nc, A, S, H, out)


def shape_constants():
    import numpy as np

    n = np.arange(NFFT)[:, None] * np.arange(FREQS)[None, :] * (2 * np.pi / NFFT)
    dft = np.concatenate([np.cos(n), -np.sin(n)], 1).astype(np.float32)
    coord = np.clip((np.arange(T) + np.float32(0.5)) * (FRAMES / T) - 0.5, 0, FRAMES - 1).astype(np.float32)
    i0 = np.floor(coord).astype(np.int32)
    i1 = np.minimum(i0 + 1, FRAMES - 1)
    w = coord - i0
    interp = np.zeros((FRAMES + 1, T), np.float32)
    interp[i0, np.arange(T)] += 1 - w
    interp[i1, np.arange(T)] += w
    interp[FRAMES] = 1
    hd = 16
    inv = 1.0 / 10000.0 ** (np.arange(0, hd, 2, dtype=np.float32) / np.float32(hd))
    fr = np.outer(np.arange(T, dtype=np.float32), inv.astype(np.float32)).astype(np.float32)
    c, s = np.cos(fr), np.sin(fr)
    rot = np.stack([np.concatenate([c, c], 1), np.concatenate([s, -s], 1)], 0).astype(np.float32)
    rot = rot.reshape(2, TPB, P, hd).transpose(2, 0, 1, 3)
    k = np.arange(P)
    return {
        "dft": dft, "interp": interp, "rot": rot,
        "iota_v": np.tile(np.arange(V, dtype=np.float32), (P, 1)),
        "iota128": np.tile(np.arange(P, dtype=np.float32), (P, 1)),
        "k128": np.tile(np.arange(P, dtype=np.float32) * P, (P, 1)),
        "batch_row": np.tile((np.arange(TILES) // TPB * CAP).astype(np.float32), (P, 1)),
        "part_id": k.astype(np.float32)[:, None],
        "ident": np.eye(P, dtype=np.float32),
        "upper": (k[:, None] <= k[None, :]).astype(np.float32),
        "strict": (k[:, None] < k[None, :]).astype(np.float32),
        "ones": np.ones((P, P), np.float32),
    }
def layout(inputs):
    import numpy as np

    x = {k: np.asarray(v) for k, v in inputs.items()}
    L = shape_constants()
    ids = x["x"].astype(np.int32, copy=False)
    half = NFFT // 2
    padded = np.pad(ids, ((0, 0), (half, half)), mode="reflect")
    L["ids"] = ids
    L["frame_ids"] = padded.reshape(B * FRAMES, NFFT).T
    L["window"] = x["L0_tok_window"][:, None]
    L["tok_proj_w"] = x["L0_tok_proj_w"].reshape(D_STFT, FREQS, V).transpose(2, 1, 0)
    L["proj_b"] = x["L0_tok_proj_b"][None, :]
    L["emb"] = x["L0_tok_emb_table"]
    order = np.concatenate([np.arange(8), 8 + (np.arange(8) + 4) % 8])
    heads = lambda w: w.reshape(16, 16, D)[order].reshape(D, D).T
    rows = lambda w: w.reshape(2, P, -1).transpose(1, 0, 2)
    L["wqk"] = rows(np.concatenate([heads(x["L0_attn_Wq"]), heads(x["L0_attn_Wk"])], 1))
    L["wv"], L["wo"] = rows(x["L0_attn_Wv"].T), rows(x["L0_attn_Wproj"].T)
    L["lambdas"] = np.stack([x["L0_attn_lambda_q1"], x["L0_attn_lambda_k1"], x["L0_attn_lambda_q2"],
                             x["L0_attn_lambda_k2"]]).reshape(2, 2, 8)
    L["gate_w"], L["sh_gate"] = rows(x["L0_ffn_gate_w"]), rows(x["L0_ffn_shared_gate_w"])
    L["sh_up"], L["sh_down"] = rows(x["L0_ffn_shared_up_w"]), x["L0_ffn_shared_down_w"].reshape(4, P, D).transpose(1, 0, 2)
    gu = np.concatenate([x["L0_ffn_routed_gate_w"], x["L0_ffn_routed_up_w"]], 2)
    L["ro_gu"] = gu.reshape(32, 2, P, 1024).transpose(0, 2, 1, 3)
    L["ro_down"] = x["L0_ffn_routed_down_w"].reshape(32, 4, P, D).transpose(0, 2, 1, 3)
    L["r_w1"], L["r_w2"] = rows(x["L1_attn_r_w1"].T), np.pad(x["L1_attn_r_w2"].T, ((0, 0), (0, P - 16)))
    L["r_b1"], L["r_b2"] = x["L1_attn_r_b1"][:, None], x["L1_attn_r_b2"][:, None]
    w, bias = x["L1_attn_qkv_w"], x["L1_attn_qkv_b"]
    L["l1_wqk"] = w[0:2 * D].T.reshape(2, P, 4, P).transpose(1, 0, 2, 3)
    L["l1_wv"], L["l1_bv"] = rows(w[2 * D:].T), bias[None, 2 * D:]
    L["l1_bias"] = bias[0:2 * D].reshape(4, P).T
    L["w_router"] = rows(x["L1_ffn_w_router"])
    gu = np.concatenate([x["L1_ffn_w_gate"], x["L1_ffn_w_fc"]], 2)
    L["ex_gu"] = gu.reshape(16, 2, P, 256).transpose(2, 0, 1, 3)
    L["ex_down"] = x["L1_ffn_w_proj"].transpose(1, 0, 2)
    return {k: np.ascontiguousarray(v) for k, v in L.items()}


def kernel(**inputs):
    import numpy as _np
    import concourse.bacc as _bacc
    from concourse import mybir as _mybir
    from concourse.bass_utils import run_bass_kernel_spmd as _run

    nc = _bacc.Bacc("TRN2", target_bir_lowering=False, num_devices=1)
    arrays, args = {}, {}
    for name, a in layout(inputs).items():
        arrays[f"in_{name}_dram"] = a
        args[name] = nc.dram_tensor(f"in_{name}_dram", a.shape, _mybir.dt.from_np(a.dtype), kind="ExternalInput").ap()
    out = nc.dram_tensor("out_0_dram", (B, T, D), _mybir.dt.float32, kind="ExternalOutput").ap()
    build(nc, args, out)
    r = _run(nc, [arrays], core_ids=[0])
    return r.results[0]["out_0_dram"]
```

```python
from contextlib import ExitStack

import numpy as np

import concourse.bass as bass
from concourse import mybir

ALU = mybir.AluOpType
ACT = mybir.ActivationFunctionType
AX = mybir.AxisListType
F32 = mybir.dt.float32
BF16 = mybir.dt.bfloat16
I32 = mybir.dt.int32
U32 = mybir.dt.uint32

P = 128
B, T, D = 16, 512, 256
V, D_EMB = 64, 179
D_STFT = D - D_EMB
FRAMES, FREQS, NFFT = 9, 33, 64
TILES = B * T // P
TPB = T // P
LN_EPS = 1e-5
RMS_EPS = float(np.finfo(np.float32).eps)
LAMBDA_INIT = 0.8 - 0.6 * float(np.exp(-0.3 * 1))

class Bufs:

    def __init__(self, nc, ctx, stage):
        self.nc, self.ctx, self.stage, self.sems = nc, ctx, stage, []
        ctx.callback(self.clear)

    def clear(self):
        if self.sems:
            self.nc.clear_and_free_semaphores(self.sems)
            self.nc.all_engine_barrier()

    def sb(self, name, shape, dt=F32):
        return self.ctx.enter_context(self.nc.sbuf_tensor(f"{self.stage}_{name}", shape, dt))

    def ps(self, name, shape, dt=F32):
        return self.ctx.enter_context(self.nc.psum_tensor(f"{self.stage}_{name}", shape, dt))

    def sem(self, name):
        self.sems.append(self.nc.alloc_semaphore(f"{self.stage}_{name}"))
        return self.sems[-1]

def embed_tokens(nc, A, S, H):
    NBT = B * FRAMES
    HALF = NBT // 2
    PER = 7
    GROUPS = -(-NBT // PER)
    C2 = 2 * FREQS
    with ExitStack() as ctx:
        m = Bufs(nc, ctx, "tok")
        frame_ids = m.sb("frame_ids", [NFFT, NBT], I32)
        frame_idf = m.sb("frame_idf", [NFFT, NBT])
        iota_v = m.sb("iota_v", [NFFT, V])
        part_id = m.sb("part_id", [V, 1])
        window = m.sb("window", [NFFT, 1])
        dft = m.sb("dft", [NFFT, C2])
        wdft = m.sb("wdft", [NFFT, C2])
        frames = m.sb("frames", [NFFT, NBT, V])
        squares = m.sb("squares", [V, 2, PER, C2])
        mag = m.sb("mag", [V, FREQS, NBT])
        proj_w = m.sb("proj_w", [V, FREQS, D_STFT])
        emb = m.sb("emb", [V, D_EMB])
        pf = m.sb("pf", [HALF, 2, D_STFT])
        pfb = m.sb("pfb", [FRAMES + 1, B, D_STFT])
        interp = m.sb("interp", [FRAMES + 1, T])
        ids_row = m.sb("ids_row", [V, 2, T], I32)
        onehot = m.sb("onehot", [V, 2, T])
        spec = m.ps("spec", [V, 2, 512])
        pproj = m.ps("pproj", [HALF, 2, 512])
        tok = m.ps("tok", [P, 4, 512])
        consts_in, weights_in, bias_in, interp_in = m.sem("consts_in"), m.sem("weights_in"), m.sem("bias_in"), m.sem("interp_in")
        idf_ready, wdft_ready, frames_ready = m.sem("idf_ready"), m.sem("wdft_ready"), m.sem("frames_ready")
        spec_ready, squares_ready, power_ready, mag_ready = m.sem("spec_ready"), m.sem("squares_ready"), m.sem("power_ready"), m.sem("mag_ready")
        proj_ready, pf_ready, pf_out, pf_back = m.sem("proj_ready"), m.sem("pf_ready"), m.sem("pf_out"), m.sem("pf_back")
        ids_in = [m.sem(f"ids_in{k}") for k in range(2)]
        onehot_ready, tok_ready, tok_copied = m.sem("onehot_ready"), m.sem("tok_ready"), m.sem("tok_copied")
        block = ctx.enter_context(nc.Block())
        PAIRS = B // 2

        @block.sync
        def _(sp):
            sp.dma_start(frame_ids[:, :], A["frame_ids"][:, :]).then_inc(consts_in, 16)
            sp.dma_start(iota_v[:, :], A["iota_v"][0:NFFT, :]).then_inc(consts_in, 16)
            sp.dma_start(window[:, :], A["window"][:, :]).then_inc(consts_in, 16)
            sp.dma_start(dft[:, :], A["dft"][:, :]).then_inc(consts_in, 16)
            sp.dma_start(part_id[:, :], A["part_id"][0:V, :]).then_inc(consts_in, 16)
            sp.dma_start(proj_w[:, :, :], A["tok_proj_w"][:, :, :]).then_inc(weights_in, 16)
            sp.dma_start(emb[:, :], A["emb"][:, :]).then_inc(weights_in, 16)
            sp.dma_start(interp[:, :], A["interp"][:, :]).then_inc(interp_in, 16)
            for b in range(B):
                sp.dma_start(pfb[FRAMES:FRAMES + 1, b, :], A["proj_b"][:, :]).then_inc(bias_in, 16)
            sp.wait_ge(pf_ready, 2)
            sp.dma_start(S["frames"].rearrange("(g p) j -> p g j", g=2), pf[:, :, :]).then_inc(pf_out, 16)
            sp.wait_ge(pf_out, 16)
            sp.dma_start(pfb[0:FRAMES, :, :], S["frames"].rearrange("(b t) j -> t b j", t=FRAMES)).then_inc(pf_back, 16)
            with sp.Fori(0, PAIRS) as j:
                for k in range(2):
                    sp.wait_ge(onehot_ready, j * 2 + k + 1)
                    sp.dma_start(ids_row[:, k, :], A["ids"][bass.ds(j * 2 + k, 1), :].to_broadcast([V, T])
                                 ).then_inc(ids_in[k], 16)

        @block.vector
        def _(dve):
            dve.wait_ge(consts_in, 80)
            nc.vector.tensor_copy(frame_idf[:, :], frame_ids[:, :]).then_inc(idf_ready, 1)
            nc.vector.tensor_scalar(wdft[:, :], dft[:, :], window[:, 0:1], None, ALU.mult).then_inc(wdft_ready, 1)
            dve.wait_ge(idf_ready, 1)
            nc.vector.tensor_tensor(frames[:, :, :],
                                    frame_idf[:, :].unsqueeze(2).to_broadcast([NFFT, NBT, V]),
                                    iota_v[:, :].unsqueeze(1).to_broadcast([NFFT, NBT, V]),
                                    ALU.is_equal).then_inc(frames_ready, 1)
            for g in range(GROUPS):
                n = min(PER, NBT - g * PER)
                dve.wait_ge(squares_ready, g + 1)
                sq = squares[:, g % 2, 0:n, :]
                nc.vector.tensor_tensor(mag[:, :, g * PER:g * PER + n], sq[:, :, 0:FREQS].rearrange("v n f -> v f n"),
                                        sq[:, :, FREQS:C2].rearrange("v n f -> v f n"), ALU.add).then_inc(power_ready, 1)
            for h in range(2):
                dve.wait_ge(proj_ready, h + 1)
                nc.vector.tensor_copy(pf[:, h, :], pproj[:, h, 0:D_STFT]).then_inc(pf_ready, 1)
            nc.vector.sem_inc(onehot_ready, 2)
            with dve.Fori(0, PAIRS) as j:
                for k in range(2):
                    dve.wait_ge(ids_in[k], j * 16 + 16)
                    dve.wait_ge(tok_ready, j * 8 + k * 4 + 4)
                    nc.vector.tensor_scalar(onehot[:, k, :], ids_row[:, k, :], part_id[:, 0:1], None, ALU.is_equal
                                            ).then_inc(onehot_ready, 1)

        @block.scalar
        def _(act):
            for g in range(GROUPS):
                n = min(PER, NBT - g * PER)
                act.wait_ge(spec_ready, g + 1)
                if g >= 2:
                    act.wait_ge(power_ready, g - 1)
                nc.scalar.activation(squares[:, g % 2, 0:n, :],
                                     spec[:, g % 2, 0:n * C2].rearrange("v (n f) -> v n f", n=n), ACT.Square
                                     ).then_inc(squares_ready, 1)
            act.wait_ge(power_ready, GROUPS)
            nc.scalar.activation(mag[:, :, :], mag[:, :, :], ACT.Sqrt).then_inc(mag_ready, 1)
            with act.Fori(0, PAIRS) as j:
                for k in range(2):
                    for q in range(TPB):
                        act.wait_ge(tok_ready, j * 8 + k * 4 + q + 9)
                        nc.scalar.activation(H[:, bass.ds(j * 8 + k * 4 + q, 1), :], tok[:, q, 0:D].unsqueeze(1), ACT.Copy
                                             ).then_inc(tok_copied, 1)

        @block.tensor
        def _(pe):
            pe.sem_inc(tok_ready, 8)
            pe.wait_ge(frames_ready, 1)
            pe.wait_ge(wdft_ready, 1)
            for g in range(GROUPS):
                n = min(PER, NBT - g * PER)
                if g >= 2:
                    pe.wait_ge(squares_ready, g - 1)
                for i in range(n):
                    mm = nc.tensor.matmul(spec[:, g % 2, i * C2:(i + 1) * C2], frames[:, g * PER + i, :], wdft[:, :],
                                          start=True, stop=True)
                mm.then_inc(spec_ready, 1)
            pe.wait_ge(mag_ready, 1)
            pe.wait_ge(weights_in, 32)
            for h in range(2):
                for f in range(FREQS):
                    mm = nc.tensor.matmul(pproj[:, h, 0:D_STFT], mag[:, f, h * HALF:(h + 1) * HALF], proj_w[:, f, :],
                                          start=f == 0, stop=f == FREQS - 1)
                mm.then_inc(proj_ready, 1)
            pe.wait_ge(bias_in, 16 * B)
            pe.wait_ge(interp_in, 16)
            pe.wait_ge(pf_back, 16)
            pe.sem_inc(tok_copied, 4)
            with pe.Fori(0, PAIRS) as j:
                for k in range(2):
                    pe.wait_ge(onehot_ready, j * 2 + k + 3)
                    for q in range(TPB):
                        pe.wait_ge(tok_copied, j * 8 + k * 4 + q + 1)
                        nc.tensor.matmul(tok[:, q, 0:D_EMB], onehot[:, k, q * P:(q + 1) * P], emb[:, :],
                                         start=True, stop=True)
                        nc.tensor.matmul(tok[:, q, D_EMB:D], interp[:, q * P:(q + 1) * P],
                                         pfb[:, bass.ds(j * 2 + k, 1), :].squeeze(1),
                                         start=True, stop=True).then_inc(tok_ready, 1)

NH, HD = 16, 16
NG = 4
MANY = 99
DROP = -1e30
Q_PARTS, K_PARTS = (0, 0, 0, 1, 1, 2), (0, 1, 2, 0, 1, 0)
ROWS = len(Q_PARTS) * HD

class At:

    def __init__(self, j, half):
        self.j, self.half, self.b = j, half, j * 2 + half

    def next(self, n):
        h = self.half + n
        return At(self.j + h // 2, h % 2) if h >= 2 else At(self.j, h)

def first_batch(at):
    return isinstance(at.j, int) and at.j == at.half == 0

def later(at, g, n):
    return at.next((g + n) // NG) if g + n >= NG else at, (g + n) % NG

def before(at, g):
    if g:
        return at, g - 1
    return (At(at.j, 0) if at.half else At(at.j - 1, 1)), NG - 1

def run_pairs(eng, slot):
    def pair(j, first, last):
        for half in range(2):
            for g in range(NG):
                left = (1 - half) * NG + NG - 1 - g
                slot(At(j, half), g, left if last else MANY, first and half == 0 and g == 0)

    pair(0, True, False)
    with eng.Fori(1, B // 2 - 1) as j:
        pair(j, False, False)
    pair(B // 2 - 1, False, True)

def diff_attention(nc, A, S, H):
    NPAIR, VD, GH = 8, 2 * HD, 4
    STACK = 12 * 16
    STEPS = {(0, 1): ("V0",), (0, 2): ("V1",), (0, 3): ("OUT0", "OUT1"), (1, 3): ("F0",), (2, 0): ("F1",),
             (2, 1): ("F2",), (2, 2): ("F3",), (3, 0): ("X0", "X1"), (3, 1): ("QK0",), (3, 2): ("QK1",), (3, 3): ("QK2", "QK3")}
    AHEAD = {"V": 1, "F": 1, "X": 2, "Q": 2, "O": -1}
    PRO = ["X0", "X1", "QK0", "QK1", "QK2", "QK3", "V0", "V1", "F0", "F1", "F2", "F3"]
    keys = [key for at in sorted(STEPS) for key in STEPS[at]]
    EVENTS = len(keys)
    START = len(PRO) + 6
    with ExitStack() as ctx:
        m = Bufs(nc, ctx, "dif")
        wqk, wv, wo = m.sb("wqk", [P, 2, 2 * D]), m.sb("wv", [P, 2, D]), m.sb("wo", [P, 2, D])
        ident, upper, rot = m.sb("ident", [P, P]), m.sb("upper", [P, P]), m.sb("rot", [P, 2, TPB, HD])
        ident16, after16, ones = m.sb("ident16", [P, P], BF16), m.sb("after16", [P, P], BF16), m.sb("ones", [P, VD])
        lam_in, lam_prod, lam = m.sb("lam_in", [P, 2, 2, 8]), m.sb("lam_prod", [P, 2, 8]), m.sb("lam", [P, 4])
        rms_eps, half_neg = m.sb("rms_eps", [P, 32]), m.sb("rms_half_neg", [P, 32])
        xT = m.sb("xT", [P, 2, T])
        qk, sq = m.sb("qk", [P, TPB, 2 * D]), m.sb("sq", [P, TPB, 2 * D])
        ss, rr = m.sb("ss", [P, TPB * 32]), m.sb("rr", [P, TPB * 32])
        rest, parts = m.sb("rest", [P, 2, T]), m.sb("parts", [P, 2, 3, T], BF16)
        qs, ks = m.sb("qs", [ROWS, 2, NH, T], BF16), m.sb("ks", [ROWS, 2, NH, T], BF16)
        v = m.sb("v", [P, 2, TPB, D])
        prob = m.sb("prob", [P, 8, T])
        rden, yh, yT = m.sb("rden", [P, T]), m.sb("yh", [P, 2, T]), m.sb("yT", [P, 2, T])
        norm = Norm(m)
        score, work = [m.ps(f"score{i}", [P, T]) for i in range(2)], [m.ps(f"work{i}", [P, T]) for i in range(2)]
        o, den = [m.ps(f"o{i}", [P, T]) for i in range(2)], [m.ps(f"den{i}", [P, T]) for i in range(2)]
        names = ("loaded", "set", "lam_step", "xn_ready", "work_full", "high_ready", "mid_ready", "low_ready", "qk_copied", "ss_ready",
                 "ms_ready", "rms_ready", "rot_step", "qk_ready", "score_full", "exp_done", "av_done", "rden_ready", "yh_ready",
                 "y_ready", "passed")
        (loaded, set_, lam_step, xn_ready, work_full, high_ready, mid_ready, low_ready, qk_copied, ss_ready, ms_ready, rms_ready,
         rot_step, qk_ready, score_full, exp_done, av_done, rden_ready, yh_ready, y_ready, passed) = (m.sem(x) for x in names)
        work_copied, parts_out, stack_in = ([m.sem(f"{x}{k}") for k in range(2)] for x in ("work_copied", "parts_out", "stack_in"))
        block = ctx.enter_context(nc.Block())
        LOADED = 16 * 7
        xn = lambda t: sq[:, t, 0:D]

        present = [(half, key) for half in range(2) for key in keys if AHEAD[key[0]] + half < 2]

        def number(at, key, left):
            if left == MANY:
                return at.b * (EVENTS // 2), START + keys.index(key)
            return (B - 2) * (EVENTS // 2), START + present.index((at.half, key))

        def events(at, g, s, left):
            out = []
            for key in STEPS.get((g, s), ()):
                ahead = AHEAD[key[0]]
                if ahead < 0 and first_batch(at) or left < NG * ahead - g:
                    continue
                out.append((key, at.next(ahead) if ahead > 0 else before(at, 0)[0], number(at, key, left)))
            return out

        LAST = [(f"OUT{x}", At(B // 2 - 1, 1), ((B - 2) * (EVENTS // 2), START + len(present) + x)) for x in range(2)]

        def prologue_events(b):
            return [(key, At(0, b), (0, b * len(PRO) + n)) for n, key in enumerate(PRO[:6] if b else PRO)]

        full_at = lambda n: n[0] * 2 + (n[1] + 1)
        claim_at = lambda n: n[0] + (n[1] // 2 + 1)
        copied_at = lambda n: n[0] + (n[1] // 2 + 2)

        @block.sync
        def _(sp):
            for dst, src in ((wqk[:, :, :], A["wqk"]), (wv[:, :, :], A["wv"]), (wo[:, :, :], A["wo"]), (ident[:, :], A["ident"]),
                             (upper[:, :], A["upper"]), (rot[:, :, :, :], A["rot"])):
                sp.dma_start(dst, src).then_inc(loaded, 16)
            sp.dma_start(lam_in[:, :, :, :], A["lambdas"].partition_broadcast(P)).then_inc(loaded, 16)
            for k in range(2):
                sp.sem_inc(parts_out[k], 16)

            def put_parts(at, x):
                sp.wait_ge(low_ready, at.b * 4 + (x + 1))
                sp.dma_start(S["parts"][at.half, x // 2, :, (x % 2) * P:(x % 2) * P + P, :].rearrange("a p t -> p a t"),
                             parts[:, x % 2, :, :]).then_inc(parts_out[x % 2], 16)

            def get_stacks(at):
                for k in range(2):
                    sp.wait_ge(parts_out[k], at.b * 32 + 48)
                    sp.sem_inc(passed, 1)
                for i, (stack, order) in enumerate(((qs, Q_PARTS), (ks, K_PARTS))):
                    for r, a in enumerate(order):
                        sp.dma_start(stack[r * HD:(r + 1) * HD, at.half, :, :],
                                     S["parts"][at.half, i, a].rearrange("(h d) t -> d h t", d=HD)).then_inc(stack_in[at.half], 16)

            for x in range(4):
                put_parts(At(0, 0), x)
            get_stacks(At(0, 0))

            def slot(at, g, left, first):
                if left < NG - g:
                    return
                a = at.next(1)
                if g == 2:
                    if not isinstance(a.j, int) or a.j:
                        sp.wait_ge(stack_in[a.half], a.j * STACK)
                        sp.sem_inc(passed, 1)
                    put_parts(a, 0)
                    put_parts(a, 1)
                    put_parts(a, 2)
                    put_parts(a, 3)
                    if not isinstance(a.j, int) or a.j:
                        sp.wait_ge(score_full, at.b * 64)
                        sp.sem_inc(passed, 1)
                    get_stacks(a)

            run_pairs(sp, slot)

        @block.vector
        def _(dve):
            def rotate(b, i):
                dve.wait_ge(rms_ready, b * TPB + (2 * i + 2))
                t = slice(2 * i, 2 * i + 2)
                every = lambda x: x[:, t, :].rearrange("p t (h d) -> p (t h) d", d=HD)
                nc.vector.tensor_tensor(every(qk), every(qk), rr[:, i * 64:(i + 1) * 64].unsqueeze(2).to_broadcast([P, 64, HD]),
                                        ALU.mult).then_inc(rot_step, 1)
                dve.wait_ge(rot_step, b * 8 + (4 * i + 1))
                by = lambda x: x[:, t, :].rearrange("p t (h d) -> p t h d", d=HD)
                cs = lambda i, a, z: rot[:, i, t, a:z].unsqueeze(2).to_broadcast([P, 2, 32, z - a])
                nc.vector.tensor_tensor(by(sq)[:, :, :, 0:8], by(qk)[:, :, :, 8:16], cs(1, 0, 8), ALU.mult).then_inc(rot_step, 1)
                nc.vector.tensor_tensor(by(sq)[:, :, :, 8:16], by(qk)[:, :, :, 0:8], cs(1, 8, 16), ALU.mult).then_inc(rot_step, 1)
                dve.wait_ge(rot_step, b * 8 + (4 * i + 3))
                nc.vector.tensor_tensor(by(qk), by(qk), cs(0, 0, 16), ALU.mult).then_inc(rot_step, 1)
                dve.wait_ge(rot_step, b * 8 + (4 * i + 4))
                nc.vector.tensor_tensor(qk[:, t, :], qk[:, t, :], sq[:, t, :], ALU.add).then_inc(qk_ready, 1)

            def finish(at, g):
                G, hf = at.b * NG, g % 2
                dve.wait_ge(av_done, at.b * 16 + (g * 4 + 6))
                dve.wait_ge(yh_ready, G + (g + 2))
                nc.vector.reciprocal(rden[:, :], den[hf][:, :]).then_inc(rden_ready, 1)
                dve.wait_ge(rden_ready, G + (g + 1))
                nc.vector.tensor_tensor(yh[:, hf, :], o[hf][:, :], rden[:, :], ALU.mult).then_inc(yh_ready, 1)
                if hf:
                    dve.wait_ge(yh_ready, G + (g + 3))
                    nc.vector.scalar_tensor_tensor(yT[:, g // 2, :], yh[:, 1, :], lam[:, 3:4], yh[:, 0, :], ALU.mult, ALU.add
                                                   ).then_inc(y_ready, 1)

            def event(key, at, n):
                k, x = n[1] % 2, int(key[-1])
                if key[0] == "Q":
                    dve.wait_ge(work_copied[k], copied_at(n))
                    nc.vector.tensor_reduce(ss[:, x * 32:(x + 1) * 32], sq[:, x, :].rearrange("p (h d) -> p h d", d=HD),
                                            AX.X, ALU.add).then_inc(ss_ready, 1)
                if key[0] == "V":
                    dve.wait_ge(work_full, full_at(n))
                    nc.vector.tensor_copy(v[:, at.half, 2 * x:2 * x + 2, :], work[k][:, :].rearrange("p (t d) -> p t d", t=2)
                                          ).then_inc(work_copied[k], 1)
                if key[0] == "O":
                    dve.wait_ge(work_full, full_at(n))
                    hh = H[:, bass.ds(at.b * TPB + 2 * x, 2), :]
                    nc.vector.tensor_tensor(hh, work[k][:, :].rearrange("p (t d) -> p t d", t=2), hh, ALU.add).then_inc(work_copied[k], 1)
                if key[0] == "F":
                    dve.wait_ge(high_ready, at.b * 4 + (x + 1))
                    nc.vector.tensor_tensor(rest[:, x % 2, :], work[k][:, :], parts[:, x % 2, 0, :], ALU.subtract).then_inc(work_copied[k], 1)
                    dve.wait_ge(work_copied[k], copied_at(n))
                    nc.vector.tensor_copy(parts[:, x % 2, 1, :], rest[:, x % 2, :]).then_inc(mid_ready, 1)

            norm.constants(nc)
            nc.vector.memset(half_neg[:, :], -0.5).then_inc(set_, 1)
            nc.vector.memset(rms_eps[:, :], RMS_EPS * HD).then_inc(set_, 1)
            nc.vector.memset(ones[:, :], 1.0).then_inc(set_, 1)
            nc.vector.sem_inc(yh_ready, 2)
            dve.wait_ge(loaded, LOADED)
            nc.vector.tensor_copy(ident16[:, :], ident[:, :]).then_inc(set_, 1)
            nc.vector.tensor_scalar(after16[:, :], upper[:, :], 1.0, -DROP, ALU.subtract, ALU.mult).then_inc(set_, 1)
            nc.vector.tensor_tensor(lam_prod[:, :, :], lam_in[:, :, 0, :], lam_in[:, :, 1, :], ALU.mult).then_inc(lam_step, 1)
            dve.wait_ge(lam_step, 1)
            nc.vector.tensor_reduce(lam[:, 0:2], lam_prod[:, :, :], AX.X, ALU.add).then_inc(lam_step, 1)
            dve.wait_ge(lam_step, 3)
            nc.vector.tensor_tensor(lam[:, 2:3], lam[:, 0:1], lam[:, 1:2], ALU.subtract).then_inc(lam_step, 1)
            dve.wait_ge(lam_step, 4)
            nc.vector.tensor_scalar(lam[:, 3:4], lam[:, 2:3], -1.0, -LAMBDA_INIT, ALU.mult, ALU.add).then_inc(lam_step, 1)
            dve.wait_ge(lam_step, 5)
            for b in range(2):
                norm.stats(nc, dve, H, b)
                norm.apply(nc, dve, H, b, xn, xn_ready)
                for e in prologue_events(b)[:6]:
                    event(*e)
                if b == 0:
                    for i in range(2):
                        rotate(0, i)
                    for e in prologue_events(0)[6:]:
                        event(*e)

            def slot(at, g, left, first):
                one, two = left >= NG - g, left >= 2 * NG - g
                for s in range(4):
                    if s == 1 and not first:
                        finish(*before(at, g))
                    if (g, s) == (0, 2) and two:
                        norm.stats(nc, dve, H, at.b + 2)
                    for e in events(at, g, s, left):
                        event(*e)
                    if g == 0 and s >= 2 and one:
                        rotate(at.b + 1, s - 2)
                    if (g, s) == (2, 1) and two:
                        dve.wait_ge(qk_ready, at.b * 2 + 4)
                        norm.apply(nc, dve, H, at.b + 2, xn, xn_ready)

            run_pairs(dve, slot)
            finish(At(B // 2 - 1, 1), NG - 1)
            for e in LAST:
                event(*e)

        @block.gpsimd
        def _(pool):
            def rms_pow(b, t):
                pool.wait_ge(ss_ready, b * TPB + (t + 1))
                c = slice(t * 32, (t + 1) * 32)
                nc.gpsimd.tensor_tensor(ss[:, c], ss[:, c], rms_eps[:, :], ALU.add).then_inc(ms_ready, 1)
                pool.wait_ge(ms_ready, b * TPB + (t + 1))
                nc.gpsimd.tensor_tensor(rr[:, c], ss[:, c], half_neg[:, :], ALU.pow).then_inc(rms_ready, 1)

            def low_part(b, x):
                pool.wait_ge(mid_ready, b * 4 + (x + 1))
                nc.gpsimd.tensor_tensor(parts[:, x % 2, 2, :], rest[:, x % 2, :], parts[:, x % 2, 1, :], ALU.subtract).then_inc(low_ready, 1)

            def event(key, at, n):
                if key[0] == "Q":
                    rms_pow(at.b, int(key[2]))
                if key[0] == "F":
                    low_part(at.b, int(key[1]))

            pool.wait_ge(norm.set, 2)
            pool.wait_ge(set_, 5)
            for b in range(2):
                norm.power(nc, pool, b)
                for e in prologue_events(b):
                    event(*e)

            def slot(at, g, left, first):
                for s in range(4):
                    for e in events(at, g, s, left):
                        event(*e)
                    if (g, s) == (0, 2) and left >= 2 * NG - g:
                        norm.power(nc, pool, at.b + 2)

            run_pairs(pool, slot)

        @block.scalar
        def _(act):
            def exps(at, g, kc):
                for i in range(GH):
                    act.wait_ge(score_full, at.b * 64 + (g * 16 + kc * GH + i + 1))
                    if i == 0:
                        act.wait_ge(av_done, at.b * 16 + (g * 4 + kc + 1))
                    nc.scalar.activation(prob[:, (kc * GH + i) % 8, 0:T - kc * P], score[i % 2][:, 0:T - kc * P], ACT.Exp,
                                         scale=HD ** 0.5).then_inc(exp_done, 1)

            def event(key, at, n):
                k, x = n[1] % 2, int(key[-1])
                if key[0] == "X":
                    act.wait_ge(work_full, full_at(n))
                    nc.scalar.activation(xT[:, x, :], work[k][:, :], ACT.Copy).then_inc(work_copied[k], 1)
                if key[0] == "Q":
                    act.wait_ge(work_full, full_at(n))
                    nc.scalar.activation(qk[:, x, :], work[k][:, :], ACT.Copy).then_inc(qk_copied, 1)
                    nc.scalar.activation(sq[:, x, :], work[k][:, :], ACT.Square).then_inc(work_copied[k], 1)
                if key[0] == "F":
                    act.wait_ge(work_full, full_at(n))
                    act.wait_ge(parts_out[x % 2], at.b * 32 + (x // 2 * 16 + 16))
                    nc.scalar.activation(parts[:, x % 2, 0, :], work[k][:, :], ACT.Copy).then_inc(high_ready, 1)

            for k in range(2):
                nc.scalar.sem_inc(work_copied[k], 1)
            nc.scalar.sem_inc(exp_done, 2)
            act.wait_ge(lam_step, 2)
            nc.scalar.activation(lam[:, 0:2], lam[:, 0:2], ACT.Exp).then_inc(lam_step, 1)
            for b in range(2):
                for e in prologue_events(b):
                    event(*e)

            def slot(at, g, left, first):
                for s in range(4):
                    exps(at, g, s)
                    for e in events(at, g, s, left):
                        event(*e)

            run_pairs(act, slot)

        @block.tensor
        def _(pe):
            def event(key, at, n):
                k, x = n[1] % 2, int(key[-1])
                if key == "X0":
                    pe.wait_ge(xn_ready, at.b * TPB + TPB)
                if key == "QK0":
                    pe.wait_ge(work_copied[(k + 1) % 2], n[0] + ((n[1] - 1) // 2 + 2))
                if key == "F0":
                    pe.wait_ge(qk_ready, at.b * 2 + 2)
                if key == "OUT0":
                    pe.wait_ge(y_ready, at.b * 2 + 2)
                pe.wait_ge(work_copied[k], claim_at(n))
                flat = work[k]
                if key[0] in "XF":
                    src = (lambda t: sq[:, t, x * P:(x + 1) * P]) if key[0] == "X" else (lambda t: qk[:, t, x * P:(x + 1) * P])
                    for t in range(TPB):
                        mm = nc.tensor.transpose(flat[:, t * P:(t + 1) * P], src(t), ident[:, :])
                elif key[0] == "Q":
                    for c in range(2):
                        mm = nc.tensor.matmul(flat[:, :], xT[:, c, x * P:(x + 1) * P], wqk[:, c, :], start=c == 0, stop=c == 1)
                else:
                    src, w = (xT, wv) if key[0] == "V" else (yT, wo)
                    for i in range(2):
                        for c in range(2):
                            t = 2 * x + i
                            mm = nc.tensor.matmul(flat[:, i * D:(i + 1) * D], src[:, c, t * P:(t + 1) * P], w[:, c, :],
                                                  start=c == 0, stop=c == 1)
                mm.then_inc(work_full, 1)

            def scores(at, g, kc, i):
                n, hd = T - kc * P, (g % 2) * NPAIR + g // 2 * GH + i
                pe.wait_ge(exp_done, at.b * 64 + (g * 16 + kc * GH + i + 1))
                nc.tensor.matmul(score[i % 2][:, 0:n], ks[:, at.half, hd, kc * P:(kc + 1) * P], qs[:, at.half, hd, kc * P:T],
                                 start=True, stop=False)
                nc.tensor.matmul(score[i % 2][:, 0:P], ident16[:, :], after16[:, :], start=False, stop=True).then_inc(score_full, 1)

            def values(at, g, kc, p):
                hf = g % 2
                if p == 0:
                    pe.wait_ge(exp_done, at.b * 64 + (g * 16 + kc * GH + GH + 2))
                    if kc == 0:
                        pe.wait_ge(yh_ready, at.b * NG + (g + 1))
                for i in range(GH):
                    out = (o if i // 2 == p else den)[hf]
                    lhs = v[:, at.half, kc, (g // 2 * GH + i) * VD:(g // 2 * GH + i + 1) * VD] if i // 2 == p else ones[:, :]
                    mm = nc.tensor.matmul(out[32 * i:32 * i + 32, kc * P:T], lhs, prob[:, (kc * GH + i) % 8, 0:T - kc * P],
                                          start=kc == 0, stop=kc == TPB - 1)
                if p == 1:
                    mm.then_inc(av_done, 1)

            pe.sem_inc(av_done, 2)
            pe.wait_ge(loaded, LOADED)
            pe.wait_ge(set_, 5)
            for b in range(2):
                for e in prologue_events(b):
                    event(*e)

            def slot(at, g, left, first):
                if g == 0:
                    pe.wait_ge(stack_in[at.half], at.j * STACK + STACK)
                for s in range(4):
                    u = (at, g, s - 1) if s else before(at, g) + (TPB - 1,)
                    for p in range(2):
                        scores(at, g, s, 2 * p)
                        scores(at, g, s, 2 * p + 1)
                        if s or not first:
                            values(*u, p)
                        if p == 0:
                            for e in events(at, g, s, left):
                                event(*e)
                    if first and s == 3:
                        for k in range(2):
                            pe.wait_ge(work_copied[k], copied_at((0, START + k)))
                        pe.sem_inc(work_full, 2)
                        for k in range(2):
                            pe.sem_inc(work_copied[k], 1)

            run_pairs(pe, slot)
            for p in range(2):
                values(At(B // 2 - 1, 1), NG - 1, TPB - 1, p)
            for e in LAST:
                event(*e)

def expert_stream(nc, m, N, I, STEP, *, turn_ready, x_of, place, down_of, mul_ready, mul_also, identT,
                  dve_more, act_first, act_more, pool_prog, sync_prog, finish, prologue_dve, dve_before, peel_first=False, dve_last=lambda dve: None):
    NI = I // P
    xT, gs, hs, hT = (m.sb(s, sh) for s, sh in (("xT", [P, 2, 2, P]), ("gs", [P, 2, I]), ("hs", [P, 2, I]), ("hT", [P, 2, NI, P])))
    pT, pG, pU, pD = ([m.ps(f"{s}{k}", [P, 512]) for k in range(2)] for s in ("pT", "pG", "pU", "pD"))
    names = ("x_turned", "xT_ready", "gu_full", "silu_ready", "hs_ready", "h_turned", "hT_ready", "down_full", "down_read")
    s = {x: m.sem(x) for x in names}
    block = m.ctx.enter_context(nc.Block())

    def steps(eng, step):
        if peel_first:
            for q in range(STEP):
                step(q, q % 2, q, 0, STEP)
        with eng.Fori(int(peel_first), N // STEP - 1) as i:
            for q in range(STEP):
                step(i * STEP + q, q % 2, q, i, STEP)
        for q in range(STEP):
            step(N - STEP + q, q % 2, q, N // STEP - 1, STEP - 1 - q)

    @block.tensor
    def _(pe):
        for x, n in (("x_turned", 4), ("gu_full", 1), ("h_turned", 2), ("down_full", 1)):
            pe.sem_inc(s[x], n)

        def turn(n, k, q, i):
            turn_ready(pe, n, q, i)
            pe.wait_ge(s["xT_ready"], n + 1)
            for c in range(2):
                mm = nc.tensor.transpose(pT[k][:, c * P:(c + 1) * P], x_of(n, q, c), identT[:, :])
            mm.then_inc(s["x_turned"], 1)

        def multiply(n, k, where):
            gate, up = mul_ready(pe, where)
            pe.wait_ge(s["xT_ready"], n + 3)
            pe.wait_ge(s["hs_ready"], n + 1)
            mul_also(pe, n, k, xT, pT)
            for w, bank in ((gate, pG), (up, pU)):
                for c in range(2):
                    mm = nc.tensor.matmul(bank[k][:, 0:I], xT[:, k, c, :], w(c), start=c == 0, stop=c == 1)
            mm.then_inc(s["gu_full"], 1)

        def turn_h(n, k):
            pe.wait_ge(s["hs_ready"], n + 3)
            pe.wait_ge(s["down_read"], n + 1)
            for c in range(NI):
                mm = nc.tensor.transpose(pD[k][:, c * P:(c + 1) * P], hs[:, k, c * P:(c + 1) * P], identT[:, :])
            mm.then_inc(s["h_turned"], 1)

        def down(n, k, q, i):
            w = down_of(pe, place(pe, n, q, i))
            pe.wait_ge(s["hT_ready"], n + 1)
            for c in range(NI):
                mm = nc.tensor.matmul(pD[k][:, 0:D], hT[:, k, c, :], w(c), start=c == 0, stop=c == NI - 1)
            mm.then_inc(s["down_full"], 1)

        turn(0, 0, 0, 0)
        turn(1, 1, 1, 0)
        multiply(0, 0, place(pe, 0, 0, 0))

        def step(n, k, q, i, left):
            where = place(pe, n + 1, (q + 1) % STEP, i + (q + 1) // STEP) if left >= 1 else None
            if left >= 2:
                turn(n + 2, k, (q + 2) % STEP, i + (q + 2) // STEP)
            turn_h(n, k)
            if left >= 1:
                multiply(n + 1, 1 - k, where)
            down(n, k, q, i)

        steps(pe, step)

    @block.scalar
    def _(act):
        act.sem_inc(s["xT_ready"], 2)

        def copy_x(n, k):
            act.wait_ge(s["x_turned"], n + 5)
            nc.scalar.activation(xT[:, k, :, :], pT[k][:, 0:D].rearrange("p (c t) -> p c t", c=2), ACT.Copy).then_inc(s["xT_ready"], 1)

        def silu(n, k):
            act.wait_ge(s["gu_full"], n + 2)
            act.wait_ge(s["hs_ready"], n + 1)
            nc.scalar.activation(gs[:, k, :], pG[k][:, 0:I], ACT.Silu).then_inc(s["silu_ready"], 1)

        def copy_h(n, k):
            act.wait_ge(s["h_turned"], n + 3)
            nc.scalar.activation(hT[:, k, :, :], pD[k][:, 0:NI * P].rearrange("p (c t) -> p c t", c=NI), ACT.Copy).then_inc(s["hT_ready"], 1)

        act_first(act, s)
        copy_x(0, 0)
        copy_x(1, 1)
        silu(0, 0)

        def step(n, k, q, i, left):
            if left >= 2:
                copy_x(n + 2, k)
            copy_h(n, k)
            if left >= 1:
                silu(n + 1, 1 - k)
            act_more(act, n, k, q, i, left, s)

        steps(act, step)

    @block.vector
    def _(dve):
        dve.sem_inc(s["hs_ready"], 2)
        dve.sem_inc(s["down_read"], 2)
        prologue_dve(dve)

        def gated(n, k):
            dve.wait_ge(s["silu_ready"], n + 1)
            dve.wait_ge(s["h_turned"], n + 1)
            nc.vector.tensor_tensor(hs[:, k, :], gs[:, k, :], pU[k][:, 0:I], ALU.mult).then_inc(s["hs_ready"], 1)

        dve_more(dve, 0, 0, pT)
        gated(0, 0)
        

        def step(n, k, q, i, left):
            dve_before(dve, n, q, i, left, s)
            if left >= 1:
                dve_more(dve, n + 1, 1 - k, pT)
                gated(n + 1, 1 - k)
            finish(dve, n, k, q, i, left, s, pD)

        steps(dve, step)
        dve_last(dve)

    if pool_prog:
        @block.gpsimd
        def _(pool):
            pool_prog(pool, s)

    if sync_prog:
        @block.sync
        def _(sp):
            sync_prog(sp, s, steps)

def zero_rows(sp, dram, rows, zeros, zeroed):
    v = dram.rearrange("(g p r) d -> g p (r d)", p=P, r=8)
    for g in range(rows // (8 * P)):
        sp.dma_start(v[g], zeros[:, :]).then_inc(zeroed, 16)
    sp.wait_ge(zeroed, 16 * (rows // (8 * P)))

class Norm:

    def __init__(self, m):
        self.pause = m.sb("pause", [P, 1])
        self.bn, self.mv = m.sb("bn", [P, TPB, 6]), m.sb("mv", [P, TPB, 2])
        self.var, self.rstd = m.sb("var", [P, TPB]), m.sb("rstd", [P, TPB])
        self.eps, self.half_neg = m.sb("eps", [P, TPB]), m.sb("half_neg", [P, TPB])
        self.bn_done, self.aggr_done = m.sem("bn_done"), m.sem("aggr_done")
        self.var_done, self.rstd_ready, self.set = m.sem("var_done"), m.sem("rstd_ready"), m.sem("norm_set")

    def constants(self, nc):
        nc.vector.memset(self.eps[:, :], LN_EPS).then_inc(self.set, 1)
        nc.vector.memset(self.half_neg[:, :], -0.5).then_inc(self.set, 1)

    def stats(self, nc, dve, H, g):
        for t in range(TPB):
            nc.vector.bn_stats(self.bn[:, t, :], H[:, bass.ds(g * TPB + t, 1), :].squeeze(1)).then_inc(self.bn_done, 1)
        dve.wait_ge(self.bn_done, g * TPB + TPB)
        nc.vector.memset(self.pause[:, :], 0.0)
        for t in range(TPB):
            nc.vector.bn_aggr(self.mv[:, t, :], self.bn[:, t, :]).then_inc(self.aggr_done, 1)

    def power(self, nc, pool, g):
        pool.wait_ge(self.aggr_done, g * TPB + TPB)
        nc.gpsimd.tensor_tensor(self.var[:, :], self.mv[:, :, 1:2].squeeze(2), self.eps[:, :], ALU.add).then_inc(self.var_done, 1)
        pool.wait_ge(self.var_done, g + 1)
        nc.gpsimd.tensor_tensor(self.rstd[:, :], self.var[:, :], self.half_neg[:, :], ALU.pow).then_inc(self.rstd_ready, 1)

    def apply(self, nc, dve, H, g, dst, ready):
        dve.wait_ge(self.rstd_ready, g + 1)
        for t in range(TPB):
            nc.vector.tensor_scalar(dst(t), H[:, bass.ds(g * TPB + t, 1), :].squeeze(1), self.mv[:, t, 0:1],
                                    self.rstd[:, t:t + 1], ALU.subtract, ALU.mult).then_inc(ready, 1)

E1, I1 = 32, 512
SORT_TILES = 96
RING = 4

def top1_experts(nc, A, S, H, slot):
    with ExitStack() as outer:
        m = Bufs(nc, outer, "t1")
        tile_tab = m.sb("tile_tab", [P, 2, SORT_TILES], I32)
        end_tab = m.sb("end_tab", [P, RING + E1], I32)
        with ExitStack() as both:
            m = Bufs(nc, both, "t1n")
            xs = m.sb("xs", [P, TILES, D])
            top, top_i = m.sb("top", [P, TILES]), m.sb("top_i", [P, TILES])
            shared_expert(nc, A, S, H, xs, top, top_i)
            sort_tokens(nc, A, S, xs, top, top_i, slot, tile_tab, end_tab)
        routed_experts(nc, A, S, tile_tab, end_tab)

def shared_expert(nc, A, S, H, xs, top, top_i):
    with ExitStack() as ctx:
        m = Bufs(nc, ctx, "sh")
        wg, wu, wd = m.sb("wg", [P, 2, I1]), m.sb("wu", [P, 2, I1]), m.sb("wd", [P, I1 // P, D])
        wr, ident = m.sb("wr", [P, 2, E1]), m.sb("ident", [P, P])
        xn = m.sb("xn", [P, TPB, D])
        zeros = m.sb("zeros", [P, 2048])
        norm, xn_ready = Norm(m), m.sem("xn_ready")
        loaded, xs_ready, zero_set, zeroed = m.sem("loaded"), m.sem("xs_ready"), m.sem("zero_set"), m.sem("zeroed")
        max_ready, index_ready, routed, logits_full = (m.sem(s) for s in ("max_ready", "index_ready", "routed", "logits_full"))
        pause = norm.pause
        lg, mx, mi = m.sb("lg", [P, E1]), m.sb("mx", [P, 8]), m.sb("mi", [P, 8], U32)

        def turn_ready(pe, n, q, i):
            pe.wait_ge(loaded, 16 * 5)
            pe.wait_ge(routed, n + 1)
            pe.wait_ge(xn_ready, n + 1)

        def logits(pe, n, k, xT, pT):
            for c in range(2):
                mm = nc.tensor.matmul(pT[k][:, D:D + E1], xT[:, k, c, :], wr[:, c, :], start=c == 0, stop=c == 1)
            mm.then_inc(logits_full, 1)

        def prologue(dve):
            norm.constants(nc)
            dve.sem_inc(routed, 2)
            nc.vector.memset(zeros[:, :], 0.0).then_inc(zero_set, 1)
            norm.stats(nc, dve, H, 0)
            norm.apply(nc, dve, H, 0, lambda t: xn[:, t, :], xn_ready)

        def norm_ahead(dve, n, q, i, left, s):
            if q == 0 and left == 4:
                norm.stats(nc, dve, H, i + 1)
            if q == 1 and left == 4:
                dve.wait_ge(s["x_turned"], i * 4 + 8)
                dve.wait_ge(xs_ready, i * 4 + 4)
                norm.apply(nc, dve, H, i + 1, lambda t: xn[:, t, :], xn_ready)

        def largest(dve, n, k, pT):
            dve.wait_ge(logits_full, n + 1)
            nc.vector.tensor_copy(lg[:, :], pT[k][:, D:D + E1]).then_inc(routed, 1)
            dve.wait_ge(routed, n + 3)
            nc.vector.memset(pause[:, :], 0.0)
            nc.vector.max(mx[:, :], lg[:, :]).then_inc(max_ready, 1)
            dve.wait_ge(max_ready, n + 1)
            nc.vector.memset(pause[:, :], 0.0)
            nc.vector.max_index(mi[:, :], mx[:, :], lg[:, :]).then_inc(index_ready, 1)
            dve.wait_ge(index_ready, n + 1)
            nc.vector.tensor_copy(top[:, bass.ds(n, 1)], mx[:, 0:1])
            nc.vector.tensor_copy(top_i[:, bass.ds(n, 1)], mi[:, 0:1])

        def finish(dve, n, k, q, i, left, s, pD):
            dve.wait_ge(s["down_full"], n + 2)
            hh = H[:, bass.ds(n, 1), :].squeeze(1)
            nc.vector.tensor_tensor(hh, pD[k][:, 0:D], hh, ALU.add).then_inc(s["down_read"], 1)

        def pool_prog(pool, s):
            pool.wait_ge(norm.set, 2)

            def keep(g):
                for t in range(TPB):
                    pool.wait_ge(xn_ready, g * TPB + t + 1)
                    nc.gpsimd.tensor_copy(xs[:, bass.ds(g * TPB + t, 1), :].squeeze(1), xn[:, t, :]).then_inc(xs_ready, 1)

            norm.power(nc, pool, 0)
            keep(0)
            with pool.Fori(0, B - 1) as i:
                norm.power(nc, pool, i + 1)
                keep(i + 1)

        def sync_prog(sp, s, steps):
            for dst, name in ((wg, "sh_gate"), (wu, "sh_up"), (wd, "sh_down"), (wr, "gate_w")):
                sp.dma_start(dst[:, :, :], A[name]).then_inc(loaded, 16)
            sp.dma_start(ident[:, :], A["ident"]).then_inc(loaded, 16)
            sp.wait_ge(zero_set, 1)
            zero_rows(sp, S["sorted_x"], SORT_TILES * P, zeros, zeroed)

        expert_stream(nc, m, TILES, I1, 4, turn_ready=turn_ready, x_of=lambda n, q, c: xn[:, q, c * P:(c + 1) * P],
                      mul_ready=lambda pe, where: (lambda c: wg[:, c, :], lambda c: wu[:, c, :]),
                      down_of=lambda pe, where: (lambda c: wd[:, c, :]), place=lambda pe, n, q, i: None, mul_also=logits, identT=ident, dve_more=largest,
                      act_first=lambda *a: None, act_more=lambda *a: None, pool_prog=pool_prog, sync_prog=sync_prog, finish=finish, prologue_dve=prologue, dve_before=norm_ahead)

def sort_tokens(nc, A, S, xs, top, top_i, slot, tile_tab, end_tab):
    with ExitStack() as ctx:
        m = Bufs(nc, ctx, "st")
        iota, k128 = m.sb("iota", [P, P]), m.sb("k128", [P, P])
        strict_f, strict, ones = m.sb("strict_f", [P, P]), m.sb("strict", [P, P], BF16), m.sb("ones", [P, P], BF16)
        idx, score = m.sb("idx", [P, TILES]), m.sb("score", [P, TILES])
        hot = m.sb("hot", [P, TILES, E1], BF16)
        tot, run, flag = m.sb("tot", [P, E1, TILES]), m.sb("run", [P, E1, TILES]), m.sb("flag", [P, E1, TILES])
        ntile, end, base = m.sb("ntile", [P, E1]), m.sb("end", [P, E1]), m.sb("base", [P, E1])
        tile_e, tile_f = m.sb("tile_e", [P, SORT_TILES, E1]), m.sb("tile_f", [P, SORT_TILES])
        slot_f, score_in = m.sb("slot_f", [P, TILES]), m.sb("score_in", [P, TILES])
        pre = [m.ps(f"pre{g}", [P, 512]) for g in range(4)]
        sums = [m.ps(f"sums{g}", [P, 512]) for g in range(4)]
        loaded, step, counted, score_ready = m.sem("loaded"), m.sem("step"), m.sem("counted"), m.sem("score_ready")
        scaled, scattered = m.sem("scaled"), m.sem("scattered")
        block = ctx.enter_context(nc.Block())
        GT = TILES // 4

        @block.sync
        def _(sp):
            for dst, name in ((iota, "iota128"), (k128, "k128"), (strict_f, "strict")):
                sp.dma_start(dst[:, :], A[name]).then_inc(loaded, 16)

        @block.scalar
        def _(act):
            act.wait_ge(step, 1)
            nc.scalar.activation(score[:, :], score_in[:, :], ACT.Sigmoid).then_inc(score_ready, 1)

        @block.tensor
        def _(pe):
            pe.wait_ge(step, 5)
            for g in range(4):
                r = hot[:, g * GT:(g + 1) * GT, :].rearrange("p t e -> p (t e)")
                nc.tensor.matmul(pre[g][:, :], strict[:, :], r, start=True, stop=True).then_inc(counted, 1)
                nc.tensor.matmul(sums[g][:, :], ones[:, :], r, start=True, stop=True).then_inc(counted, 1)

        @block.vector
        def _(dve):
            n = [0]

            def link(ins):
                n[0] += 1
                ins.then_inc(step, 1)
                dve.wait_ge(step, n[0])

            link(nc.vector.tensor_copy(score_in[:, :], top[:, :]))
            dve.wait_ge(loaded, 48)
            link(nc.vector.tensor_copy(idx[:, :], top_i[:, :]))
            link(nc.vector.tensor_copy(strict[:, :], strict_f[:, :]))
            link(nc.vector.memset(ones[:, :], 1.0))
            link(nc.vector.tensor_tensor(hot[:, :, :], iota[:, 0:E1].unsqueeze(1).to_broadcast([P, TILES, E1]),
                                         idx[:, :].unsqueeze(2).to_broadcast([P, TILES, E1]), ALU.is_equal))
            link(nc.vector.memset(flag[:, :, :], 1.0))
            link(nc.vector.memset(flag[:, :, 0:1], 0.0))
            dve.wait_ge(counted, 8)
            for g in range(4):
                link(nc.vector.tensor_copy(tot[:, :, g * GT:(g + 1) * GT], sums[g][:, :].rearrange("p (t e) -> p e t", e=E1)))
            flat = lambda x: x[:, :, :].rearrange("p e t -> p (e t)")
            link(nc.vector.tensor_tensor_scan(flat(run), flat(flag), flat(tot), 0.0, ALU.mult, ALU.add))
            link(nc.vector.tensor_tensor(flag[:, :, :], run[:, :, TILES - 1:TILES].to_broadcast([P, E1, TILES]),
                                         k128[:, 0:TILES].unsqueeze(1).to_broadcast([P, E1, TILES]), ALU.is_gt))
            link(nc.vector.tensor_reduce(ntile[:, :], flag[:, :, :], AX.X, ALU.add))
            link(nc.vector.memset(base[:, :], 1.0))
            link(nc.vector.tensor_tensor_scan(end[:, :], base[:, :], ntile[:, :], 0.0, ALU.mult, ALU.add))
            link(nc.vector.tensor_tensor(base[:, :], end[:, :], ntile[:, :], ALU.subtract))
            link(nc.vector.tensor_scalar(base[:, :], base[:, :], float(P), None, ALU.mult))
            link(nc.vector.tensor_tensor(run[:, :, :], run[:, :, :], tot[:, :, :], ALU.subtract))
            link(nc.vector.tensor_tensor(run[:, :, :], run[:, :, :], base[:, :].unsqueeze(2).to_broadcast([P, E1, TILES]), ALU.add))
            place = tot[:, :, :].rearrange("p e t -> p (e t)").rearrange("p (t e) -> p t e", e=E1)
            for g in range(4):
                link(nc.vector.tensor_tensor(place[:, g * GT:(g + 1) * GT, :], pre[g][:, :].rearrange("p (t e) -> p t e", e=E1),
                                             run[:, :, g * GT:(g + 1) * GT].rearrange("p e t -> p t e"), ALU.add))
            link(nc.vector.tensor_tensor(place, place, hot[:, :, :], ALU.mult))
            link(nc.vector.tensor_reduce(slot_f[:, :], place, AX.X, ALU.add))
            link(nc.vector.tensor_copy(slot[:, :], slot_f[:, :]))
            dve.wait_ge(score_ready, 1)
            for g in range(8):
                nc.vector.tensor_tensor(xs[:, 8 * g:8 * g + 8, :], xs[:, 8 * g:8 * g + 8, :],
                                        score[:, 8 * g:8 * g + 8].unsqueeze(2).to_broadcast([P, 8, D]), ALU.mult).then_inc(scaled, 1)
            link(nc.vector.tensor_tensor(tile_e[:, :, :], end[:, :].unsqueeze(1).to_broadcast([P, SORT_TILES, E1]),
                                         iota[:, 0:SORT_TILES].unsqueeze(2).to_broadcast([P, SORT_TILES, E1]), ALU.is_le))
            link(nc.vector.tensor_reduce(tile_f[:, :], tile_e[:, :, :], AX.X, ALU.add))
            link(nc.vector.tensor_scalar(tile_f[:, :], tile_f[:, :], float(E1 - 1), None, ALU.min))
            link(nc.vector.tensor_copy(tile_tab[:, 0, :], tile_f[:, :]))
            link(nc.vector.tensor_scalar(tile_tab[:, 1, :], tile_tab[:, 0, :], RING - 1, None, ALU.bitwise_and))
            link(nc.vector.memset(end_tab[:, :], 0))
            link(nc.vector.tensor_copy(end_tab[:, RING:RING + E1], end[:, :]))

        @block.gpsimd
        def _(pool):
            for t in range(TILES):
                pool.wait_ge(scaled, t // 8 + 1)
                nc.gpsimd.indirect_dma_start(S["sorted_x"], bass.IndirectOffsetOnAxis(ap=slot[:, t:t + 1], axis=0),
                                             xs[:, t, :], None).then_inc(scattered, 16)
            pool.wait_ge(scattered, 16 * TILES)

def routed_experts(nc, A, S, tile_tab, end_tab):
    with ExitStack() as ctx:
        m = Bufs(nc, ctx, "ro")
        wgu, wd = m.sb("wgu", [P, RING, 2, 2 * I1]), m.sb("wd", [P, RING, I1 // P, D])
        ident, xt, o = m.sb("ident", [P, P]), m.sb("xt", [P, 4, D]), m.sb("o", [P, 4, D])
        id_in, gu_in, wd_in, gu_go, wd_go = (m.sem(x) for x in ("id_in", "gu_in", "wd_in", "gu_go", "wd_go"))
        x_in = [m.sem(f"x_in{k}") for k in range(4)]
        o_out = [m.sem(f"o_out{k}") for k in range(4)]
        xv = S["sorted_x"].rearrange("(n p) d -> n p d", p=P)
        yv = S["sorted_y"].rearrange("(n p) d -> n p d", p=P)

        def turn_ready(pe, n, q, i):
            pe.wait_ge(id_in, 16)
            pe.wait_ge(x_in[q], i * 16 + 16)

        def place(pe, n, q, i):
            e = pe.value_load(tile_tab[0:1, 0, bass.ds(n, 1)], min_val=0, max_val=E1 - 1)
            r = pe.value_load(tile_tab[0:1, 1, bass.ds(n, 1)], min_val=0, max_val=RING - 1)
            return e, r

        def mul_ready(pe, where):
            e, r = where
            pe.wait_ge(gu_in, e * 16 + 16)
            w = lambda a: (lambda c: wgu[:, bass.ds(r, 1), c, a:a + I1].squeeze(1))
            return w(0), w(I1)

        def down_of(pe, where):
            e, r = where
            pe.wait_ge(wd_in, e * 16 + 16)
            return lambda c: wd[:, bass.ds(r, 1), c, :].squeeze(1)

        def finish(dve, n, k, q, i, left, s, pD):
            dve.wait_ge(s["down_full"], n + 2)
            dve.wait_ge(o_out[q], i * 16 + 16)
            nc.vector.tensor_copy(o[:, q, :], pD[k][:, 0:D]).then_inc(s["down_read"], 1)

        def act_first(act, s):
            for k in range(4):
                act.dma_start(xt[:, k, :], xv[k]).then_inc(x_in[k], 16)
                act.sem_inc(o_out[k], 16)

        def act_more(act, n, k, q, i, left, s):
            if left == 4:
                act.wait_ge(s["x_turned"], n + 5)
                act.dma_start(xt[:, q, :], xv[bass.ds(n + 4, 1)].squeeze(0)).then_inc(x_in[q], 16)
            act.wait_ge(s["down_read"], n + 3)
            act.dma_start(yv[bass.ds(n, 1)].squeeze(0), o[:, q, :]).then_inc(o_out[q], 16)
            if left == 0:
                for k in range(4):
                    act.wait_ge(o_out[k], 16 * (SORT_TILES // 4) + 16)

        def load_expert(eng, e, k, dst, src, arrived, used, go, first=False):
            gone = eng.value_load(end_tab[0:1, bass.ds(e, 1)], min_val=0, max_val=SORT_TILES)
            eng.wait_ge(used, gone + 1)
            eng.sem_inc(go, 1)
            if not first:
                eng.wait_ge(arrived, e * 16)
                if src is A["ro_down"]:
                    eng.sem_inc(go, 1)
            eng.dma_start(dst[:, k, :, :], src[bass.ds(e, 1)].squeeze(0)).then_inc(arrived, 16)

        def pool_prog(pool, s):
            for k in range(RING):
                load_expert(pool, k, k, wd, A["ro_down"], wd_in, s["down_full"], wd_go, k == 0)
            with pool.Fori(1, E1 // RING) as i:
                for k in range(RING):
                    load_expert(pool, i * RING + k, k, wd, A["ro_down"], wd_in, s["down_full"], wd_go)

        def sync_prog(sp, s, steps):
            sp.dma_start(ident[:, :], A["ident"]).then_inc(id_in, 16)
            for k in range(RING):
                load_expert(sp, k, k, wgu, A["ro_gu"], gu_in, s["gu_full"], gu_go, k == 0)
            with sp.Fori(1, E1 // RING) as i:
                for k in range(RING):
                    load_expert(sp, i * RING + k, k, wgu, A["ro_gu"], gu_in, s["gu_full"], gu_go)

        expert_stream(nc, m, SORT_TILES, I1, 4, turn_ready=turn_ready, x_of=lambda n, q, c: xt[:, q, c * P:(c + 1) * P],
                      mul_ready=mul_ready, down_of=down_of, place=place, mul_also=lambda *a: None, identT=ident,
                      dve_more=lambda *a: None, act_first=act_first, act_more=act_more, pool_prog=pool_prog,
                      sync_prog=sync_prog, finish=finish, prologue_dve=lambda dve: None, dve_before=lambda *a: None)

KEEP = 204

def sparse_attention(nc, A, S, H, slot):
    routing_scores(nc, A, S, H, slot)
    masked_attention(nc, A, S, H)

def routing_scores(nc, A, S, H, slot):
    HID = 64
    R = 2 * TPB
    with ExitStack() as ctx:
        m = Bufs(nc, ctx, "rs")
        w1, w2, b1, b2, ident = m.sb("w1", [P, 2, HID]), m.sb("w2", [HID, P]), m.sb("b1", [HID, 1]), m.sb("b2", [NH, 1]), m.sb("ident", [P, P])
        rows = m.sb("rows", [P, R, D])
        xn, xT = m.sb("xn", [P, TPB, D]), m.sb("xT", [P, 2, 2, T])
        h1, r1, r2 = m.sb("h1", [HID, 2, T]), m.sb("r1", [NH, 2, T]), m.sb("r2", [NH, 2, T])
        norm = Norm(m)
        turn = [m.ps(f"turn{c}", [P, T]) for c in range(2)]
        hid, lg = [m.ps(f"hid{k}", [P, T]) for k in range(2)], [m.ps(f"lg{k}", [P, T]) for k in range(2)]
        loaded, added, xn_ready, x_turned, xT_ready = (m.sem(x) for x in ("loaded", "added", "xn_ready", "x_turned", "xT_ready"))
        hid_full, h1_ready, lg_full, r1_ready, r2_ready = (m.sem(x) for x in ("hid_full", "h1_ready", "lg_full", "r1_ready", "r2_ready"))
        r_out, got = [m.sem(f"r_out{k}") for k in range(2)], [m.sem(f"got{r}") for r in range(R)]
        block = ctx.enter_context(nc.Block())
        LOADED = 16 * 5

        @block.sync
        def _(sp):
            for dst, name in ((w1[:, :, :], "r_w1"), (w2[:, :], "r_w2"), (b1[:, :], "r_b1"), (b2[:, :], "r_b2"), (ident[:, :], "ident")):
                sp.dma_start(dst, A[name]).then_inc(loaded, 16)
            for k in range(2):
                sp.sem_inc(r_out[k], 16)
            rv = S["route"].rearrange("(b h) t -> b h t", h=NH)
            with sp.Fori(0, B // 2) as j:
                for k in range(2):
                    sp.wait_ge(r2_ready, j * 2 + k + 1)
                    sp.dma_start(rv[bass.ds(j * 2 + k, 1)].squeeze(0), r2[:, k, :]).then_inc(r_out[k], 16)
            for k in range(2):
                sp.wait_ge(r_out[k], 16 * (B // 2 + 1))

        @block.gpsimd
        def _(pool):
            def gather(b):
                for t in range(b * TPB, (b + 1) * TPB):
                    if t >= R:
                        pool.wait_ge(added, t - R + 1)
                    nc.gpsimd.indirect_dma_start(rows[:, t % R, :], None, S["sorted_y"],
                                                 bass.IndirectOffsetOnAxis(ap=slot[:, t:t + 1], axis=0)).then_inc(got[t % R], 16)

            gather(0)
            pool.wait_ge(norm.set, 2)
            for b in range(B):
                if b + 1 < B:
                    gather(b + 1)
                norm.power(nc, pool, b)

        @block.vector
        def _(dve):
            norm.constants(nc)
            dve.sem_inc(x_turned, 2)
            with dve.Fori(0, B // 2) as j:
                for k in range(2):
                    b = j * 2 + k
                    for t in range(TPB):
                        hh = H[:, bass.ds(b * TPB + t, 1), :].squeeze(1)
                        dve.wait_ge(got[k * TPB + t], j * 16 + 16)
                        nc.vector.tensor_tensor(hh, hh, rows[:, k * TPB + t, :], ALU.add).then_inc(added, 1)
                    dve.wait_ge(added, b * TPB + TPB)
                    nc.vector.memset(norm.pause[:, :], 0.0)
                    norm.stats(nc, dve, H, b)
                    dve.wait_ge(x_turned, b * 2 + 2)
                    norm.apply(nc, dve, H, b, lambda t: xn[:, t, :], xn_ready)

        @block.scalar
        def _(act):
            for s, n in ((xT_ready, 2), (h1_ready, 2), (r1_ready, 2)):
                act.sem_inc(s, n)
            act.wait_ge(loaded, LOADED)

            def copy_x(b, k):
                for c in range(2):
                    act.wait_ge(x_turned, b * 2 + (c + 3))
                    nc.scalar.activation(xT[:, k, c, :], turn[c][:, :], ACT.Copy).then_inc(xT_ready, 1)

            def batch(j, k, more):
                b = j * 2 + k
                if more:
                    copy_x(b + 1, 1 - k)
                act.wait_ge(hid_full, b + 1)
                nc.scalar.activation(h1[:, k, :], hid[k][0:HID, :], ACT.Relu, bias=b1[:, 0:1]).then_inc(h1_ready, 1)
                act.wait_ge(lg_full, b + 1)
                nc.scalar.activation(r1[:, k, :], lg[k][0:NH, :], ACT.Sigmoid, bias=b2[:, 0:1]).then_inc(r1_ready, 1)
                act.wait_ge(r1_ready, b + 3)
                act.wait_ge(r_out[k], j * 16 + 16)
                nc.scalar.activation(r2[:, k, :], r1[:, k, :], ACT.Sigmoid).then_inc(r2_ready, 1)

            copy_x(0, 0)
            with act.Fori(0, B // 2 - 1) as j:
                for k in range(2):
                    batch(j, k, True)
            for k in range(2):
                batch(B // 2 - 1, k, k == 0)

        @block.tensor
        def _(pe):
            pe.wait_ge(loaded, LOADED)

            def turn_x(b):
                pe.wait_ge(xn_ready, b * TPB + TPB)
                for c in range(2):
                    pe.wait_ge(xT_ready, b * 2 + (c + 1))
                    for t in range(TPB):
                        mm = nc.tensor.transpose(turn[c][:, t * P:(t + 1) * P], xn[:, t, c * P:(c + 1) * P], ident[:, :])
                    mm.then_inc(x_turned, 1)

            def batch(j, k, more):
                b = j * 2 + k
                if more:
                    turn_x(b + 1)
                pe.wait_ge(xT_ready, b * 2 + 4)
                pe.wait_ge(h1_ready, b + 1)
                for c in range(2):
                    mm = nc.tensor.matmul(hid[k][0:HID, :], w1[:, c, :], xT[:, k, c, :], start=c == 0, stop=c == 1)
                mm.then_inc(hid_full, 1)
                pe.wait_ge(h1_ready, b + 3)
                pe.wait_ge(r1_ready, b + 1)
                nc.tensor.matmul(lg[k][:, :], w2[:, :], h1[:, k, :], start=True, stop=True).then_inc(lg_full, 1)

            turn_x(0)
            with pe.Fori(0, B // 2 - 1) as j:
                for k in range(2):
                    batch(j, k, True)
            for k in range(2):
                batch(B // 2 - 1, k, k == 0)

def masked_attention(nc, A, S, H):
    GH = 4
    ROUNDS = -(-KEEP // 8)
    SPARE = ROUNDS * 8 - KEEP
    TAKEN = -1.0
    STACK = 13 * 16
    ORD = {(0, "FIN"): 0, (0, "MAX"): 1, (0, "V0"): 2, (0, "V1"): 3, (1, "FIN"): 4, (1, "MAX"): 5, (1, "X0"): 6,
           (2, "FIN"): 7, (2, "MAX"): 8, (2, "X1"): 9, (2, "Q0"): 10,
           (3, "FIN"): 11, (3, "MAX"): 12, (3, "Q1"): 13, (3, "K0"): 14, (3, "K1"): 15}
    STEP = {(0, 4): "V0", (0, 6): "V1", (1, 6): "X0", (2, 4): "X1", (2, 6): "Q0", (3, 4): "Q1", (3, 6): "K0",
            (3, 7): "K1"}
    CHUNK = {"Q0": 0, "Q1": 1, "K0": 2, "K1": 3}
    PRO = ["X0", "X1", "Q0", "Q1", "K0", "K1", "V0", "V1"]
    with ExitStack() as ctx:
        m = Bufs(nc, ctx, "ma")
        w, wv, ident, bias = m.sb("w", [P, 2, 4, P]), m.sb("wv", [P, 2, D]), m.sb("ident", [P, P]), m.sb("bias", [P, 4])
        ident16, bv = m.sb("ident16", [P, P], BF16), m.sb("bv", [P, D])
        xn, xT = m.sb("xn", [P, TPB, D]), m.sb("xT", [P, 2, T])
        full, rest, parts = m.sb("full", [P, 2, T]), m.sb("rest", [P, 2, T]), m.sb("parts", [P, 2, 3, T], BF16)
        qs, ks = m.sb("qs", [P, 2, NH, T], BF16), m.sb("ks", [P, 2, NH, T], BF16)
        v1 = m.sb("v1", [P, 2, TPB, NH, 2 * HD])
        nmax, nrest, nparts = m.sb("nmax", [P, 2, GH, TPB]), m.sb("nrest", [P, GH, TPB]), m.sb("nparts", [P, 2, TPB, 3, GH], BF16)
        nturned = m.sb("nturned", [3 * GH, T], BF16)
        prob, sumT = m.sb("prob", [P, 8, T]), m.sb("sumT", [P, 2, T])
        rden, part = m.sb("rden", [P, TPB, GH]), m.sb("part", [P, TPB, GH, HD])
        left_scores, mx, mask = m.sb("left_scores", [P, 2, 2, T]), m.sb("mx", [P, 2, 8]), m.sb("mask", [P, 2, T], BF16)
        norm = Norm(m)
        s1 = [m.ps(f"s1_{i}", [P, 2, T]) for i in range(2)]
        s2 = [m.ps(f"s2_{i}", [P, T]) for i in range(2)]
        sums, work = m.ps("sums", [P, T]), m.ps("work", [P, T])
        names = ("loaded", "ones_set", "v_ones", "id_ready", "xn_ready", "work_full", "work_copied", "rest_ready", "mid_ready", "low_ready", "full_ready",
                 "s1_full", "max_ready", "nsplit", "nparts_ready", "nturned_ready", "s2_full", "exp_done", "av_done",
                 "sum_copied", "rden_ready", "part_ready", "nmid_ready", "passed", "pool_passed",
                 "route_in", "found", "taken", "mask_made", "mask_out")
        (loaded, ones_set, v_ones, id_ready, xn_ready, work_full, work_copied, rest_ready, mid_ready, low_ready, full_ready, s1_full, max_ready, nsplit,
         nparts_ready, nturned_ready, s2_full, exp_done, av_done, sum_copied, rden_ready, part_ready, nmid_ready, passed, pool_passed,
         route_in, found, taken, mask_made, mask_out) = (m.sem(x) for x in names)
        parts_out = [m.sem(f"parts_out{k}") for k in range(2)]
        stack_in, nmax_out, nmax_in = ([m.sem(f"{x}{k}") for k in range(2)] for x in ("stack_in", "nmax_out", "nmax_in"))
        block = ctx.enter_context(nc.Block())
        LOADED = 16 * 5

        present = [(half, g, key) for half in range(2) for g, key in ORD
                   if key == "FIN" or (key == "MAX" and (half, g) != (1, NG - 1)) or (key[0] == "V" and half == 0)]
        LAST_ORD = {k: i for i, k in enumerate(present)}
        LAST_EVENT = (B - 2) * 16 + 16 + len(present)

        def ordinal(at, g, key, left):
            if left == MANY:
                return at.b * 16 + (16 + ORD[g, key])
            return (B - 2) * 16 + 16 + LAST_ORD[at.half, g, key]

        def events(at, g, s, left):
            key = STEP.get((g, s))
            if key is None:
                return None
            ahead = 1 if g == 0 else 2
            if left < NG * ahead - g:
                return None
            return key, at.next(ahead), ordinal(at, g, key, left)

        @block.sync
        def _(sp):
            for g in range(2):
                sp.dma_start(left_scores[:, g, 0, :], S["route"][g * P:(g + 1) * P, :]).then_inc(route_in, 16)
            for dst, name in ((w[:, :, :, :], "l1_wqk"), (wv[:, :, :], "l1_wv"), (ident[:, :], "ident"), (bias[:, :], "l1_bias")):
                sp.dma_start(dst, A[name]).then_inc(loaded, 16)
            sp.dma_start(bv[:, :], A["l1_bv"].to_broadcast([P, D])).then_inc(loaded, 16)
            for k in range(2):
                sp.sem_inc(parts_out[k], 16)
                sp.sem_inc(nmax_in[k], 16)

            def put_parts(at, x):
                sp.wait_ge(low_ready, at.b * 4 + x + 1)
                sp.dma_start(S["parts"][at.half, x // 2, :, (x % 2) * P:(x % 2) * P + P, :].rearrange("a p t -> p a t"),
                             parts[:, x % 2, :, :]).then_inc(parts_out[x % 2], 16)

            def get_stacks(at):
                for k in range(2):
                    sp.wait_ge(parts_out[k], at.b * 32 + 48)
                    sp.sem_inc(passed, 1)
                for i, (stack, order) in enumerate(((qs, Q_PARTS), (ks, K_PARTS))):
                    for r, a in enumerate(order):
                        sp.dma_start(stack[r * HD:(r + 1) * HD, at.half, :, :],
                                     S["parts"][at.half, i, a].rearrange("(h d) t -> d h t", d=HD)).then_inc(stack_in[at.half], 16)

            def get_mask(at):
                sp.dma_start(ks[ROWS:ROWS + 1, at.half, :, :],
                             S["mask"].rearrange("(b h) t -> b h t", h=NH)[bass.ds(at.b, 1)]).then_inc(stack_in[at.half], 16)

            def move_maxima(at, g):
                sp.wait_ge(nturned_ready, at.b * NG + g + 1)
                sp.sem_inc(passed, 1)
                sp.wait_ge(nmax_in[g % 2], at.b * 32 + (g // 2 * 16 + 16))
                sp.dma_start(S["maxima"][g % 2], nturned[:, :]).then_inc(nmax_out[g % 2], 16)
                sp.wait_ge(nmax_out[g % 2], at.b * 32 + (g // 2 * 16 + 16))
                sp.dma_start(qs[ROWS + 1:ROWS + 4, at.half, g * GH:(g + 1) * GH, :],
                             S["maxima"][g % 2].rearrange("(a h) t -> a h t", h=GH)).then_inc(nmax_in[g % 2], 16)

            def prologue():
                for x in range(4):
                    put_parts(At(0, 0), x)
                get_stacks(At(0, 0))
                for x in range(4):
                    put_parts(At(0, 1), x)
                for g in range(2):
                    sp.wait_ge(mask_made, g + 3)
                    sp.dma_start(S["mask"][g * P:(g + 1) * P, :], mask[:, g, :]).then_inc(mask_out, 16)
                sp.wait_ge(mask_out, 32)
                sp.wait_ge(ones_set, 2)
                get_mask(At(0, 0))
                get_stacks(At(0, 1))
                sp.wait_ge(ones_set, 4)
                get_mask(At(0, 1))
                move_maxima(At(0, 0), 0)

            def slot(at, g, left, first):
                if left >= 1:
                    move_maxima(*later(at, g, 1))
                if g == 0 and not first and left >= NG:
                    sp.wait_ge(s2_full, at.b * 64)
                    sp.sem_inc(passed, 1)
                    get_stacks(at.next(1))
                    get_mask(at.next(1))
                if g == 2 and left >= 2 * NG - g:
                    sp.wait_ge(stack_in[at.half], at.j * STACK + STACK)
                    sp.sem_inc(passed, 1)
                for x in {2: (0,), 3: (1, 2, 3)}.get(g, ()):
                    if left >= 2 * NG - g:
                        put_parts(at.next(2), x)

            prologue()
            run_pairs(sp, slot)
            for k in range(2):
                sp.wait_ge(nmax_in[k], 32 * B + 16)

        @block.gpsimd
        def _(pool):
            def power(b):
                norm.power(nc, pool, b)

            def low_part(b, x, n):
                pool.wait_ge(work_copied, n + 2)
                k = x % 2
                nc.gpsimd.tensor_tensor(rest[:, k, :], full[:, k, :], parts[:, k, 0, :], ALU.subtract).then_inc(rest_ready, 1)
                pool.wait_ge(rest_ready, b * 4 + x + 1)
                pool.sem_inc(pool_passed, 1)
                nc.gpsimd.tensor_copy(parts[:, k, 1, :], rest[:, k, :]).then_inc(mid_ready, 1)
                pool.wait_ge(mid_ready, b * 4 + x + 1)
                nc.gpsimd.tensor_tensor(parts[:, k, 2, :], rest[:, k, :], parts[:, k, 1, :], ALU.subtract).then_inc(low_ready, 1)

            def prologue():
                pool.wait_ge(norm.set, 2)
                def set_ones(stack, a, z, half, n):
                    nc.gpsimd.memset(stack[a:z, half, :, :], 1.0).then_inc(ones_set, 1)
                    pool.wait_ge(ones_set, n)

                power(0)
                pool.wait_ge(norm.rstd_ready, 1)
                set_ones(ks, ROWS, ROWS + 4, 0, 1)
                for x in range(4):
                    low_part(0, x, 2 + x)
                power(1)
                pool.wait_ge(norm.rstd_ready, 2)
                set_ones(qs, ROWS, ROWS + 1, 0, 2)
                for x in range(4):
                    low_part(1, x, 8 + 2 + x)
                pool.wait_ge(low_ready, 8)
                set_ones(ks, ROWS, ROWS + 4, 1, 3)
                set_ones(qs, ROWS, ROWS + 1, 1, 4)

            def slot(at, g, left, first):
                if g == 1 and left >= 2 * NG - g:
                    power(at.b + 2)
                for s in range(8):
                    e = events(at, g, s, left)
                    if e and e[0] in CHUNK:
                        low_part(e[1].b, CHUNK[e[0]], e[2])

            prologue()
            run_pairs(pool, slot)

        @block.tensor
        def _(pe):
            work16 = work[:, :].bitcast(BF16)

            def claim(n):
                pe.wait_ge(work_copied, n + 1)

            def event(key, at, n):
                if key == "X0":
                    pe.wait_ge(xn_ready, at.b * TPB + TPB)
                claim(n)
                if key[0] == "X":
                    c = int(key[1])
                    for t in range(TPB):
                        mm = nc.tensor.transpose(work[:, t * P:(t + 1) * P], xn[:, t, c * P:(c + 1) * P], ident[:, :])
                elif key[0] == "V":
                    for i in range(2):
                        t = 2 * int(key[1]) + i
                        for c in range(2):
                            mm = nc.tensor.matmul(work[:, i * D:(i + 1) * D], xT[:, c, t * P:(t + 1) * P], wv[:, c, :],
                                                  start=c == 0, stop=c == 1)
                else:
                    for c in range(2):
                        mm = nc.tensor.matmul(work[:, :], w[:, c, CHUNK[key], :], xT[:, c, :], start=c == 0, stop=c == 1)
                mm.then_inc(work_full, 1)

            def turn_maxima(at, g, n):
                pe.wait_ge(nparts_ready, at.b * NG + g + 1)
                claim(n)
                for qc in range(TPB):
                    mm = nc.tensor.transpose(work16[0:3 * GH, qc * P:(qc + 1) * P], nparts[:, g % 2, qc, :, :].rearrange("p a h -> p (a h)"),
                                             ident16[:, :])
                mm.then_inc(work_full, 1)

            def turn_sums(at, g, n):
                pe.wait_ge(sum_copied, at.b * NG + g + 1)
                claim(n)
                for qc in range(TPB):
                    mm = nc.tensor.transpose(work[:, qc * P:(qc + 1) * P], sumT[:, (g + 1) % 2, qc * P:(qc + 1) * P], ident[:, :])
                mm.then_inc(work_full, 1)

            def pass1(at, g, u):
                if g == 0 and u == 0:
                    pe.wait_ge(stack_in[at.half], at.j * STACK + STACK)
                h = g * GH + u // 2
                pe.wait_ge(max_ready, at.b * 32 + (g * 8 + u + 1))
                for i in range(2):
                    qc = (u % 2) * 2 + i
                    mm = nc.tensor.matmul(s1[u % 2][:, i, :], qs[0:ROWS + 1, at.half, h, qc * P:(qc + 1) * P],
                                          ks[0:ROWS + 1, at.half, h, :], start=True, stop=True)
                mm.then_inc(s1_full, 1)

            def pass2(at, g, u):
                if u == 0:
                    pe.wait_ge(nmax_in[g % 2], at.b * 32 + (g // 2 * 16 + 32))
                kc, h = u // GH, g * GH + u % GH
                pe.wait_ge(exp_done, at.b * 64 + (g * 16 + u + 1))
                nc.tensor.matmul(s2[u % 2][:, :], ks[0:ROWS + 4, at.half, h, kc * P:(kc + 1) * P], qs[0:ROWS + 4, at.half, h, :],
                                 start=True, stop=True).then_inc(s2_full, 1)

            def values(at, g, kc):
                pe.wait_ge(exp_done, at.b * 64 + (g * 16 + kc * GH + GH + 2))
                if kc == 0:
                    pe.wait_ge(sum_copied, at.b * NG + g + 1)
                for i in range(GH):
                    mm = nc.tensor.matmul(sums[32 * i:32 * i + 32, :], v1[:, at.half, kc, g * GH + i, :], prob[:, (kc * GH + i) % 8, :],
                                          start=kc == 0, stop=kc == TPB - 1)
                mm.then_inc(av_done, 1)

            def prologue():
                pe.sem_inc(av_done, 2)
                pe.wait_ge(loaded, LOADED)
                pe.wait_ge(id_ready, 1)
                pe.wait_ge(v_ones, 1)
                for n, key in enumerate(PRO + PRO[:6]):
                    event(key, At(0, n // 8), n)
                for u in range(8):
                    pass1(At(0, 0), 0, u)
                for u in range(8):
                    pass1(At(0, 0), 1, u)
                turn_maxima(At(0, 0), 0, 14)
                pe.wait_ge(work_copied, 16)
                pe.sem_inc(work_full, 2)

            def slot(at, g, left, first):
                for s in range(8):
                    if left >= 2:
                        a, h = later(at, g, 2)
                        pass1(a, h, s)
                    for u in (2 * s, 2 * s + 1):
                        pass2(at, g, u)
                    if s == 0 and not first:
                        values(*before(at, g), TPB - 1)
                    if s == 1 and not first:
                        turn_sums(at, g, ordinal(at, g, "FIN", left))
                    if s == 2 and left >= 1:
                        turn_maxima(*later(at, g, 1), ordinal(at, g, "MAX", left))
                    if s in (3, 5, 7):
                        values(at, g, (s - 3) // 2)
                    e = events(at, g, s, left)
                    if e:
                        event(*e)

            prologue()
            run_pairs(pe, slot)
            values(At(B // 2 - 1, 1), NG - 1, TPB - 1)
            turn_sums(At(B // 2, 0), 0, LAST_EVENT)

        @block.vector
        def _(dve):
            def maximum(at, g, u):
                dve.wait_ge(s1_full, at.b * 32 + (g * 8 + u + 1))
                if u == 0:
                    dve.wait_ge(nsplit, at.b * 2 * NG + (g * 2 + 2))
                h, q = u // 2, (u % 2) * 2
                nc.vector.tensor_reduce(nmax[:, g % 2, h, q:q + 2], s1[u % 2][:, :, :], AX.X, ALU.max, negate=True).then_inc(max_ready, 1)

            def split_maxima(at, g):
                dve.wait_ge(max_ready, at.b * 32 + (g * 8 + 8 + 2))
                out = lambda a: nparts[:, g % 2, :, a, :].rearrange("p q h -> p h q")
                nc.vector.tensor_copy(out(0), nmax[:, g % 2, :, :]).then_inc(nsplit, 1)
                dve.wait_ge(nsplit, at.b * 2 * NG + (g * 2 + 5))
                nc.vector.tensor_tensor(nrest[:, :, :], nmax[:, g % 2, :, :], out(0), ALU.subtract).then_inc(nsplit, 1)
                dve.wait_ge(nsplit, at.b * 2 * NG + (g * 2 + 6))
                nc.vector.tensor_copy(out(1), nrest[:, :, :]).then_inc(nmid_ready, 1)
                dve.wait_ge(nmid_ready, at.b * NG + (g + 1))
                nc.vector.tensor_tensor(out(2), nrest[:, :, :], out(1), ALU.subtract).then_inc(nparts_ready, 1)

            def copy_maxima(at, g, n, first=False):
                if not first:
                    a, h = before(at, g)
                    dve.wait_ge(nmax_out[h % 2], a.b * 32 + (h // 2 * 16 + 16))
                dve.wait_ge(work_full, n + 1)
                nc.vector.tensor_copy(nturned[:, :], work[0:3 * GH, :].bitcast(BF16)[:, 0:T]).then_inc(work_copied, 1)

            def finish(at, g, n):
                G = at.b * NG + g
                a, h = before(at, g)
                dve.wait_ge(work_full, n + 1)
                o = work[:, :].rearrange("p (q h c) -> p q h c", q=TPB, h=GH)
                nc.vector.reciprocal(rden[:, :, :], o[:, :, :, HD:HD + 1].squeeze(3)).then_inc(rden_ready, 1)
                dve.wait_ge(rden_ready, G)
                nc.vector.tensor_tensor(part[:, :, :, :], o[:, :, :, 0:HD], rden[:, :, :].unsqueeze(3).to_broadcast([P, TPB, GH, HD]),
                                        ALU.mult).then_inc(work_copied, 1)
                dve.wait_ge(work_copied, n + 2)
                hh = H[:, bass.ds(a.b * TPB, TPB), h * GH * HD:(h + 1) * GH * HD]
                nc.vector.tensor_tensor(hh, hh, part[:, :, :, :].rearrange("p q h d -> p q (h d)"), ALU.add).then_inc(part_ready, 1)

            def event(key, at, n):
                if key[0] == "V":
                    t = 2 * int(key[1])
                    dve.wait_ge(work_full, n + 1)
                    nc.vector.tensor_tensor(v1[:, at.half, t:t + 2, :, 0:HD], work[:, :].rearrange("p (t h d) -> p t h d", t=2, d=HD),
                                            bv[:, :].rearrange("p (h d) -> p h d", d=HD).unsqueeze(1).to_broadcast([P, 2, NH, HD]),
                                            ALU.add).then_inc(work_copied, 1)

            def keep_rounds(a, z):
                for r in range(a, z):
                    for g in range(2):
                        if r:
                            dve.wait_ge(taken, 2 * r + g - 1)
                        nc.vector.max(mx[:, g, :], left_scores[:, g, r % 2, :]).then_inc(found, 1)
                    for g in range(2):
                        dve.wait_ge(found, 2 * r + g + 1)
                        if r == ROUNDS - 1:
                            nc.vector.memset(mx[:, g, 8 - SPARE:8], TAKEN).then_inc(mask_made, 1)
                    for g in range(2):
                        if r == ROUNDS - 1:
                            dve.wait_ge(mask_made, g + 1)
                        nc.vector.match_replace(left_scores[:, g, 1 - r % 2, :], mx[:, g, :], left_scores[:, g, r % 2, :], TAKEN
                                                ).then_inc(taken, 1)

            def make_mask():
                dve.wait_ge(taken, 2 * ROUNDS)
                for g in range(2):
                    nc.vector.tensor_scalar(left_scores[:, g, 1 - ROUNDS % 2, :], left_scores[:, g, ROUNDS % 2, :], TAKEN, 1.0,
                                            ALU.is_equal, ALU.subtract).then_inc(taken, 1)
                for g in range(2):
                    dve.wait_ge(taken, 2 * ROUNDS + g + 1)
                    nc.vector.tensor_scalar(mask[:, g, :], left_scores[:, g, 1 - ROUNDS % 2, :], -DROP, None, ALU.mult
                                            ).then_inc(mask_made, 1)

            def prologue():
                norm.constants(nc)
                nc.vector.memset(v1[:, :, :, :, HD:2 * HD], 1.0).then_inc(v_ones, 1)
                dve.sem_inc(max_ready, 2)
                dve.sem_inc(nsplit, 4)
                dve.wait_ge(loaded, LOADED)
                nc.vector.tensor_copy(ident16[:, :], ident[:, :]).then_inc(id_ready, 1)
                dve.wait_ge(id_ready, 1)
                nc.vector.tensor_scalar(bias[:, 0:2], bias[:, 0:2], HD ** -0.5, None, ALU.mult).then_inc(id_ready, 1)
                SHARE = -(-ROUNDS // 8)
                done = 0
                for b in range(2):
                    norm.stats(nc, dve, H, b)
                    if b:
                        dve.wait_ge(work_full, 2)
                    norm.apply(nc, dve, H, b, lambda t: xn[:, t, :], xn_ready)
                    if b == 0:
                        dve.wait_ge(route_in, 32)
                    for n, key in enumerate(PRO if b == 0 else PRO[:6]):
                        if key in CHUNK:
                            keep_rounds(done, min(done + SHARE, ROUNDS))
                            done = min(done + SHARE, ROUNDS)
                        event(key, At(0, b), b * 8 + n)
                make_mask()
                for g in range(2):
                    for u in range(8):
                        maximum(At(0, 0), g, u)
                    split_maxima(At(0, 0), g)
                copy_maxima(At(0, 0), 0, 14, True)
                dve.wait_ge(work_copied, 16)
                dve.sem_inc(nturned_ready, 1)

            def slot(at, g, left, first):
                if g == 1 and left >= 2 * NG - g:
                    norm.stats(nc, dve, H, at.b + 2)
                for s in range(8):
                    if left >= 2:
                        a, h = later(at, g, 2)
                        maximum(a, h, s)
                    if g == 1 and s == 4 and left >= 2 * NG - g:
                        norm.apply(nc, dve, H, at.b + 2, lambda t: xn[:, t, :], xn_ready)
                    if s == 1 and not first:
                        finish(at, g, ordinal(at, g, "FIN", left))
                    if s == 2 and left >= 1:
                        a, h = later(at, g, 1)
                        copy_maxima(a, h, ordinal(at, g, "MAX", left))
                        dve.wait_ge(work_copied, ordinal(at, g, "MAX", left) + 2)
                        dve.sem_inc(nturned_ready, 1)
                    e = events(at, g, s, left)
                    if e:
                        event(*e)
                if left >= 2:
                    a, h = later(at, g, 2)
                    split_maxima(a, h)

            prologue()
            run_pairs(dve, slot)
            finish(At(B // 2, 0), 0, LAST_EVENT)

        @block.scalar
        def _(act):
            def exps(at, g, u):
                act.wait_ge(s2_full, at.b * 64 + (g * 16 + u + 1))
                act.wait_ge(av_done, at.b * 16 + (g * 4 + u // GH + 1))
                nc.scalar.activation(prob[:, u % 8, :], s2[u % 2][:, :], ACT.Exp).then_inc(exp_done, 1)

            def copy_sums(at, g):
                act.wait_ge(av_done, at.b * 16 + (g * 4 + 6))
                nc.scalar.activation(sumT[:, g % 2, :], sums[:, :], ACT.Copy).then_inc(sum_copied, 1)

            def event(key, at, n):
                if key[0] == "V":
                    return
                act.wait_ge(work_full, n + 1)
                if key[0] == "X":
                    nc.scalar.activation(xT[:, int(key[1]), :], work[:, :], ACT.Copy).then_inc(work_copied, 1)
                    return
                x = CHUNK[key]
                kw = dict(bias=bias[:, x:x + 1], scale=HD ** -0.5 if x < 2 else 1.0)
                act.wait_ge(parts_out[x % 2], at.b * 32 + (x // 2 * 16 + 16))
                nc.scalar.activation(full[:, x % 2, :], work[:, :], ACT.Identity, **kw).then_inc(full_ready, 1)
                nc.scalar.activation(parts[:, x % 2, 0, :], work[:, :], ACT.Identity, **kw).then_inc(work_copied, 1)

            def prologue():
                act.sem_inc(work_copied, 1)
                act.sem_inc(exp_done, 2)
                act.sem_inc(sum_copied, 1)
                act.wait_ge(id_ready, 2)
                for n, key in enumerate(PRO + PRO[:6]):
                    event(key, At(0, n // 8), n)
                act.wait_ge(work_copied, 16)
                act.sem_inc(work_copied, 2)

            def slot(at, g, left, first):
                for s in range(8):
                    for u in (2 * s, 2 * s + 1):
                        exps(at, g, u)
                    if s == 0 and not first:
                        copy_sums(*before(at, g))
                    e = events(at, g, s, left)
                    if e:
                        event(*e)

            prologue()
            run_pairs(act, slot)
            copy_sums(At(B // 2 - 1, 1), NG - 1)

E2, I2, CAP = 16, 128, 64
SLOT_ROWS = E2 * B * CAP
PAIR_ROWS = E2 * 2 * CAP

def top2_experts(nc, A, S, H, out):
    with ExitStack() as outer:
        m = Bufs(nc, outer, "t2")
        read_slot = m.sb("read_slot", [P, 2, TILES], I32)
        weight = m.sb("weight", [P, 2, TILES])
        write_slot = m.sb("write_slot", [P, 2, TILES], I32)
        xs = m.sb("xs", [P, TILES, D])
        with ExitStack() as both:
            m = Bufs(nc, both, "t2n")
            lgs = m.sb("lgs", [P, TILES, E2])
            router_logits(nc, A, S, H, xs, lgs)
            dispatch(nc, A, lgs, read_slot, write_slot, weight)
        slot_experts(nc, A, S, H, xs, read_slot, write_slot, weight, out)

def router_logits(nc, A, S, H, xs, lgs):
    with ExitStack() as ctx:
        m = Bufs(nc, ctx, "rl")
        wr, ident, zeros = m.sb("wr", [P, 2, E2]), m.sb("ident", [P, P]), m.sb("zeros", [P, 2048])
        xn, xT = m.sb("xn", [P, 2, TPB, D]), m.sb("xT", [P, 2, 2, T])
        norm = Norm(m)
        turn, lg = [m.ps(f"turn{c}", [P, T]) for c in range(2)], [m.ps(f"lg{k}", [P, T]) for k in range(2)]
        loaded, zero_set, zeroed = m.sem("loaded"), m.sem("zero_set"), m.sem("zeroed")
        xn_ready, xs_ready, x_turned, xT_ready, lg_full, lg_read = (m.sem(x) for x in (
            "xn_ready", "xs_ready", "x_turned", "xT_ready", "lg_full", "lg_read"))
        block = ctx.enter_context(nc.Block())

        @block.sync
        def _(sp):
            sp.dma_start(wr[:, :, :], A["w_router"]).then_inc(loaded, 16)
            sp.dma_start(ident[:, :], A["ident"]).then_inc(loaded, 16)
            sp.wait_ge(zero_set, 1)
            zero_rows(sp, S["slots_x"], SLOT_ROWS, zeros, zeroed)

        @block.gpsimd
        def _(pool):
            pool.wait_ge(norm.set, 2)
            with pool.Fori(0, B) as g:
                norm.power(nc, pool, g)

        @block.vector
        def _(dve):
            norm.constants(nc)
            nc.vector.memset(zeros[:, :], 0.0).then_inc(zero_set, 1)
            dve.sem_inc(x_turned, 4)
            dve.sem_inc(xs_ready, 2)
            with dve.Fori(0, B // 2) as j:
                for k in range(2):
                    b = j * 2 + k
                    norm.stats(nc, dve, H, b)
                    dve.wait_ge(x_turned, b * 2 + 2)
                    dve.wait_ge(xs_ready, b + 1)
                    norm.apply(nc, dve, H, b, lambda t: xn[:, k, t, :], xn_ready)

        @block.scalar
        def _(act):
            act.sem_inc(xT_ready, 2)
            act.sem_inc(lg_read, 2)

            def copy_x(b, k):
                act.wait_ge(xn_ready, b * TPB + TPB)
                nc.scalar.activation(xs[:, bass.ds(b * TPB, TPB), :], xn[:, k, :, :], ACT.Copy).then_inc(xs_ready, 1)
                for c in range(2):
                    act.wait_ge(x_turned, b * 2 + (c + 5))
                    nc.scalar.activation(xT[:, k, c, :], turn[c][:, :], ACT.Copy).then_inc(xT_ready, 1)

            def batch(b, k, more):
                if more:
                    copy_x(b + 1, 1 - k)
                act.wait_ge(lg_full, b + 1)
                nc.scalar.activation(lgs[:, bass.ds(b * TPB, TPB), :], lg[k][:, 0:TPB * E2].rearrange("p (t e) -> p t e", e=E2),
                                     ACT.Copy).then_inc(lg_read, 1)

            copy_x(0, 0)
            with act.Fori(0, B // 2 - 1) as j:
                for k in range(2):
                    batch(j * 2 + k, k, True)
            for k in range(2):
                batch(B - 2 + k, k, k == 0)

        @block.tensor
        def _(pe):
            pe.wait_ge(loaded, 32)

            def turn_x(b, k):
                pe.wait_ge(xn_ready, b * TPB + TPB)
                for c in range(2):
                    pe.wait_ge(xT_ready, b * 2 + (c + 1))
                    for t in range(TPB):
                        mm = nc.tensor.transpose(turn[c][:, t * P:(t + 1) * P], xn[:, k, t, c * P:(c + 1) * P], ident[:, :])
                    mm.then_inc(x_turned, 1)

            def batch(b, k, more):
                if more:
                    turn_x(b + 1, 1 - k)
                pe.wait_ge(xT_ready, b * 2 + 4)
                pe.wait_ge(lg_read, b + 1)
                for t in range(TPB):
                    for c in range(2):
                        mm = nc.tensor.matmul(lg[k][:, t * E2:(t + 1) * E2], xT[:, k, c, t * P:(t + 1) * P], wr[:, c, :],
                                              start=c == 0, stop=c == 1)
                mm.then_inc(lg_full, 1)

            turn_x(0, 0)
            with pe.Fori(0, B // 2 - 1) as j:
                for k in range(2):
                    batch(j * 2 + k, k, True)
            for k in range(2):
                batch(B - 2 + k, k, k == 0)

def dispatch(nc, A, lgs, read_slot, write_slot, weight):
    FAR = float(2 * SLOT_ROWS)
    with ExitStack() as ctx:
        m = Bufs(nc, ctx, "dp")
        iota, base = m.sb("iota", [P, P]), m.sb("base", [P, TILES])
        strict_f, strict, ones = m.sb("strict_f", [P, P]), m.sb("strict", [P, P], BF16), m.sb("ones", [P, P], BF16)
        big, probs = m.sb("big", [P, TILES]), m.sb("probs", [P, TILES, E2])
        top, top_i = m.sb("top", [P, TILES, 8]), m.sb("top_i", [P, TILES, 8], U32)
        idx, hot = m.sb("idx", [P, 2, TILES]), m.sb("hot", [P, 2, TILES, E2], BF16)
        tot, run, flag = (m.sb(x, [P, B, E2, 2 * TPB]) for x in ("tot", "run", "flag"))
        place, pos, over = m.sb("place", [P, TILES, E2]), m.sb("pos", [P, 2, TILES]), m.sb("over", [P, 2, TILES])
        row = m.sb("row", [P, 2, TILES])
        pre = [m.ps(f"pre{g}", [P, 512]) for g in range(4)]
        sums = [m.ps(f"sums{g}", [P, 512]) for g in range(4)]
        loaded, step, counted, exp_done = (m.sem(x) for x in ("loaded", "step", "counted", "exp_done"))
        block = ctx.enter_context(nc.Block())
        bc = lambda x: x.unsqueeze(2).to_broadcast([P, TILES, E2])
        HOT_STEP = 2 + 2 * TILES + 5 + 3

        @block.sync
        def _(sp):
            for dst, name in ((iota, "iota128"), (base, "batch_row"), (strict_f, "strict")):
                sp.dma_start(dst[:, :], A[name]).then_inc(loaded, 16)

        @block.scalar
        def _(act):
            act.wait_ge(step, 2)
            nc.scalar.activation(probs[:, :, :], probs[:, :, :], ACT.Exp).then_inc(exp_done, 1)

        @block.tensor
        def _(pe):
            pe.wait_ge(step, HOT_STEP)
            for c in range(2):
                for g in range(2):
                    r = hot[:, c, g * 32:(g + 1) * 32, :].rearrange("p t e -> p (t e)")
                    nc.tensor.matmul(pre[2 * c + g][:, :], strict[:, :], r, start=True, stop=True).then_inc(counted, 1)
                    nc.tensor.matmul(sums[2 * c + g][:, :], ones[:, :], r, start=True, stop=True).then_inc(counted, 1)

        @block.vector
        def _(dve):
            n = [0]

            def link(ins, wait=True):
                n[0] += 1
                ins.then_inc(step, 1)
                if wait:
                    dve.wait_ge(step, n[0])

            link(nc.vector.tensor_reduce(big[:, :], lgs[:, :, :], AX.X, ALU.max))
            link(nc.vector.tensor_tensor(probs[:, :, :], lgs[:, :, :], bc(big[:, :]), ALU.subtract))
            dve.wait_ge(exp_done, 1)
            link(nc.vector.tensor_reduce(big[:, :], probs[:, :, :], AX.X, ALU.add))
            link(nc.vector.reciprocal(big[:, :], big[:, :]))
            link(nc.vector.tensor_tensor(probs[:, :, :], probs[:, :, :], bc(big[:, :]), ALU.mult))
            for t in range(TILES):
                link(nc.vector.max(top[:, t, :], probs[:, t, :]), wait=t == TILES - 1)
            for t in range(TILES):
                link(nc.vector.max_index(top_i[:, t, :], top[:, t, :], probs[:, t, :]), wait=t == TILES - 1)
            dve.wait_ge(loaded, 48)
            link(nc.vector.tensor_copy(strict[:, :], strict_f[:, :]))
            link(nc.vector.memset(ones[:, :], 1.0))
            link(nc.vector.tensor_copy(idx[:, :, :], top_i[:, :, 0:2].rearrange("p t c -> p c t")))
            for c in range(2):
                link(nc.vector.tensor_tensor(hot[:, c, :, :], iota[:, 0:E2].unsqueeze(1).to_broadcast([P, TILES, E2]),
                                             bc(idx[:, c, :]), ALU.is_equal))
            assert n[0] == HOT_STEP
            link(nc.vector.tensor_copy(weight[:, :, :], top[:, :, 0:2].rearrange("p t c -> p c t")))
            link(nc.vector.memset(flag[:, :, :, :], 1.0))
            link(nc.vector.memset(flag[:, :, :, 0:1], 0.0))
            dve.wait_ge(counted, 8)
            for c in range(2):
                for g in range(2):
                    link(nc.vector.tensor_copy(tot[:, 8 * g:8 * g + 8, :, c * TPB:(c + 1) * TPB],
                                               sums[2 * c + g][:, :].rearrange("p (b q e) -> p b e q", q=TPB, e=E2)))
            flat = lambda x: x[:, :, :, :].rearrange("p b e q -> p (b e q)")
            link(nc.vector.tensor_tensor_scan(flat(run), flat(flag), flat(tot), 0.0, ALU.mult, ALU.add))
            link(nc.vector.tensor_tensor(flat(run), flat(run), flat(tot), ALU.subtract))
            for c in range(2):
                for g in range(2):
                    link(nc.vector.tensor_tensor(place[:, 32 * g:32 * g + 32, :].rearrange("p (b q) e -> p b q e", q=TPB),
                                                 pre[2 * c + g][:, :].rearrange("p (b q e) -> p b q e", q=TPB, e=E2),
                                                 run[:, 8 * g:8 * g + 8, :, c * TPB:(c + 1) * TPB].rearrange("p b e q -> p b q e"), ALU.add))
                link(nc.vector.tensor_tensor(place[:, :, :], place[:, :, :], hot[:, c, :, :], ALU.mult))
                link(nc.vector.tensor_reduce(pos[:, c, :], place[:, :, :], AX.X, ALU.add))
                link(nc.vector.tensor_scalar(row[:, c, :], idx[:, c, :], float(2 * CAP), None, ALU.mult))
                link(nc.vector.tensor_tensor(row[:, c, :], row[:, c, :], base[:, :], ALU.add))
            link(nc.vector.tensor_scalar(over[:, :, :], pos[:, :, :], float(CAP), FAR, ALU.is_ge, ALU.mult))
            link(nc.vector.tensor_scalar(pos[:, :, :], pos[:, :, :], float(CAP - 1), None, ALU.min))
            link(nc.vector.tensor_tensor(row[:, :, :], row[:, :, :], pos[:, :, :], ALU.add))
            link(nc.vector.tensor_copy(read_slot[:, :, :], row[:, :, :]))
            link(nc.vector.tensor_tensor(row[:, :, :], row[:, :, :], over[:, :, :], ALU.add))
            link(nc.vector.tensor_copy(write_slot[:, :, :], row[:, :, :]))

def slot_experts(nc, A, S, H, xs, read_slot, write_slot, weight, out):
    N, R, PT = SLOT_ROWS // P, 4, 2 * TPB
    PAIRS = B // 2
    with ExitStack() as ctx:
        m = Bufs(nc, ctx, "se")
        wgu, wd = m.sb("wgu", [P, E2, 2, 2 * I2]), m.sb("wd", [P, E2, D])
        ident, xt, o = m.sb("ident", [P, P]), m.sb("xt", [P, 4, D]), m.sb("o", [P, 4, D])
        g = m.sb("g", [P, R, 2, D])
        pause = m.sb("pause", [P, 1])
        loaded, scattered, summed, stored, passed = (m.sem(x) for x in ("loaded", "scattered", "summed", "stored", "passed"))
        x_in, o_out, got, w_in = ([m.sem(f"{x}{k}") for k in range(4)] for x in ("x_in", "o_out", "got", "w_in"))
        xv = S["slots_x"].rearrange("(n p) d -> n p d", p=P)
        yv = S["slots_y"].rearrange("(n p) d -> n p d", p=P)
        ov = out.rearrange("b (q p) d -> (b q) p d", p=P)

        def turn_ready(pe, n, q, i):
            pe.wait_ge(loaded, 16)
            pe.wait_ge(x_in[q % 4], i * 4 * 16 + (q // 4 * 16 + 16))

        def finish(dve, n, k, q, i, left, s, pD):
            dve.wait_ge(s["down_full"], n + 2)
            dve.wait_ge(o_out[q % 4], i * 4 * 16 + (q // 4 * 16 + 16))
            nc.vector.tensor_copy(o[:, q % 4, :], pD[k][:, 0:D]).then_inc(s["down_read"], 1)
            if q % 2 and not (isinstance(i, int) and i == 0):
                add(dve, i - 1, q // 2)

        def add(dve, j, u):
            t = j * PT + u
            dve.wait_ge(got[u % R], j * (PT // R * 32) + (u // R * 32 + 32))
            nc.vector.memset(pause[:, :], 0.0)
            for c in range(2):
                if c:
                    dve.wait_ge(summed, t * 2 + 1)
                hh = H[:, bass.ds(t, 1), :].squeeze(1)
                nc.vector.scalar_tensor_tensor(out=hh, in0=g[:, u % R, c, :], scalar=weight[:, c, bass.ds(t, 1)],
                                               in1=hh, op0=ALU.mult, op1=ALU.add).then_inc(summed, 1)

        def pool_prog(pool, s):
            def scatter(j):
                if j:
                    pool.wait_ge(scattered, 32 * PT * j)
                for t in range(j * PT, (j + 1) * PT):
                    for c in range(2):
                        nc.gpsimd.indirect_dma_start(S["slots_x"][0:(j + 1) * PAIR_ROWS, :], bass.IndirectOffsetOnAxis(ap=write_slot[:, c, t:t + 1], axis=0),
                                                     xs[:, t, :], None, bounds_check=(j + 1) * PAIR_ROWS - 1, oob_is_err=False).then_inc(scattered, 16)

            def gather(j):
                for k in range(4):
                    pool.wait_ge(o_out[k], 64 * (j + 1) + 16)
                for t in range(j * PT, (j + 1) * PT):
                    if t >= R:
                        pool.wait_ge(summed, 2 * (t - R + 1))
                    for c in range(2):
                        nc.gpsimd.indirect_dma_start(g[:, t % R, c, :], None, S["slots_y"][0:(j + 1) * PAIR_ROWS, :],
                                                     bass.IndirectOffsetOnAxis(ap=read_slot[:, c, t:t + 1], axis=0)).then_inc(got[t % R], 16)

            for j in range(2):
                scatter(j)
            for j in range(PAIRS):
                if j + 2 < PAIRS:
                    scatter(j + 2)
                gather(j)

        def sync_prog(sp, s, steps):
            sp.dma_start(ident[:, :], A["ident"]).then_inc(loaded, 16)
            sp.wait_ge(scattered, 32 * PT)
            for k in range(4):
                sp.dma_start(xt[:, k, :], xv[k]).then_inc(x_in[k], 16)
                sp.sem_inc(o_out[k], 16)

            def store(j, u):
                t = j * PT + u
                sp.wait_ge(summed, t * 2 + 2)
                sp.dma_start(ov[bass.ds(t, 1)].squeeze(0), H[:, bass.ds(t, 1), :].squeeze(1)).then_inc(stored, 16)

            def step(n, k, q, i, left):
                if q == E2 - 4 and left >= 4:
                    sp.wait_ge(scattered, i * (32 * PT) + 64 * PT)
                    sp.sem_inc(passed, 1)
                if left >= 4:
                    sp.wait_ge(s["x_turned"], n + 5)
                    sp.dma_start(xt[:, q % 4, :], xv[bass.ds(n + 4, 1)].squeeze(0)).then_inc(x_in[q % 4], 16)
                sp.wait_ge(s["down_read"], n + 3)
                sp.dma_start(yv[bass.ds(n, 1)].squeeze(0), o[:, q % 4, :]).then_inc(o_out[q % 4], 16)
                if q % 2 and not (isinstance(i, int) and i == 0):
                    store(i - 1, q // 2)

            steps(sp, step)
            for u in range(PT):
                store(PAIRS - 1, u)
            sp.wait_ge(stored, 16 * TILES)

        def last_adds(dve):
            for u in range(PT):
                add(dve, PAIRS - 1, u)

        def load_weights(act, s):
            for c in range(4):
                es = slice(c * 4, c * 4 + 4)
                act.dma_start(wgu[:, es, :, :], A["ex_gu"][:, es, :, :]).then_inc(w_in[c], 16)
                act.dma_start(wd[:, es, :], A["ex_down"][:, es, :]).then_inc(w_in[c], 16)

        def mul_ready(pe, e):
            pe.wait_ge(w_in[e // 4], 32)
            return (lambda c: wgu[:, e, c, 0:I2]), (lambda c: wgu[:, e, c, I2:2 * I2])

        none = lambda *a: None
        expert_stream(nc, m, N, I2, E2, turn_ready=turn_ready, x_of=lambda n, q, c: xt[:, q % 4, c * P:(c + 1) * P],
                      mul_ready=mul_ready, place=lambda pe, n, q, i: q, down_of=lambda pe, e: (lambda c: wd[:, e, :]),
                      mul_also=none, identT=ident, dve_more=none, act_first=load_weights, act_more=none, pool_prog=pool_prog,
                      sync_prog=sync_prog, finish=finish, prologue_dve=none, dve_before=none, peel_first=True, dve_last=last_adds)

SCRATCH = [("frames", [B * FRAMES, D_STFT], F32), ("sorted_x", [SORT_TILES * P, D], F32), ("sorted_y", [SORT_TILES * P, D], F32),
           ("slots_x", [SLOT_ROWS, D], F32), ("slots_y", [SLOT_ROWS, D], F32),
           ("route", [B * NH, T], F32), ("mask", [B * NH, T], BF16),
           ("parts", [2, 2, 3, D, T], BF16), ("maxima", [2, 12, T], BF16)]

def build(nc, A, out):
    S = {name: nc.dram_tensor(f"scratch_{name}", shape, dt).ap() for name, shape, dt in SCRATCH}
    with nc.sbuf_tensor("hidden", [P, TILES, D], F32) as H:
        embed_tokens(nc, A, S, H)
        diff_attention(nc, A, S, H)
        with nc.sbuf_tensor("slot", [P, TILES], I32) as slot:
            top1_experts(nc, A, S, H, slot)
            sparse_attention(nc, A, S, H, slot)
        top2_experts(nc, A, S, H, out)

def shape_constants():
    import numpy as np

    n = np.arange(NFFT)[:, None] * np.arange(FREQS)[None, :] * (2 * np.pi / NFFT)
    dft = np.concatenate([np.cos(n), -np.sin(n)], 1).astype(np.float32)
    coord = np.clip((np.arange(T) + np.float32(0.5)) * (FRAMES / T) - 0.5, 0, FRAMES - 1).astype(np.float32)
    i0 = np.floor(coord).astype(np.int32)
    i1 = np.minimum(i0 + 1, FRAMES - 1)
    w = coord - i0
    interp = np.zeros((FRAMES + 1, T), np.float32)
    interp[i0, np.arange(T)] += 1 - w
    interp[i1, np.arange(T)] += w
    interp[FRAMES] = 1
    hd = 16
    inv = 1.0 / 10000.0 ** (np.arange(0, hd, 2, dtype=np.float32) / np.float32(hd))
    fr = np.outer(np.arange(T, dtype=np.float32), inv.astype(np.float32)).astype(np.float32)
    c, s = np.cos(fr), np.sin(fr)
    rot = np.stack([np.concatenate([c, c], 1), np.concatenate([s, -s], 1)], 0).astype(np.float32)
    rot = rot.reshape(2, TPB, P, hd).transpose(2, 0, 1, 3)
    k = np.arange(P)
    return {
        "dft": dft, "interp": interp, "rot": rot,
        "iota_v": np.tile(np.arange(V, dtype=np.float32), (P, 1)),
        "iota128": np.tile(np.arange(P, dtype=np.float32), (P, 1)),
        "k128": np.tile(np.arange(P, dtype=np.float32) * P, (P, 1)),
        "batch_row": np.tile((np.arange(TILES) // (2 * TPB) * (2 * E2 * CAP) + np.arange(TILES) // TPB % 2 * CAP).astype(np.float32), (P, 1)),
        "part_id": k.astype(np.float32)[:, None],
        "ident": np.eye(P, dtype=np.float32),
        "upper": (k[:, None] <= k[None, :]).astype(np.float32),
        "strict": (k[:, None] < k[None, :]).astype(np.float32),
        "ones": np.ones((P, P), np.float32),
    }
def layout(inputs):
    import numpy as np

    x = {k: np.asarray(v) for k, v in inputs.items()}
    L = shape_constants()
    ids = x["x"].astype(np.int32, copy=False)
    half = NFFT // 2
    padded = np.pad(ids, ((0, 0), (half, half)), mode="reflect")
    L["ids"] = ids
    L["frame_ids"] = padded.reshape(B * FRAMES, NFFT).T
    L["window"] = x["L0_tok_window"][:, None]
    L["tok_proj_w"] = x["L0_tok_proj_w"].reshape(D_STFT, FREQS, V).transpose(2, 1, 0)
    L["proj_b"] = x["L0_tok_proj_b"][None, :]
    L["emb"] = x["L0_tok_emb_table"]
    rows = lambda w: w.reshape(2, P, -1).transpose(1, 0, 2)
    L["wqk"] = rows(np.concatenate([x["L0_attn_Wq"].T, x["L0_attn_Wk"].T], 1))
    L["wv"], L["wo"] = rows(x["L0_attn_Wv"].T), rows(x["L0_attn_Wproj"].T)
    L["lambdas"] = np.stack([x["L0_attn_lambda_q1"], x["L0_attn_lambda_k1"], x["L0_attn_lambda_q2"],
                             x["L0_attn_lambda_k2"]]).reshape(2, 2, 8)
    L["gate_w"], L["sh_gate"] = rows(x["L0_ffn_gate_w"]), rows(x["L0_ffn_shared_gate_w"])
    L["sh_up"], L["sh_down"] = rows(x["L0_ffn_shared_up_w"]), x["L0_ffn_shared_down_w"].reshape(4, P, D).transpose(1, 0, 2)
    gu = np.concatenate([x["L0_ffn_routed_gate_w"], x["L0_ffn_routed_up_w"]], 2)
    L["ro_gu"] = gu.reshape(32, 2, P, 1024).transpose(0, 2, 1, 3)
    L["ro_down"] = x["L0_ffn_routed_down_w"].reshape(32, 4, P, D).transpose(0, 2, 1, 3)
    L["r_w1"], L["r_w2"] = rows(x["L1_attn_r_w1"].T), np.pad(x["L1_attn_r_w2"].T, ((0, 0), (0, P - 16)))
    L["r_b1"], L["r_b2"] = x["L1_attn_r_b1"][:, None], x["L1_attn_r_b2"][:, None]
    w, bias = x["L1_attn_qkv_w"], x["L1_attn_qkv_b"]
    L["l1_wqk"] = w[0:2 * D].T.reshape(2, P, 4, P).transpose(1, 0, 2, 3)
    L["l1_wv"], L["l1_bv"] = rows(w[2 * D:].T), bias[None, 2 * D:]
    L["l1_bias"] = bias[0:2 * D].reshape(4, P).T
    L["w_router"] = rows(x["L1_ffn_w_router"])
    gu = np.concatenate([x["L1_ffn_w_gate"], x["L1_ffn_w_fc"]], 2)
    L["ex_gu"] = gu.reshape(16, 2, P, 256).transpose(2, 0, 1, 3)
    L["ex_down"] = x["L1_ffn_w_proj"].transpose(1, 0, 2)
    return {k: np.ascontiguousarray(v) for k, v in L.items()}

def kernel(**inputs):
    import numpy as _np
    import concourse.bacc as _bacc
    from concourse import mybir as _mybir
    from concourse.bass_utils import run_bass_kernel_spmd as _run

    nc = _bacc.Bacc("TRN2", target_bir_lowering=False, num_devices=1)
    arrays, args = {}, {}
    for name, a in layout(inputs).items():
        arrays[f"in_{name}_dram"] = a
        args[name] = nc.dram_tensor(f"in_{name}_dram", a.shape, _mybir.dt.from_np(a.dtype), kind="ExternalInput").ap()
    out = nc.dram_tensor("out_0_dram", (B, T, D), _mybir.dt.float32, kind="ExternalOutput").ap()
    build(nc, args, out)
    r = _run(nc, [arrays], core_ids=[0])
    return r.results[0]["out_0_dram"]
```
